# Optimizing a Trainium2 kernel written in Bass

```python
import numpy as np
import jax
import jax.numpy as jnp

def _softmax(x, axis=-1):
    return jax.nn.softmax(x, axis=axis)

def _gelu(x):
    return jax.nn.gelu(x, approximate=True)

def _silu(x):
    return jax.nn.silu(x)

def _sigmoid(x):
    return jax.nn.sigmoid(x)

def _layernorm(x, axis=-1, eps=1e-05):
    m = jnp.mean(x, axis=axis, keepdims=True)
    v = jnp.var(x, axis=axis, keepdims=True)
    return (x - m) / jnp.sqrt(v + eps)

def _scatter_add(tgt, idx, src, axis=0):
    return tgt.at[idx].add(src)

def _segment_sum(src, seg, n):
    return jax.ops.segment_sum(src, seg, n)
kernel_name = 'mk_decoder_postln_d2_seqx_r4_916ea8'

def setup_inputs(seed: int=0):
    np.random.seed(seed)
    _w = jnp.asarray

    def _rec_inputs():
        import jax
        import jax.numpy as jnp
        _rk = jax.random.key(seed)
        x = 7.22e-05 + 1 * jax.random.normal(jax.random.fold_in(_rk, 1), (32, 128, 256), jnp.float32)
        _lenS = 128 - jax.random.randint(jax.random.fold_in(_rk, 7), (32,), 0, max(1, 128 // 4) + 1, jnp.int32)
        _lenS2 = 128 - jax.random.randint(jax.random.fold_in(_rk, 8), (32,), 0, max(1, 128 // 4) + 1, jnp.int32)
        _ctx_1024P = jax.random.normal(jax.random.fold_in(_rk, 11), (32, 16, 256), jnp.float32)
        _ctx_1024c = jax.random.dirichlet(jax.random.fold_in(_rk, 511), 0.3 * jnp.ones((16,), jnp.float32), (32, 128))
        _ctx_1024t = jnp.einsum('bsk,bkd->bsd', _ctx_1024c, _ctx_1024P)
        _ctx_1024t = _ctx_1024t * jax.lax.rsqrt(jnp.mean(jnp.square(_ctx_1024t)) + 1e-12) * 0.953939
        ctx_1024 = 4.13588e-05 + 0.999923 * (_ctx_1024t + 0.3 * jax.random.normal(jax.random.fold_in(_rk, 611), (32, 128, 256), jnp.float32))
        return (x, ctx_1024)
    x, ctx_1024 = _rec_inputs()

    def _L0_attn_setup():
        import jax, jax.numpy as jnp
        import numpy as np
        D_MODEL = 256
        N_HEADS = 16
        D_HEAD = D_MODEL // N_HEADS
        SCALE = 1.0 / np.sqrt(D_HEAD).astype(np.float32)

        def _feature_map(x):
            return jax.nn.elu(x) + 1.0
        key = jax.random.key(seed)
        ks = jax.random.split(key, 7)
        b, s = (4, 512)
        w = 1.0 / np.sqrt(D_MODEL).astype(np.float32)
        return {'x': jax.random.normal(ks[0], (b, s, D_MODEL), dtype=jnp.float32), 'Wq': jax.random.normal(ks[1], (D_MODEL, D_MODEL), dtype=jnp.float32) * w, 'Wk': jax.random.normal(ks[2], (D_MODEL, D_MODEL), dtype=jnp.float32) * w, 'Wv': jax.random.normal(ks[3], (D_MODEL, D_MODEL), dtype=jnp.float32) * w, 'Wo': jax.random.normal(ks[4], (D_MODEL, D_MODEL), dtype=jnp.float32) * w, 'Wg': jax.random.normal(ks[5], (N_HEADS, D_MODEL), dtype=jnp.float32) * w, 'bg': jax.random.normal(ks[6], (N_HEADS,), dtype=jnp.float32) * 0.02}
    _L0_attn_all = _L0_attn_setup()
    _L0_attn_in = {k: v for k, v in _L0_attn_all.items() if k in ('Wq', 'Wk', 'Wv', 'Wo', 'Wg', 'bg')}
    del _L0_attn_all

    def _L0_xattn_setup():
        import jax, jax.numpy as jnp
        import numpy as np
        D_MODEL = 256
        NUM_HEADS = 16
        HEAD_DIM = D_MODEL // NUM_HEADS
        B, S = (4, 512)
        key = jax.random.key(seed)
        ks = jax.random.split(key, 11)
        scale = 1.0 / np.sqrt(D_MODEL)
        inp = {'query': jax.random.normal(ks[0], (B, S, D_MODEL), dtype=jnp.float32), 'key': jax.random.normal(ks[1], (B, S, D_MODEL), dtype=jnp.float32), 'value': jax.random.normal(ks[2], (B, S, D_MODEL), dtype=jnp.float32), 'Wq': jax.random.normal(ks[3], (D_MODEL, D_MODEL), dtype=jnp.float32) * scale, 'bq': jnp.zeros((D_MODEL,), dtype=jnp.float32), 'Wk': jax.random.normal(ks[4], (D_MODEL, D_MODEL), dtype=jnp.float32) * scale, 'bk': jnp.zeros((D_MODEL,), dtype=jnp.float32), 'Wv': jax.random.normal(ks[5], (D_MODEL, D_MODEL), dtype=jnp.float32) * scale, 'bv': jnp.zeros((D_MODEL,), dtype=jnp.float32), 'Wo': jax.random.normal(ks[6], (D_MODEL, D_MODEL), dtype=jnp.float32) * scale, 'bo': jnpp.zeros((D_MODEL,), dtype=jnp.float32) if False else jnp.zeros((D_MODEL,), dtype=jnp.float32)}
        return inp
    _L0_xattn_all = _L0_xattn_setup()
    _L0_xattn_in = {k: v for k, v in _L0_xattn_all.items() if k in ('Wq', 'bq', 'Wk', 'bk', 'Wv', 'bv', 'Wo', 'bo')}
    del _L0_xattn_all

    def _L0_ffn_setup():
        import jax, jax.numpy as jnp
        import numpy as np
        B, S, D = (2, 1024, 256)
        H = 1024
        E = 8
        K = 4
        key = jax.random.key(seed)
        kx, kr, ku, kd = jax.random.split(key, 4)
        x = jax.random.normal(kx, (B, S, D), dtype=jnp.float32)
        router_w = jax.random.normal(kr, (D, E), dtype=jnp.float32) / np.sqrt(D)
        up_w = jax.random.normal(ku, (E, D, H), dtype=jnp.float32) / np.sqrt(D)
        down_w = jax.random.normal(kd, (E, H, D), dtype=jnp.float32) / np.sqrt(H)
        return {'x': x, 'router_w': router_w, 'up_w': up_w, 'down_w': down_w}
    _L0_ffn_all = _L0_ffn_setup()
    _L0_ffn_in = {k: v for k, v in _L0_ffn_all.items() if k in ('router_w', 'up_w', 'down_w')}
    del _L0_ffn_all

    def _L1_attn_setup():
        import jax, jax.numpy as jnp
        import numpy as np
        B, N, DIM_IN, DIM_INNER, DIM_OUT, WINDOW = (4, 1024, 256, 256, 256, 128)
        key = jax.random.key(seed)
        k1, k2, k3, k4 = jax.random.split(key, 4)
        x = jax.random.normal(k1, (B, N, DIM_IN), dtype=jnp.float32)
        w_qkv = jax.random.normal(k2, (DIM_IN, 3 * DIM_INNER), dtype=jnp.float32) / np.sqrt(DIM_IN)
        w_out = jax.random.normal(k3, (DIM_INNER, DIM_OUT), dtype=jnp.float32) / np.sqrt(DIM_INNER)
        b_out = jax.random.normal(k4, (DIM_OUT,), dtype=jnp.float32) * 0.01
        return {'x': x, 'w_qkv': w_qkv, 'w_out': w_out, 'b_out': b_out}
    _L1_attn_all = _L1_attn_setup()
    _L1_attn_in = {k: v for k, v in _L1_attn_all.items() if k in ('w_qkv', 'w_out', 'b_out')}
    del _L1_attn_all

    def _L1_xattn_setup():
        import jax, jax.numpy as jnp
        import numpy as np
        NUM_HEADS = 16
        D_MODEL = 256
        HEAD_DIM = D_MODEL // NUM_HEADS
        B, S = (2, 512)
        key = jax.random.key(seed)
        ks = jax.random.split(key, 11)
        scale = 1.0 / np.sqrt(D_MODEL)
        inp = {'query': jax.random.normal(ks[0], (B, S, D_MODEL), jnp.float32), 'key': jax.random.normal(ks[1], (B, S, D_MODEL), jnp.float32), 'value': jax.random.normal(ks[2], (B, S, D_MODEL), jnp.float32), 'Wq': jax.random.normal(ks[3], (D_MODEL, D_MODEL), jnp.float32) * scale, 'bq': jnp.zeros((D_MODEL,), jnp.float32), 'Wk': jax.random.normal(ks[4], (D_MODEL, D_MODEL), jnp.float32) * scale, 'bk': jnp.zeros((D_MODEL,), jnp.float32), 'Wv': jax.random.normal(ks[5], (D_MODEL, D_MODEL), jnp.float32) * scale, 'bv': jnp.zeros((D_MODEL,), jnp.float32), 'Wo': jax.random.normal(ks[6], (D_MODEL, D_MODEL), jnp.float32) * scale, 'bo': jnp.zeros((D_MODEL,), jnp.float32)}
        return inp
    _L1_xattn_all = _L1_xattn_setup()
    _L1_xattn_in = {k: v for k, v in _L1_xattn_all.items() if k in ('Wq', 'bq', 'Wk', 'bk', 'Wv', 'bv', 'Wo', 'bo')}
    del _L1_xattn_all

    def _L1_ffn_setup():
        import jax, jax.numpy as jnp
        import numpy as np
        key = jax.random.key(seed)
        k0, k1, k2, k3 = jax.random.split(key, 4)
        B, S, D, F, E = (8, 512, 256, 512, 8)
        x = jax.random.normal(k0, (B, S, D), dtype=jnp.float32)
        Wg = jax.random.normal(k1, (D, E), dtype=jnp.float32) * 0.02
        W1 = jax.random.normal(k2, (E, D, F), dtype=jnp.float32) * 0.02
        W2 = jax.random.normal(k3, (E, F, D), dtype=jnp.float32) * 0.02
        return {'x': x, 'Wg': Wg, 'W1': W1, 'W2': W2}
    _L1_ffn_all = _L1_ffn_setup()
    _L1_ffn_in = {k: v for k, v in _L1_ffn_all.items() if k in ('Wg', 'W1', 'W2')}
    del _L1_ffn_all
    return {'x': x, 'ctx_1024': ctx_1024, 'L0_attn_Wq': _L0_attn_in['Wq'], 'L0_attn_Wk': _L0_attn_in['Wk'], 'L0_attn_Wv': _L0_attn_in['Wv'], 'L0_attn_Wo': _L0_attn_in['Wo'], 'L0_attn_Wg': _L0_attn_in['Wg'], 'L0_attn_bg': _L0_attn_in['bg'], 'L0_xattn_Wq': _L0_xattn_in['Wq'], 'L0_xattn_bq': _L0_xattn_in['bq'], 'L0_xattn_Wk': _L0_xattn_in['Wk'], 'L0_xattn_bk': _L0_xattn_in['bk'], 'L0_xattn_Wv': _L0_xattn_in['Wv'], 'L0_xattn_bv': _L0_xattn_in['bv'], 'L0_xattn_Wo': _L0_xattn_in['Wo'], 'L0_xattn_bo': _L0_xattn_in['bo'], 'L0_ffn_router_w': _L0_ffn_in['router_w'], 'L0_ffn_up_w': _L0_ffn_in['up_w'], 'L0_ffn_down_w': _L0_ffn_in['down_w'], 'L1_attn_w_qkv': _L1_attn_in['w_qkv'], 'L1_attn_w_out': _L1_attn_in['w_out'], 'L1_attn_b_out': _L1_attn_in['b_out'], 'L1_xattn_Wq': _L1_xattn_in['Wq'], 'L1_xattn_bq': _L1_xattn_in['bq'], 'L1_xattn_Wk': _L1_xattn_in['Wk'], 'L1_xattn_bk': _L1_xattn_in['bk'], 'L1_xattn_Wv': _L1_xattn_in['Wv'], 'L1_xattn_bv': _L1_xattn_in['bv'], 'L1_xattn_Wo': _L1_xattn_in['Wo'], 'L1_xattn_bo': _L1_xattn_in['bo'], 'L1_ffn_Wg': _L1_ffn_in['Wg'], 'L1_ffn_W1': _L1_ffn_in['W1'], 'L1_ffn_W2': _L1_ffn_in['W2']}

def reference(x, ctx_1024, L0_attn_Wq, L0_attn_Wk, L0_attn_Wv, L0_attn_Wo, L0_attn_Wg, L0_attn_bg, L0_xattn_Wq, L0_xattn_bq, L0_xattn_Wk, L0_xattn_bk, L0_xattn_Wv, L0_xattn_bv, L0_xattn_Wo, L0_xattn_bo, L0_ffn_router_w, L0_ffn_up_w, L0_ffn_down_w, L1_attn_w_qkv, L1_attn_w_out, L1_attn_b_out, L1_xattn_Wq, L1_xattn_bq, L1_xattn_Wk, L1_xattn_bk, L1_xattn_Wv, L1_xattn_bv, L1_xattn_Wo, L1_xattn_bo, L1_ffn_Wg, L1_ffn_W1, L1_ffn_W2):
    import jax
    import jax.numpy as jnp

    def _L0_attn_ref(x, Wq, Wk, Wv, Wo, Wg, bg):
        import jax, jax.numpy as jnp
        import numpy as np
        D_MODEL = 256
        N_HEADS = 16
        D_HEAD = D_MODEL // N_HEADS
        SCALE = 1.0 / np.sqrt(D_HEAD).astype(np.float32)

        def _feature_map(x):
            return jax.nn.elu(x) + 1.0
        b, s, _ = x.shape
        q = (x @ Wq.T).reshape(b, s, N_HEADS, D_HEAD)
        k = (x @ Wk.T).reshape(b, s, N_HEADS, D_HEAD)
        v = (x @ Wv.T).reshape(b, s, N_HEADS, D_HEAD)
        q = _feature_map(q * SCALE)
        k = _feature_map(k)
        gate = jax.nn.sigmoid(x @ Wg.T + bg)
        qt = jnp.moveaxis(q, 1, 0)
        kt = jnp.moveaxis(k, 1, 0)
        vt = jnp.moveaxis(v, 1, 0)
        gt = jnp.moveaxis(gate, 1, 0)
        S0 = jnp.zeros((b, N_HEADS, D_HEAD, D_HEAD), dtype=x.dtype)

        def step(S, inp):
            q_t, k_t, v_t, g_t = inp
            S = g_t[:, :, None, None] * S + k_t[..., :, None] * v_t[..., None, :]
            y_t = jnp.einsum('bhi,bhij->bhj', q_t, S)
            return (S, y_t)
        _, ys = jax.lax.scan(step, S0, (qt, kt, vt, gt))
        y = jnp.moveaxis(ys, 0, 1).reshape(b, s, D_MODEL)
        return y @ Wo.T

    def _L0_xattn_ref(query, key, value, Wq, bq, Wk, bk, Wv, bv, Wo, bo):
        import jax, jax.numpy as jnp
        import numpy as np
        D_MODEL = 256
        NUM_HEADS = 16
        HEAD_DIM = D_MODEL // NUM_HEADS
        B, S = (4, 512)

        def split_heads(x):
            b, s, _ = x.shape
            return x.reshape(b, s, NUM_HEADS, HEAD_DIM).transpose(0, 2, 1, 3)
        q = split_heads(query @ Wq.T + bq)
        k = split_heads(key @ Wk.T + bk)
        v = split_heads(value @ Wv.T + bv)
        scores = jnp.einsum('bhqd,bhkd->bhqk', q, k) / np.sqrt(HEAD_DIM).astype(np.float32)
        attn = jax.nn.softmax(scores, axis=-1)
        ctx = jnp.einsum('bhqk,bhkd->bhqd', attn, v)
        b = ctx.shape[0]
        ctx = ctx.transpose(0, 2, 1, 3).reshape(b, -1, D_MODEL)
        return ctx @ Wo.T + bo

    def _L0_ffn_ref(x, router_w, up_w, down_w):
        import jax, jax.numpy as jnp
        import numpy as np
        B, S, D = (2, 1024, 256)
        H = 1024
        E = 8
        K = 4
        router_logits = jnp.einsum('bsd,de->bse', x, router_w)
        routing_weights = jax.nn.softmax(router_logits, axis=-1)
        topk_weights, topk_indices = jax.lax.top_k(routing_weights, K)
        topk_weights = topk_weights / jnp.sum(topk_weights, axis=-1, keepdims=True)
        h = jnp.einsum('bsd,edh->bseh', x, up_w)
        h = jax.nn.gelu(h)
        expert_outputs = jnp.einsum('bseh,ehd->bsed', h, down_w)
        gathered = jnp.take_along_axis(expert_outputs, topk_indices[:, :, :, None], axis=2)
        output = jnp.sum(topk_weights[:, :, :, None] * gathered, axis=2)
        return output

    def _L1_attn_ref(x, w_qkv, w_out, b_out):
        import jax, jax.numpy as jnp
        import numpy as np
        B, N, DIM_IN, DIM_INNER, DIM_OUT, WINDOW = (4, 1024, 256, 256, 256, 128)
        b, n, _ = x.shape
        w = WINDOW
        scale = DIM_INNER ** (-0.5)
        qkv = jnp.einsum('bnd,de->bne', x, w_qkv)
        q, k, v = jnp.split(qkv, 3, axis=-1)
        nw = n // w
        win = lambda t: t.reshape(b, nw, w, DIM_INNER)
        q, k, v = (win(q), win(k), win(v))
        kp = jnp.pad(k, ((0, 0), (1, 0), (0, 0), (0, 0)))
        k2 = jnp.concatenate([kp[:, :-1], kp[:, 1:]], axis=2)
        v2 = k2
        sim = jnp.einsum('bwid,bwjd->bwij', q, k2) * scale
        i, j = (w, 2 * w)
        mask = jnp.triu(jnp.ones((i, j), dtype=bool), j - i + 1)
        mask_value = -jnp.finfo(sim.dtype).max
        sim = jnp.where(mask[None, None], mask_value, sim)
        attn = jax.nn.softmax(sim, axis=-1)
        out = jnp.einsum('bwij,bwjd->bwid', attn, v2)
        out = out.reshape(b, n, DIM_INNER)[:, :n]
        return jnp.einsum('bnd,de->bne', out, w_out) + b_out

    def _L1_xattn_ref(query, key, value, Wq, bq, Wk, bk, Wv, bv, Wo, bo):
        import jax, jax.numpy as jnp
        import numpy as np
        NUM_HEADS = 16
        D_MODEL = 256
        HEAD_DIM = D_MODEL // NUM_HEADS
        B, S = (2, 512)
        b, s, _ = query.shape
        Q = query @ Wq + bq
        K = key @ Wk + bk
        V = value @ Wv + bv
        Q = Q.reshape(b, s, NUM_HEADS, HEAD_DIM).transpose(0, 2, 1, 3)
        K = K.reshape(b, -1, NUM_HEADS, HEAD_DIM).transpose(0, 2, 1, 3)
        V = V.reshape(b, -1, NUM_HEADS, HEAD_DIM).transpose(0, 2, 1, 3)
        scores = jnp.einsum('bhqd,bhkd->bhqk', Q, K) / jnp.sqrt(jnp.float32(HEAD_DIM)).astype(Q.dtype)
        attn = jax.nn.softmax(scores, axis=-1)
        ctx = jnp.einsum('bhqk,bhkd->bhqd', attn, V)
        ctx = ctx.transpose(0, 2, 1, 3).reshape(b, s, D_MODEL)
        return ctx @ Wo + bo

    def _L1_ffn_ref(x, Wg, W1, W2):
        import jax, jax.numpy as jnp
        import numpy as np
        B, S, D = x.shape
        E = Wg.shape[1]
        T = B * S
        cap = max(1, T // E)
        xt = x.reshape(T, D)
        logits = xt @ Wg
        probs = jax.nn.softmax(logits, axis=-1)
        pT = probs.T
        _, top_idx = jax.lax.top_k(pT, cap)
        sel = jnp.zeros((E, T), dtype=bool).at[jnp.arange(E)[:, None], top_idx].set(True)
        masked = jnp.where(sel, pT, -jnp.inf)
        assigned = sel.any(axis=0)
        tok2exp = jnp.where(assigned, jnp.argmax(masked, axis=0), jnp.argmax(pT, axis=0))
        weights = jnp.take_along_axis(probs, tok2exp[:, None], axis=1)[:, 0]
        out = jnp.zeros_like(xt)
        for e in range(E):
            gate = jnp.where(tok2exp == e, weights, 0.0)
            h = jax.nn.gelu(xt @ W1[e], approximate=False) @ W2[e]
            out = out + gate[:, None] * h
        return out.reshape(B, S, D)
    x = _layernorm(x + _L0_attn_ref(x, L0_attn_Wq, L0_attn_Wk, L0_attn_Wv, L0_attn_Wo, L0_attn_Wg, L0_attn_bg), axis=-1)
    x = _layernorm(x + _L0_xattn_ref(x, ctx_1024, ctx_1024, L0_xattn_Wq, L0_xattn_bq, L0_xattn_Wk, L0_xattn_bk, L0_xattn_Wv, L0_xattn_bv, L0_xattn_Wo, L0_xattn_bo), axis=-1)
    x = _layernorm(x + _L0_ffn_ref(x, L0_ffn_router_w, L0_ffn_up_w, L0_ffn_down_w), axis=-1)
    x = _layernorm(x + _L1_attn_ref(x, L1_attn_w_qkv, L1_attn_w_out, L1_attn_b_out), axis=-1)
    x = _layernorm(x + _L1_xattn_ref(x, ctx_1024, ctx_1024, L1_xattn_Wq, L1_xattn_bq, L1_xattn_Wk, L1_xattn_bk, L1_xattn_Wv, L1_xattn_bv, L1_xattn_Wo, L1_xattn_bo), axis=-1)
    x = _layernorm(x + _L1_ffn_ref(x, L1_ffn_Wg, L1_ffn_W1, L1_ffn_W2), axis=-1)
    return x

_drawn_inputs = setup_inputs


def setup_inputs(seed=0):
    import zlib

    import numpy as np

    out = dict(_drawn_inputs(seed))
    spreads = {'L0_xattn_bq': (0.0, 0.286),
     'L0_xattn_bk': (0.0, 0.8),
     'L0_xattn_bv': (0.0, 0.1),
     'L0_xattn_bo': (0.0, 0.1),
     'L1_xattn_bq': (0.0, 0.403),
     'L1_xattn_bk': (0.0, 0.8),
     'L1_xattn_bv': (0.0, 0.1),
     'L1_xattn_bo': (0.0, 0.1)}
    factors = {'L0_attn_bg': 6.285,
     'L1_attn_b_out': 7.009,
     'L1_ffn_Wg': 4.013,
     'L1_ffn_W1': 3.787,
     'L1_ffn_W2': 3.7}
    for name, (base, spread) in spreads.items():
        noise = np.random.default_rng([zlib.crc32(name.encode()), seed]).standard_normal(out[name].shape)
        drawn = base * np.exp(spread * noise) if base else spread * noise
        out[name] = jnp.asarray(drawn.astype(out[name].dtype))
    for name, factor in factors.items():
        out[name] = (out[name] * factor).astype(out[name].dtype)
    return out
```

```python
import numpy as np
import concourse.bass as bass
from concourse import mybir
from contextlib import ExitStack

F32 = mybir.dt.float32
U32 = mybir.dt.uint32
ALU = mybir.AluOpType
ACT = mybir.ActivationFunctionType
AX = mybir.AxisListType

P = 128
D = 256
DB = D // P
NB = 32
T = NB * P
NP = NB // 2
PT = 2 * P
H = 16
DH = D // H
HH = H // 2
E = 8
TOPK = 4
CAP = T // E
EPS = 1e-5
BANK = 512
BANK = 512
BANK = 512
BANK = 512
BANK = 512
BANK = 512
BANK = 512
BANK = 512
BANK = 512
BANK = 512
BANK = 512
BANK = 512
BANK = 512
HEAD_SCALE = float(DH) ** -0.5
WIN_SCALE = float(D) ** -0.5
MASKED = -3.0e38


def slot_head(s):
    group = 2 * ((s % 4) // 2) + s // 4
    return 2 * group + s % 2


def after(eng, sem, count):
    if isinstance(count, int) and count <= 0:
        return
    eng.wait_ge(sem, count)


def over_pairs(eng, step):
    step(0, 0, 0, True, False)
    with eng.Fori(0, (NP - 2) // 2) as i:
        step(2 * i + 1, i, 1, False, False)
        step(2 * i + 2, i + 1, 0, False, False)
    step(NP - 1, NP // 2 - 1, 1, False, True)


def pair_tokens(p):
    return bass.ds(p * PT, PT)


def pair_tiles(p):
    return bass.ds(p * 2, 2)


class Mem:
    pass


def open_stage(nc, ctx, tag):
    sems = []

    def sem(name):
        sems.append(nc.alloc_semaphore(f"{tag}_{name}"))
        return sems[-1]

    def clear():
        nc.clear_and_free_semaphores(sems)
        nc.all_engine_barrier()

    ctx.callback(clear)

    def sb(name, shape, dt=F32):
        return ctx.enter_context(nc.sbuf_tensor(f"{tag}_{name}", shape, dt))

    def ps(name, shape):
        size = int(np.prod(shape[1:]))
        whole = ctx.enter_context(nc.psum_tensor(f"{tag}_{name}", [P, -(-size // BANK) * BANK], F32))
        flat = whole[:, 0:size]
        if len(shape) == 2:
            return flat
        inner = {f"n{i}": n for i, n in enumerate(shape[1:])}
        return flat.rearrange(f"p ({' '.join(inner)}) -> p {' '.join(inner)}", **inner)

    return sem, sb, ps



class Tail:

    def __init__(self, sem, sb):
        self.r = sb("r", [P, 2, D])
        self.stats = sb("stats", [P, 2, 6])
        self.moments = sb("moments", [P, 2, 2])
        self.vare = sb("vare", [P, 2])
        self.rstd = sb("rstd", [P, 2])
        self.xn = sb("xn", [P, 2, D])
        self.y_done = sem("y_done")
        self.r_done = sem("r_done")
        self.moments_done = sem("moments_done")
        self.vare_done = sem("vare_done")
        self.rstd_done = sem("rstd_done")
        self.xn_done = sem("xn_done")
        self.x_stored = sem("x_stored")
        self.xT_done = sem("xT_done")
        self.xT_stored = sem("xT_stored")


def tail_residual(dve, tl, p, y, xb):
    after(dve, tl.y_done, p + 1)
    dve.tensor_tensor(tl.r[:], y, xb, ALU.add).then_inc(tl.r_done, 1)
    after(dve, tl.r_done, p + 1)


def tail_stats(dve, tl, p, r):
    for j in range(2):
        dve.bn_stats(tl.stats[:, j, :], r[:, j, :])
    dve.drain()
    for j in range(2):
        dve.bn_aggr(tl.moments[:, j, :], tl.stats[:, j, :]).then_inc(tl.moments_done, 1)


def tail_rstd(pool, mem, tl, p):
    after(pool, tl.moments_done, 2 * p + 2)
    pool.tensor_tensor(tl.vare[:], tl.moments[:, :, 1], mem.eps, ALU.add)\
        .then_inc(tl.vare_done, 1)
    after(pool, tl.vare_done, p + 1)
    pool.tensor_tensor(tl.rstd[:], tl.vare[:], mem.neg_half, ALU.pow).then_inc(tl.rstd_done, 1)


def tail_apply(dve, tl, p, r, xn_used):
    after(dve, tl.rstd_done, p + 1)
    after(dve, tl.moments_done, 2 * p + 2)
    after(dve, xn_used, p)
    for j in range(2):
        dve.tensor_scalar(tl.xn[:, j, :], r[:, j, :], tl.moments[:, j, 0:1], tl.rstd[:, j:j + 1],
                          ALU.subtract, ALU.mult).then_inc(tl.xn_done, 1)


def tail_store_x(pool, mem, tl, p):
    after(pool, tl.xn_done, 2 * p + 2)
    pool.tensor_copy(mem.x[:, pair_tiles(p), :], tl.xn[:]).then_inc(tl.x_stored, 1)


def tail_transpose(pe, mem, tl, p, bank):
    after(pe, tl.xn_done, 2 * p + 2)
    for db in range(DB):
        for j in range(2):
            last = pe.transpose(bank[:, db, j * P:(j + 1) * P], tl.xn[:, j, db * P:(db + 1) * P],
                                mem.ident)
    last.then_inc(tl.xT_done, 1)


def tail_store_xT(act, mem, tl, p, bank):
    after(act, tl.xT_done, p + 1)
    act.activation(mem.xT[:, :, pair_tokens(p)], bank, ACT.Copy).then_inc(tl.xT_stored, 1)


def project_T(pe, bank, w, moving):
    for m in range(DB):
        for db in range(DB):
            last = pe.matmul(bank[:, m, :], w[:, db, m * P:(m + 1) * P], moving(db),
                             start=(db == 0), stop=(db == DB - 1))
    return last


def project(pe, bank, featT, w):
    for j in range(2):
        for db in range(DB):
            last = pe.matmul(bank[:, j, :], featT[:, db, j * P:(j + 1) * P], w[:, db, :],
                             start=(db == 0), stop=(db == DB - 1))
    return last


def head_slots(q_even, q_odd):
    for group in range(4):
        for odd in range(2):
            yield (slice(32 * group, 32 * group + 32), 4 * (group % 2) + 2 * (group // 2) + odd,
                   q_odd if odd else q_even)


def over_pair(column):
    return column.unsqueeze(2).to_broadcast([P, DB, PT])


def over_pair(column):
    return column.unsqueeze(2).to_broadcast([P, DB, PT])


def over_pair(column):
    return column.unsqueeze(2).to_broadcast([P, DB, PT])


def over_pair(column):
    return column.unsqueeze(2).to_broadcast([P, DB, PT])


def over_pair(column):
    return column.unsqueeze(2).to_broadcast([P, DB, PT])


def over_pair(column):
    return column.unsqueeze(2).to_broadcast([P, DB, PT])


def over_pair(column):
    return column.unsqueeze(2).to_broadcast([P, DB, PT])


def over_pair(column):
    return column.unsqueeze(2).to_broadcast([P, DB, PT])


def over_pair(column):
    return column.unsqueeze(2).to_broadcast([P, DB, PT])


def over_pair(column):
    return column.unsqueeze(2).to_broadcast([P, DB, PT])


def over_pair(column):
    return column.unsqueeze(2).to_broadcast([P, DB, PT])



def gated_attention(nc, mem, x, xT0, wq, wk, wv, wo, wg, bg, diagonals_in, head_rows_in):
    with ExitStack() as ctx:
        sem, sb, ps = open_stage(nc, ctx, "ga")
        w_q, w_k, w_v, w_o = (sb(n, [P, DB, D]) for n in ("wq", "wk", "wv", "wo"))
        w_g = sb("wg", [P, DB, H])
        b_g = sb("bg", [H, 1])
        neg_bg = sb("neg_bg", [H, 1])
        head_rows = sb("head_rows", [H, H, P])
        diagonals = sb("diagonals", [P, HH, P])
        xt = [sb(f"xt{u}", [P, DB, PT]) for u in range(2)]
        xb = [sb(f"xb{u}", [P, 2, D]) for u in range(2)]
        qexp = sb("qexp", [P, DB, PT])
        kexp = sb("kexp", [P, DB, PT])
        qrelu = sb("qrelu", [P, DB, PT])
        krelu = sb("krelu", [P, DB, PT])
        qfeat = sb("qfeat", [P, DB, PT])
        q_even = [sb(f"q_even{u}", [P, DB, PT]) for u in range(2)]
        q_odd = [sb(f"q_odd{u}", [P, DB, PT]) for u in range(2)]
        k_T = [sb(f"kT{u}", [P, DB, PT]) for u in range(2)]
        v_sb = [sb(f"v{u}", [P, 2, D]) for u in range(2)]
        gexp = sb("gexp", [H, PT])
        gsum = sb("gsum", [H, PT])
        gate = [sb(f"gate{u}", [H, 2, P]) for u in range(2)]
        decay = [sb(f"decay{n}", [P, HH, P]) for n in range(2)]
        att = [sb(f"att{n}", [P, HH, P]) for n in range(2)]
        ctxn = sb("ctxn", [P, 2, D])
        ctxT = sb("ctxT", [P, DB, PT])
        tl = Tail(sem, sb)

        GB = ps("GB", [P, HH, P])
        S = [ps(f"S{n}", [P, HH, P]) for n in range(2)]
        O = ps("O", [P, 512])
        M = ps("M", [P, 2, PT])

        weights_loaded, consts_loaded = sem("weights_loaded"), sem("consts_loaded")
        xt_loaded = [sem(f"xt_loaded{u}") for u in range(2)]
        xb_loaded = [sem(f"xb_loaded{u}") for u in range(2)]
        neg_bg_done = sem("neg_bg_done")
        q_done, k_done, v_done, g_done = (sem(n) for n in ("q_done", "k_done", "v_done", "g_done"))
        qexp_done, kexp_done, gexp_done = sem("qexp_done"), sem("kexp_done"), sem("gexp_done")
        qrelu_done, qfeat_done, krelu_done = sem("qrelu_done"), sem("qfeat_done"), sem("krelu_done")
        q_ready, k_ready, v_ready = sem("q_ready"), sem("k_ready"), sem("v_ready")
        gsum_done, ginv_done, g_ready = sem("gsum_done"), sem("ginv_done"), sem("g_ready")
        gb_done, decay_done = sem("gb_done"), sem("decay_done")
        s_done, att_done = sem("s_done"), sem("att_done")
        o_done, ctx_ready, rows_done = sem("o_done"), sem("ctx_ready"), sem("rows_done")
        ctxT_done, ctxT_ready = sem("ctxT_done"), sem("ctxT_ready")

        block = ctx.enter_context(nc.Block())

        @block.sync
        def _(sp):
            def step(p, k, u, first, last):
                after(sp, g_done, p)
                sp.dma_start(xt[u][:], xT0[:, :, pair_tokens(p)]).then_inc(xt_loaded[u], 16)
                if first:
                    for dst, src in ((w_q, wq), (w_k, wk), (w_v, wv), (w_g, wg)):
                        sp.dma_start(dst[:], src).then_inc(weights_loaded, 16)
                    sp.dma_start(b_g[:], bg).then_inc(consts_loaded, 16)
                    sp.dma_start(head_rows[:], head_rows_in).then_inc(consts_loaded, 16)
                    sp.dma_start(diagonals[:], diagonals_in).then_inc(consts_loaded, 16)
                    mem.load_constants(sp, consts_loaded)
                    sp.dma_start(w_o[:], wo).then_inc(weights_loaded, 16)
                after(sp, tl.r_done, p)
                sp.dma_start(xb[u][:], x[:, pair_tiles(p), :]).then_inc(xb_loaded[u], 16)

            over_pairs(sp, step)

        consts_all = 16 * 4

        @block.gpsimd
        def _(pool):
            def masked_q(p, u):
                after(pool, qfeat_done, p + 1)
                pool.tensor_tensor(q_even[u][:], qfeat[:], over_pair(mem.even_rows), ALU.mult)\
                    .then_inc(q_ready, 1)
                pool.tensor_tensor(q_odd[u][:], qfeat[:], over_pair(mem.odd_rows), ALU.mult)\
                    .then_inc(q_ready, 1)

            def step(p, k, u, first, last):
                if not first:
                    tail_rstd(pool, mem, tl, p - 1)
                    tail_store_x(pool, mem, tl, p - 1)
                if not last:
                    masked_q(p + 1, 1 - u)

            pool.wait_ge(consts_loaded, consts_all)
            masked_q(0, 0)
            over_pairs(pool, step)
            tail_rstd(pool, mem, tl, NP - 1)
            tail_store_x(pool, mem, tl, NP - 1)

        @block.scalar
        def _(act):
            def exp_q(p):
                after(act, q_done, p + 1)
                act.activation(qexp[:], M[:], ACT.Exp, scale=HEAD_SCALE).then_inc(qexp_done, 1)

            def exp_k(p):
                after(act, k_done, p + 1)
                act.activation(kexp[:], M[:], ACT.Exp).then_inc(kexp_done, 1)

            def copy_v(p, u):
                after(act, v_done, p + 1)
                act.activation(v_sb[u][:], M[:], ACT.Copy).then_inc(v_ready, 1)

            def exp_g(p):
                after(act, g_done, p + 1)
                act.activation(gexp[:], M[0:H, 0, :], ACT.Exp, bias=neg_bg[:], scale=-1.0)\
                    .then_inc(gexp_done, 1)

            def copy_o(p, j):
                after(act, o_done, 2 * p + j + 1)
                act.activation(ctxn[:, j, :], O[:, 0:D], ACT.Copy).then_inc(ctx_ready, 1)

            def copy_ctxT(p):
                after(act, ctxT_done, p + 1)
                act.activation(ctxT[:], M[:], ACT.Copy).then_inc(ctxT_ready, 1)

            def step(p, k, u, first, last):
                if not first:
                    copy_ctxT(p - 1)
                    tail_store_xT(act, mem, tl, p - 1, M[:])
                if not last:
                    exp_q(p + 1)
                copy_o(p, 0)
                if not last:
                    exp_k(p + 1)
                    copy_v(p + 1, 1 - u)
                copy_o(p, 1)
                if not last:
                    exp_g(p + 1)

            exp_q(0)
            exp_k(0)
            copy_v(0, 0)
            act.wait_ge(neg_bg_done, 1)
            exp_g(0)
            over_pairs(act, step)
            copy_ctxT(NP - 1)
            tail_store_xT(act, mem, tl, NP - 1, M[:])

        @block.vector
        def _(dve):
            def feature_q(p, u):
                after(dve, qexp_done, p + 1)
                dve.tensor_scalar(qrelu[:], M[:], HEAD_SCALE, 0.0, ALU.mult, ALU.max)\
                    .then_inc(qrelu_done, 1)
                after(dve, qrelu_done, p + 1)
                after(dve, q_ready, 2 * p)
                dve.scalar_tensor_tensor(qfeat[:], qexp[:], 1.0, qrelu[:], ALU.min, ALU.add)\
                    .then_inc(qfeat_done, 1)

            def feature_k(p, u):
                after(dve, kexp_done, p + 1)
                dve.tensor_scalar(krelu[:], M[:], 0.0, None, ALU.max).then_inc(krelu_done, 1)
                after(dve, krelu_done, p + 1)
                dve.scalar_tensor_tensor(k_T[u][:], kexp[:], 1.0, krelu[:], ALU.min, ALU.add)\
                    .then_inc(k_ready, 1)

            def gates(p, u):
                after(dve, gexp_done, p + 1)
                dve.tensor_scalar(gsum[:], gexp[:], 1.0, None, ALU.add).then_inc(gsum_done, 1)
                after(dve, gsum_done, p + 1)
                dve.reciprocal(gate[u][:], gsum[:]).then_inc(ginv_done, 1)
                after(dve, ginv_done, p + 1)
                dve.memset(gate[u][:, :, 0:1], 0.0).then_inc(g_ready, 1)

            def half(p, n):
                h = 4 * p + n
                after(dve, att_done, h - 1)
                after(dve, gb_done, h + 1)
                dve.tensor_tensor_scan(decay[n % 2][:].rearrange("p h t -> p (h t)"),
                                       GB[:].rearrange("p h t -> p (h t)"),
                                       diagonals[:].rearrange("p h t -> p (h t)"),
                                       0.0, ALU.mult, ALU.add).then_inc(decay_done, 1)
                after(dve, decay_done, h + 1)
                after(dve, s_done, h + 1)
                dve.tensor_tensor(att[n % 2][:], S[n % 2][:], decay[n % 2][:], ALU.mult).then_inc(att_done, 1)

            def step(p, k, u, first, last):
                half(p, 0)
                half(p, 1)
                if not first:
                    dve.wait_ge(xb_loaded[1 - u], 16 * (k + u))
                    tail_residual(dve, tl, p - 1, M[:], xb[1 - u][:])
                    tail_stats(dve, tl, p - 1, tl.r)
                half(p, 2)
                if not first:
                    tail_apply(dve, tl, p - 1, tl.r, tl.x_stored)
                if not last:
                    feature_q(p + 1, 1 - u)
                half(p, 3)
                if not last:
                    feature_k(p + 1, 1 - u)
                    gates(p + 1, 1 - u)

            dve.wait_ge(consts_loaded, consts_all)
            dve.tensor_scalar(neg_bg[:], b_g[:], -1.0, None, ALU.mult).then_inc(neg_bg_done, 1)
            feature_q(0, 0)
            feature_k(0, 0)
            gates(0, 0)
            over_pairs(dve, step)
            dve.wait_ge(xb_loaded[1], 16 * (NP // 2))
            tail_residual(dve, tl, NP - 1, M[:], xb[1][:])
            tail_stats(dve, tl, NP - 1, tl.r)
            tail_apply(dve, tl, NP - 1, tl.r, tl.x_stored)

        @block.tensor
        def _(pe):
            def proj_q(p, k, u):
                pe.wait_ge(xt_loaded[u], 16 * (k + 1))
                project_T(pe, M, w_q, lambda db: xt[u][:, db, :]).then_inc(q_done, 1)

            def proj_k(p, u):
                after(pe, qfeat_done, p + 1)
                project_T(pe, M, w_k, lambda db: xt[u][:, db, :]).then_inc(k_done, 1)

            def proj_v(p, u):
                after(pe, k_ready, p + 1)
                project(pe, M, xt[u], w_v).then_inc(v_done, 1)

            def proj_g(p, u):
                after(pe, v_ready, p + 1)
                for db in range(DB):
                    last = pe.matmul(M[0:H, 0, :], w_g[:, db, :], xt[u][:, db, :],
                                     start=(db == 0), stop=(db == DB - 1))
                last.then_inc(g_done, 1)

            def spread_gates(p, n, u):
                h = 4 * p + n
                after(pe, g_ready, p + 1)
                after(pe, decay_done, h)
                blk = n % 2
                for s in range(HH):
                    head = HH * blk + slot_head(s)
                    last = pe.matmul(GB[:, s, :], head_rows[:, head, :], gate[u][:, n // 2, :],
                                     start=True, stop=True)
                last.then_inc(gb_done, 1)

            def scores(p, n, u):
                h = 4 * p + n
                blk, tok = n % 2, slice((n // 2) * P, (n // 2 + 1) * P)
                after(pe, q_ready, 2 * p + 2)
                after(pe, k_ready, p + 1)
                after(pe, att_done, h - 1)
                for rows, s, q in head_slots(q_even[u], q_odd[u]):
                    if rows.start >= 64 and s % 4 == 2:
                        after(pe, rows_done, 2 * h + (1 if rows.start == 64 else 2))
                    last = pe.matmul(S[n % 2][:, s, :], k_T[u][rows, blk, tok], q[rows, blk, tok],
                                     start=True, stop=True)
                    if rows.start < 64 and s % 4 == 1:
                        last.then_inc(rows_done, 1)
                last.then_inc(s_done, 1)

            def values(p, n, u):
                h = 4 * p + n
                blk, j = n % 2, n // 2
                after(pe, att_done, h + 1)
                after(pe, v_ready, p + 1)
                after(pe, ctx_ready, 2 * p + j)
                for s in range(HH):
                    c = (HH * blk + slot_head(s)) * DH
                    last = pe.matmul(O[:, c:c + DH], att[n % 2][:, s, :], v_sb[u][:, j, c:c + DH],
                                     start=True, stop=True)
                if blk:
                    last.then_inc(o_done, 1)

            def transpose_ctx(p):
                after(pe, ctx_ready, 2 * p + 2)
                for db in range(DB):
                    for j in range(2):
                        last = pe.transpose(M[:, db, j * P:(j + 1) * P], ctxn[:, j, db * P:(db + 1) * P],
                                            mem.ident)
                last.then_inc(ctxT_done, 1)

            def output(p):
                after(pe, ctxT_ready, p + 1)
                project(pe, M, ctxT, w_o).then_inc(tl.y_done, 1)

            def step(p, k, u, first, last):
                spread_gates(p, 0, u)
                scores(p, 0, u)
                if not first:
                    after(pe, gexp_done, p + 1)
                    transpose_ctx(p - 1)
                spread_gates(p, 1, u)
                scores(p, 1, u)
                if not first:
                    output(p - 1)
                values(p, 0, u)
                spread_gates(p, 2, u)
                scores(p, 2, u)
                values(p, 1, u)
                if not first:
                    tail_transpose(pe, mem, tl, p - 1, M)
                if not last:
                    if not first:
                        after(pe, tl.xT_stored, p)
                    proj_q(p + 1, k + u, 1 - u)
                spread_gates(p, 3, u)
                scores(p, 3, u)
                if not last:
                    proj_k(p + 1, 1 - u)
                values(p, 2, u)
                if not last:
                    proj_v(p + 1, 1 - u)
                values(p, 3, u)
                if not last:
                    proj_g(p + 1, 1 - u)

            pe.wait_ge(weights_loaded, 16 * 5)
            pe.wait_ge(consts_loaded, consts_all)
            proj_q(0, 0, 0)
            proj_k(0, 0)
            proj_v(0, 0)
            proj_g(0, 0)
            over_pairs(pe, step)
            pe.wait_ge(tl.xT_stored, NP - 1)
            transpose_ctx(NP - 1)
            output(NP - 1)
            tail_transpose(pe, mem, tl, NP - 1, M)



def cross_attention(nc, mem, tag, ctxT_in, wq, wk, wv, wo, bq, bk, bv, bo):
    with ExitStack() as ctx:
        sem, sb, ps = open_stage(nc, ctx, tag)
        w_q, w_k, w_v, w_o = (sb(n, [P, DB, D]) for n in ("wq", "wk", "wv", "wo"))
        b_q, b_k = sb("bq", [P, DB]), sb("bk", [P, DB])
        b_v, b_o = sb("bv", [P, D]), sb("bo", [P, D])
        bq_even, bq_odd = sb("bq_even", [P, DB]), sb("bq_odd", [P, DB])
        ct = [sb(f"ct{u}", [P, DB, PT]) for u in range(2)]
        xb = [sb(f"xb{u}", [P, 2, D]) for u in range(2)]
        q_even = [sb(f"q_even{u}", [P, DB, PT]) for u in range(2)]
        q_odd = [sb(f"q_odd{u}", [P, DB, PT]) for u in range(2)]
        k_T = [sb(f"kT{u}", [P, DB, PT]) for u in range(2)]
        v_sb = [sb(f"v{u}", [P, 2, H, DH + 1]) for u in range(2)]
        row_max = sb("row_max", [P, 2, HH])
        prob = [sb(f"prob{n}", [P, HH, P]) for n in range(2)]
        probT = [sb(f"probT{a}", [P, HH // 2, P]) for a in range(2)]
        inv = sb("inv", [P, 2, H])
        ctxn = sb("ctxn", [P, 2, D])
        ctxT = sb("ctxT", [P, DB, PT])
        tl = Tail(sem, sb)

        S = [ps(f"S{n}", [P, HH, P]) for n in range(2)]
        PTB = [ps(f"PT{a}", [P, HH // 2, P]) for a in range(2)]
        O = ps("O", [P, H, 32])
        M = ps("M", [P, 2, PT])

        weights_loaded = sem("weights_loaded")
        ct_loaded = [sem(f"ct_loaded{u}") for u in range(2)]
        bias_ready, ones_ready, xb_ready = sem("bias_ready"), sem("ones_ready"), sem("xb_ready")
        q_done, k_done, v_done = (sem(n) for n in ("q_done", "k_done", "v_done"))
        q_ready, k_ready, v_ready = sem("q_ready"), sem("k_ready"), sem("v_ready")
        s_done, max_done, shifted, exp_done = sem("s_done"), sem("max_done"), sem("shifted"), sem("exp_done")
        pT_done, pT_ready = [sem(f"pT_done{a}") for a in range(2)], [sem(f"pT_ready{a}") for a in range(2)]
        o_done, inv_done, ctx_ready = sem("o_done"), sem("inv_done"), sem("ctx_ready")
        rows_done = sem("rows_done")
        ctxT_done, ctxT_ready = sem("ctxT_done"), sem("ctxT_ready")

        block = ctx.enter_context(nc.Block())

        @block.sync
        def _(sp):
            def step(p, k, u, first, last):
                after(sp, v_done, p)
                sp.dma_start(ct[u][:], ctxT_in[:, :, pair_tokens(p)]).then_inc(ct_loaded[u], 16)

            for dst, src in ((w_q, wq), (w_k, wk), (w_v, wv), (w_o, wo)):
                sp.dma_start(dst[:], src).then_inc(weights_loaded, 16)
            for dst, src in ((b_q, bq), (b_k, bk), (b_v, bv.to_broadcast([P, D])), (b_o, bo.to_broadcast([P, D]))):
                sp.dma_start(dst[:], src).then_inc(weights_loaded, 16)
            over_pairs(sp, step)

        @block.gpsimd
        def _(pool):
            def add_bias(p, u):
                pool.tensor_tensor(xb[u][:], mem.x[:, pair_tiles(p), :],
                                   b_o[:].unsqueeze(1).to_broadcast([P, 2, D]), ALU.add).then_inc(xb_ready, 1)

            def step(p, k, u, first, last):
                if not first:
                    tail_rstd(pool, mem, tl, p - 1)
                    tail_store_x(pool, mem, tl, p - 1)
                if not last:
                    after(pool, tl.r_done, p)
                    add_bias(p + 1, 1 - u)

            for u in range(2):
                pool.memset(v_sb[u][:, :, :, DH:DH + 1], 1.0).then_inc(ones_ready, 1)
            pool.wait_ge(weights_loaded, 16 * 8)
            add_bias(0, 0)
            over_pairs(pool, step)
            tail_rstd(pool, mem, tl, NP - 1)
            tail_store_x(pool, mem, tl, NP - 1)

        @block.scalar
        def _(act):
            def copy_q(p, u):
                after(act, q_done, p + 1)
                for q, rows, bias in ((q_even[u], mem.even_rows, bq_even), (q_odd[u], mem.odd_rows, bq_odd)):
                    for m in range(DB):
                        act.activation(q[:, m, :], M[:, m, :], ACT.Identity, bias=bias[:, m:m + 1],
                                       scale=rows).then_inc(q_ready, 1)

            def copy_k(p, u):
                after(act, k_done, p + 1)
                for m in range(DB):
                    act.activation(k_T[u][:, m, :], M[:, m, :], ACT.Identity, bias=b_k[:, m:m + 1])\
                        .then_inc(k_ready, 1)

            def exp(p, n):
                after(act, shifted, 4 * p + n + 1)
                act.activation(prob[n % 2][:], prob[n % 2][:], ACT.Exp, scale=HEAD_SCALE).then_inc(exp_done, 1)

            def copy_pT(p, n):
                after(act, pT_done[0], 4 * p + n + 1)
                act.activation(probT[0][:], PTB[0][:], ACT.Copy).then_inc(pT_ready[0], 1)

            def copy_ctxT(p):
                after(act, ctxT_done, p + 1)
                act.activation(ctxT[:], M[:], ACT.Copy).then_inc(ctxT_ready, 1)

            def step(p, k, u, first, last):
                if not first:
                    copy_ctxT(p - 1)
                exp(p, 0)
                copy_pT(p, 0)
                exp(p, 1)
                exp(p, 2)
                copy_pT(p, 1)
                if not first:
                    tail_store_xT(act, mem, tl, p - 1, M[:])
                exp(p, 3)
                if not last:
                    copy_q(p + 1, 1 - u)
                copy_pT(p, 2)
                if not last:
                    copy_k(p + 1, 1 - u)
                copy_pT(p, 3)

            act.wait_ge(bias_ready, 2)
            copy_q(0, 0)
            copy_k(0, 0)
            over_pairs(act, step)
            copy_ctxT(NP - 1)
            tail_store_xT(act, mem, tl, NP - 1, M[:])

        @block.vector
        def _(dve):
            def shift(p, n):
                h = 4 * p + n
                after(dve, s_done, h + 1)
                dve.tensor_reduce(row_max[:, n % 2, :], S[n % 2][:], AX.X, ALU.max).then_inc(max_done, 1)
                after(dve, max_done, h + 1)
                dve.tensor_tensor(prob[n % 2][:], S[n % 2][:],
                                  row_max[:, n % 2, :].unsqueeze(2).to_broadcast([P, HH, P]),
                                  ALU.subtract).then_inc(shifted, 1)

            def copy_pT(p, n):
                after(dve, pT_done[1], 4 * p + n + 1)
                dve.tensor_copy(probT[1][:], PTB[1][:]).then_inc(pT_ready[1], 1)

            def copy_v(p, u):
                after(dve, v_done, p + 1)
                dve.tensor_tensor(v_sb[u][:, :, :, 0:DH], M[:].rearrange("p j (h d) -> p j h d", h=H),
                                  b_v[:].rearrange("p (h d) -> p h d", h=H).unsqueeze(1)
                                  .to_broadcast([P, 2, H, DH]), ALU.add).then_inc(v_ready, 1)

            def normalize(p, j):
                after(dve, o_done, 2 * p + j + 1)
                dve.reciprocal(inv[:, j, :], O[:, :, DH]).then_inc(inv_done, 1)
                after(dve, inv_done, 2 * p + j + 1)
                dve.tensor_tensor(ctxn[:, j, :].rearrange("p (h d) -> p h d", h=H), O[:, :, 0:DH],
                                  inv[:, j, :].unsqueeze(2).to_broadcast([P, H, DH]), ALU.mult)\
                    .then_inc(ctx_ready, 1)

            def residual(p, u):
                after(dve, xb_ready, p + 1)
                tail_residual(dve, tl, p, M[:], xb[u][:])
                tail_stats(dve, tl, p, tl.r)

            def step(p, k, u, first, last):
                shift(p, 0)
                shift(p, 1)
                if not first:
                    residual(p - 1, 1 - u)
                copy_pT(p, 0)
                shift(p, 2)
                if not first:
                    tail_apply(dve, tl, p - 1, tl.r, tl.x_stored)
                copy_pT(p, 1)
                shift(p, 3)
                normalize(p, 0)
                copy_pT(p, 2)
                copy_pT(p, 3)
                if not last:
                    copy_v(p + 1, 1 - u)
                normalize(p, 1)

            dve.wait_ge(weights_loaded, 16 * 8)
            dve.tensor_scalar(bq_even[:], b_q[:], mem.even_rows, None, ALU.mult).then_inc(bias_ready, 1)
            dve.tensor_scalar(bq_odd[:], b_q[:], mem.odd_rows, None, ALU.mult).then_inc(bias_ready, 1)
            copy_v(0, 0)
            over_pairs(dve, step)
            residual(NP - 1, 1)
            tail_apply(dve, tl, NP - 1, tl.r, tl.x_stored)

        @block.tensor
        def _(pe):
            def proj_q(p):
                project_T(pe, M, w_q, lambda db: mem.xT[:, db, pair_tokens(p)]).then_inc(q_done, 1)

            def proj_k(p, k, u):
                pe.wait_ge(ct_loaded[u], 16 * (k + 1))
                after(pe, q_ready, 4 * p + 4)
                project_T(pe, M, w_k, lambda db: ct[u][:, db, :]).then_inc(k_done, 1)

            def proj_v(p, u):
                after(pe, k_ready, 2 * p + 2)
                project(pe, M, ct[u], w_v).then_inc(v_done, 1)

            def scores(p, n, u):
                h = 4 * p + n
                blk, tok = n % 2, slice((n // 2) * P, (n // 2 + 1) * P)
                after(pe, q_ready, 4 * p + 4)
                after(pe, k_ready, 2 * p + 2)
                after(pe, shifted, h - 1)
                for rows, s, q in head_slots(q_even[u], q_odd[u]):
                    if rows.start >= 64 and s % 4 == 2:
                        after(pe, rows_done, 2 * h + (1 if rows.start == 64 else 2))
                    last = pe.matmul(S[n % 2][:, s, :], q[rows, blk, tok], k_T[u][rows, blk, tok],
                                     start=True, stop=True)
                    if rows.start < 64 and s % 4 == 1:
                        last.then_inc(rows_done, 1)
                last.then_inc(s_done, 1)

            def transpose_p(p, n):
                h = 4 * p + n
                after(pe, exp_done, h + 1)
                for a in range(2):
                    after(pe, pT_ready[a], h)
                    for s in range(HH // 2):
                        last = pe.transpose(PTB[a][:, s, :], prob[n % 2][:, a * (HH // 2) + s, :], mem.ident)
                    last.then_inc(pT_done[a], 1)

            def values(p, n, u):
                h = 4 * p + n
                blk, j = n % 2, n // 2
                after(pe, v_ready, p + 1)
                after(pe, ctx_ready, 2 * p + j)
                for a in range(2):
                    after(pe, pT_ready[a], h + 1)
                    for s in range(HH // 2):
                        head = HH * blk + slot_head(a * (HH // 2) + s)
                        last = pe.matmul(O[:, head, 0:DH + 1], probT[a][:, s, :], v_sb[u][:, j, head, :],
                                         start=True, stop=True)
                if blk:
                    last.then_inc(o_done, 1)

            def transpose_ctx(p):
                after(pe, ctx_ready, 2 * p + 2)
                for db in range(DB):
                    for j in range(2):
                        last = pe.transpose(M[:, db, j * P:(j + 1) * P], ctxn[:, j, db * P:(db + 1) * P],
                                            mem.ident)
                last.then_inc(ctxT_done, 1)

            def output(p):
                after(pe, ctxT_ready, p + 1)
                project(pe, M, ctxT, w_o).then_inc(tl.y_done, 1)

            def step(p, k, u, first, last):
                scores(p, 0, u)
                if not first:
                    after(pe, v_ready, p + 1)
                    transpose_ctx(p - 1)
                scores(p, 1, u)
                if not first:
                    output(p - 1)
                transpose_p(p, 0)
                scores(p, 2, u)
                values(p, 0, u)
                transpose_p(p, 1)
                if not first:
                    tail_transpose(pe, mem, tl, p - 1, M)
                scores(p, 3, u)
                values(p, 1, u)
                if not last:
                    if not first:
                        after(pe, tl.xT_stored, p)
                    proj_q(p + 1)
                transpose_p(p, 2)
                if not last:
                    proj_k(p + 1, k + u, 1 - u)
                values(p, 2, u)
                transpose_p(p, 3)
                if not last:
                    proj_v(p + 1, 1 - u)
                values(p, 3, u)

            pe.wait_ge(weights_loaded, 16 * 8)
            pe.wait_ge(ones_ready, 2)
            proj_q(0)
            proj_k(0, 0, 0)
            proj_v(0, 0)
            over_pairs(pe, step)
            pe.wait_ge(tl.xT_stored, NP - 1)
            transpose_ctx(NP - 1)
            output(NP - 1)
            tail_transpose(pe, mem, tl, NP - 1, M)



def router(nc, mem, tag, w_router, decide):
    with ExitStack() as ctx:
        sem, sb, ps = open_stage(nc, ctx, tag)
        CHUNK, NCH = 4 * P, T // (4 * P)
        w_r = sb("wr", [P, DB, E])
        logitsT = [sb(f"logitsT{a}", [E, CHUNK]) for a in range(2)]
        LT = [ps(f"LT{a}", [P, CHUNK]) for a in range(2)]
        L = ps("L", [P, NB, E])
        w_loaded, lt_done, lt_ready, l_done = sem("w_loaded"), sem("lt_done"), sem("lt_ready"), sem("l_done")
        rest = decide(nc, mem, sem, sb, ps, L, l_done)
        block = ctx.enter_context(nc.Block())

        @block.sync
        def _(sp):
            sp.dma_start(w_r[:], w_router).then_inc(w_loaded, 16)

        @block.tensor
        def _(pe):
            pe.wait_ge(w_loaded, 16)
            for c in range(NCH + 1):
                if c < NCH:
                    after(pe, lt_ready, c - 1)
                    for db in range(DB):
                        last = pe.matmul(LT[c % 2][0:E, :], w_r[:, db, :], mem.xT[:, db, c * CHUNK:(c + 1) * CHUNK],
                                         start=(db == 0), stop=(db == DB - 1))
                    last.then_inc(lt_done, 1)
                if c:
                    pe.wait_ge(lt_ready, c)
                    for j in range(4):
                        last = pe.transpose(L[:, 4 * (c - 1) + j, :], logitsT[(c - 1) % 2][:, j * P:(j + 1) * P],
                                            mem.ident[0:E, 0:E])
            last.then_inc(l_done, 1)
            rest["tensor"](pe)

        @block.scalar
        def _(act):
            for c in range(NCH):
                act.wait_ge(lt_done, c + 1)
                act.activation(logitsT[c % 2][:], LT[c % 2][0:E, :], ACT.Copy).then_inc(lt_ready, 1)
            rest["scalar"](act)

        @block.vector
        def _(dve):
            rest["vector"](dve)


def over_experts(ap):
    return ap.unsqueeze(2).to_broadcast([P, NB, E])


class Softmax:

    def __init__(self, sem, sb, L, l_done):
        self.L, self.l_done = L, l_done
        self.top, self.total, self.inv = sb("top", [P, NB]), sb("total", [P, NB]), sb("inv", [P, NB])
        self.z, self.e, self.p = sb("z", [P, NB, E]), sb("e", [P, NB, E]), sb("p", [P, NB, E])
        self.z_done, self.e_done = sem("z_done"), sem("e_done")

    def scalar(self, act):
        act.wait_ge(self.z_done, 1)
        act.activation(self.e[:], self.z[:], ACT.Exp).then_inc(self.e_done, 1)

    def vector(self, dve, link):
        dve.wait_ge(self.l_done, 1)
        link(dve.tensor_reduce(self.top[:], self.L[:], AX.X, ALU.max))
        dve.tensor_tensor(self.z[:], self.L[:], over_experts(self.top[:]), ALU.subtract)\
            .then_inc(self.z_done, 1)
        dve.wait_ge(self.e_done, 1)
        link(dve.tensor_reduce(self.total[:], self.e[:], AX.X, ALU.add))
        link(dve.reciprocal(self.inv[:], self.total[:]))
        link(dve.tensor_tensor(self.p[:], self.e[:], over_experts(self.inv[:]), ALU.mult))


def chained(dve, sem):
    count = [0]

    def link(instruction):
        count[0] += 1
        instruction.then_inc(sem, 1)
        dve.wait_ge(sem, count[0])

    return link


def top_experts(nc, mem, sem, sb, ps, L, l_done):
    soft = Softmax(sem, sb, L, l_done)
    above, equal = sb("above", [P, NB, E, E]), sb("equal", [P, NB, E, E])
    rank, chosen, kept = sb("rank", [P, NB, E]), sb("chosen", [P, NB, E]), sb("kept", [P, NB, E])
    kept_sum, kept_inv = sb("kept_sum", [P, NB]), sb("kept_inv", [P, NB])
    chain = sem("chain")

    def vector(dve):
        link = chained(dve, chain)
        soft.vector(dve, link)
        others = soft.p[:].unsqueeze(2).to_broadcast([P, NB, E, E])
        own = soft.p[:].unsqueeze(3).to_broadcast([P, NB, E, E])
        before = mem.lower8.unsqueeze(1).to_broadcast([P, NB, E, E])
        dve.tensor_tensor(above[:], others, own, ALU.is_gt)
        link(dve.tensor_tensor(equal[:], others, own, ALU.is_equal))
        link(dve.tensor_tensor(equal[:], equal[:], before, ALU.mult))
        link(dve.tensor_tensor(above[:], above[:], equal[:], ALU.add))
        link(dve.tensor_reduce(rank[:], above[:], AX.X, ALU.add))
        link(dve.tensor_scalar(chosen[:], rank[:], float(TOPK), None, ALU.is_lt))
        link(dve.tensor_tensor(kept[:], soft.p[:], chosen[:], ALU.mult))
        link(dve.tensor_reduce(kept_sum[:], kept[:], AX.X, ALU.add))
        link(dve.reciprocal(kept_inv[:], kept_sum[:]))
        link(dve.tensor_tensor(mem.gates[:], kept[:], over_experts(kept_inv[:]), ALU.mult))

    return {"tensor": lambda pe: None, "scalar": soft.scalar, "vector": vector}


BITS = 30


def selected_expert(nc, mem, sem, sb, ps, L, l_done):
    soft = Softmax(sem, sb, L, l_done)
    bit, cand, thr = (sb(n, [P, E], U32) for n in ("bit", "cand", "thr"))
    enough = sb("enough", [P, E], U32)
    flags, part = sb("flags", [P, E, NB]), sb("part", [P, E])
    above, equal, first = (sb(n, [P, NB, E]) for n in ("above", "equal", "first"))
    in_tile, upto, value, marks = (sb(n, [P, NB, E]) for n in ("in_tile", "upto", "value", "marks"))
    some, best = sb("some", [P, NB]), sb("best", [P, NB])
    need = sb("need", [P, E])
    TOT = ps("TOT", [P, E])
    BEFORE = ps("BEFORE", [P, NB, E])
    TILES = ps("TILES", [P, NB, E])
    chain, thr_done = sem("chain"), sem("thr_done")
    part_done, tot_done, bit_done = sem("part_done"), sem("tot_done"), sem("bit_done")
    cand_done, flags_done, enough_done = sem("cand_done"), sem("flags_done"), sem("enough_done")
    above_done, above_tot, equal_done, equal_tot = (sem(n) for n in ("above_done", "above_tot", "equal_done", "equal_tot"))

    def tensor(pe):
        with pe.Fori(0, BITS) as i:
            pe.wait_ge(part_done, i + 1)
            pe.matmul(TOT[:], mem.ones, part[:], start=True, stop=True).then_inc(tot_done, 1)
        pe.wait_ge(above_done, 1)
        pe.matmul(TOT[:], mem.ones, part[:], start=True, stop=True).then_inc(above_tot, 1)
        pe.wait_ge(equal_done, 1)
        pe.matmul(BEFORE[:].rearrange("p b e -> p (b e)"), mem.earlier,
                  equal[:].rearrange("p b e -> p (b e)"), start=True, stop=True)
        pe.matmul(TILES[:].rearrange("p b e -> p (b e)"), mem.ones,
                  equal[:].rearrange("p b e -> p (b e)"), start=True, stop=True).then_inc(equal_tot, 1)

    def vector(dve):
        link = chained(dve, chain)
        soft.vector(dve, link)
        by_expert = soft.p[:].rearrange("p b e -> p e b")
        thr_f = thr[:].bitcast(F32)
        dve.memset(thr[:], 0)
        link(dve.memset(bit[:], 1 << (BITS - 1)))
        with dve.Fori(0, BITS) as i:
            dve.tensor_tensor(cand[:], thr[:], bit[:], ALU.bitwise_or).then_inc(cand_done, 1)
            dve.wait_ge(cand_done, i + 1)
            dve.tensor_tensor(flags[:], by_expert, cand[:].bitcast(F32).unsqueeze(2).to_broadcast([P, E, NB]),
                              ALU.is_ge).then_inc(flags_done, 1)
            dve.wait_ge(flags_done, i + 1)
            dve.tensor_reduce(part[:], flags[:], AX.X, ALU.add).then_inc(part_done, 1)
            dve.wait_ge(tot_done, i + 1)
            dve.tensor_scalar(enough[:], TOT[:], float(CAP), None, ALU.is_ge).then_inc(enough_done, 1)
            dve.wait_ge(enough_done, i + 1)
            dve.tensor_scalar(bit[:], bit[:], 1, None, ALU.logical_shift_right).then_inc(bit_done, 1)
            dve.copy_predicated(thr[:], enough[:], cand[:]).then_inc(thr_done, 1)
            dve.wait_ge(bit_done, i + 1)
            dve.wait_ge(thr_done, i + 1)
        thr_b = thr_f.unsqueeze(1).to_broadcast([P, NB, E])
        link(dve.tensor_tensor(above[:], soft.p[:], thr_b, ALU.is_gt))
        dve.tensor_reduce(part[:], above[:].rearrange("p b e -> p e b"), AX.X, ALU.add).then_inc(above_done, 1)
        dve.tensor_tensor(equal[:], soft.p[:], thr_b, ALU.is_equal).then_inc(equal_done, 1)
        dve.wait_ge(above_tot, 1)
        link(dve.tensor_scalar(need[:], TOT[:], -1.0, float(CAP), ALU.mult, ALU.add))
        dve.wait_ge(equal_tot, 1)
        link(dve.tensor_copy(in_tile[:], TILES[:]))
        dve.wait_ge(equal_done, 1)
        for e in range(E):
            last = dve.tensor_tensor_scan(upto[:, :, e], in_tile[:, :, e], mem.zeros32, 0.0, ALU.add, ALU.add)
        link(last)
        link(dve.tensor_tensor(upto[:], upto[:], in_tile[:], ALU.subtract))
        link(dve.tensor_tensor(upto[:], BEFORE[:], upto[:], ALU.add))
        link(dve.tensor_tensor(first[:], upto[:], need[:].unsqueeze(1).to_broadcast([P, NB, E]), ALU.is_lt))
        link(dve.tensor_tensor(first[:], first[:], equal[:], ALU.mult))
        link(dve.tensor_tensor(above[:], above[:], first[:], ALU.add))
        link(dve.tensor_reduce(some[:], above[:], AX.X, ALU.max))
        link(dve.tensor_scalar(above[:], above[:], 1.0, 4.0, ALU.subtract, ALU.mult))
        link(dve.tensor_tensor(above[:], above[:], over_experts(some[:]), ALU.mult))
        link(dve.tensor_tensor(value[:], soft.p[:], above[:], ALU.add))
        link(dve.tensor_reduce(best[:], value[:], AX.X, ALU.max))
        link(dve.tensor_tensor(marks[:], value[:], over_experts(best[:]), ALU.is_equal))
        link(dve.tensor_tensor(marks[:], marks[:], mem.rising8.unsqueeze(1).to_broadcast([P, NB, E]), ALU.mult))
        link(dve.tensor_reduce(best[:], marks[:], AX.X, ALU.max))
        link(dve.tensor_tensor(marks[:], marks[:], over_experts(best[:]), ALU.is_equal))
        link(dve.tensor_tensor(mem.gates[:], soft.p[:], marks[:], ALU.mult))

    return {"tensor": tensor, "scalar": soft.scalar, "vector": vector}



def experts(nc, mem, tag, w_up, w_down, width, gelu):
    with ExitStack() as ctx:
        sem, sb, ps = open_stage(nc, ctx, tag)
        MB = width // P
        CHUNK, NCH = 4 * P, T // (4 * P)
        up = [sb(f"up{v}", [P, DB, width]) for v in range(2)]
        down = [sb(f"down{v}", [P, MB, D]) for v in range(2)]
        hT = [sb(f"hT{m}", [P, CHUNK]) for m in range(4)]
        HB = [ps(f"HB{m}", [P, CHUNK]) for m in range(4)]
        YB = [ps(f"YB{t}", [P, 512]) for t in range(4)]
        w_loaded = [sem(f"w_loaded{v}") for v in range(2)]
        up_done, gelu_done, y_done, added = sem("up_done"), sem("gelu_done"), sem("y_done"), sem("added")
        block = ctx.enter_context(nc.Block())

        def over_chunks(eng, step):
            with eng.Fori(0, E // 2) as i:
                for v in range(2):
                    with eng.Fori(0, NCH) as c:
                        step(i, v, c, NCH * (2 * i + v) + c)

        @block.sync
        def _(sp):
            for e in range(E):
                if e >= 2:
                    sp.wait_ge(y_done, 4 * NCH * (e - 1))
                sp.dma_start(up[e % 2][:], w_up[:, :, e, :]).then_inc(w_loaded[e % 2], 16)
                sp.dma_start(down[e % 2][:], w_down[:, :, e, :]).then_inc(w_loaded[e % 2], 16)

        @block.tensor
        def _(pe):
            def step(i, v, c, n):
                pe.wait_ge(w_loaded[v], 32 * (i + 1))

                def hidden(m):
                    pe.wait_ge(gelu_done, n * MB + m + 1)
                    for db in range(DB):
                        last = pe.matmul(HB[m % 4][:], up[v][:, db, m * P:(m + 1) * P],
                                         mem.xT[:, db, bass.ds(c * CHUNK, CHUNK)],
                                         start=(db == 0), stop=(db == DB - 1))
                    last.then_inc(up_done, 1)

                def output(m):
                    pe.wait_ge(gelu_done, n * MB + m + 5)
                    for t in range(4):
                        if m == 0:
                            pe.wait_ge(added, 4 * n + t + 1)
                        last = pe.matmul(YB[t][:, 0:D], hT[m % 4][:, t * P:(t + 1) * P], down[v][:, m, :],
                                         start=(m == 0), stop=(m == MB - 1))
                        if m == MB - 1:
                            last.then_inc(y_done, 1)

                hidden(0)
                for m in range(1, MB):
                    hidden(m)
                    output(m - 1)
                output(MB - 1)

            over_chunks(pe, step)

        @block.scalar
        def _(act):
            def step(i, v, c, n):
                for m in range(MB):
                    act.wait_ge(up_done, n * MB + m + 1)
                    act.activation(hT[m % 4][:], HB[m % 4][:], gelu).then_inc(gelu_done, 1)

            act.sem_inc(gelu_done, 4)
            over_chunks(act, step)

        @block.vector
        def _(dve):
            def step(i, v, c, n):
                for t in range(4):
                    dve.wait_ge(y_done, 4 * n + t + 1)
                    tile = mem.x[:, bass.ds(4 * c + t, 1), :].rearrange("p o d -> p (o d)")
                    gate = mem.gates[:, bass.ds(4 * c + t, 1), bass.ds(2 * i + v, 1)].rearrange("p o e -> p (o e)")
                    dve.scalar_tensor_tensor(tile, YB[t][:, 0:D], gate, tile, ALU.mult, ALU.add)\
                        .then_inc(added, 1)

            dve.sem_inc(added, 4)
            over_chunks(dve, step)


def norm_after_experts(nc, mem, tag, out):
    with ExitStack() as ctx:
        sem, sb, ps = open_stage(nc, ctx, tag)
        tl = Tail(sem, sb)
        M = ps("M", [P, 2, PT])
        out_stored = sem("out_stored")
        block = ctx.enter_context(nc.Block())

        @block.gpsimd
        def _(pool):
            def step(p, k, u, first, last):
                tail_rstd(pool, mem, tl, p)
                if out is None:
                    tail_store_x(pool, mem, tl, p)
            over_pairs(pool, step)

        @block.vector
        def _(dve):
            def step(p, k, u, first, last):
                r = mem.x[:, pair_tiles(p), :]
                tail_stats(dve, tl, p, r)
                if out is None:
                    after(dve, tl.xT_done, p)
                tail_apply(dve, tl, p, r, tl.x_stored)
            over_pairs(dve, step)

        if out is None:
            @block.tensor
            def _(pe):
                def step(p, k, u, first, last):
                    after(pe, tl.xT_stored, p)
                    tail_transpose(pe, mem, tl, p, M)
                over_pairs(pe, step)

            @block.scalar
            def _(act):
                def step(p, k, u, first, last):
                    tail_store_xT(act, mem, tl, p, M[:])
                over_pairs(act, step)
        else:
            @block.sync
            def _(sp):
                def step(p, k, u, first, last):
                    after(sp, tl.xn_done, 2 * p + 2)
                    sp.dma_start(out[:, pair_tiles(p), :], tl.xn[:]).then_inc(out_stored, 16)
                    after(sp, out_stored, 16 * (p + 1))
                    sp.sem_inc(tl.x_stored, 1)
                over_pairs(sp, step)



def window_attention(nc, mem, w_qkv, w_out, b_out):
    with ExitStack() as ctx:
        sem, sb, ps = open_stage(nc, ctx, "wa")
        w_qk = sb("wqk", [P, DB, 2 * D])
        w_q, w_k = w_qk[:, :, 0:D], w_qk[:, :, D:2 * D]
        w_o = sb("wo", [P, DB, D])
        b_o = sb("bo", [P, D])
        xb = [sb(f"xb{u}", [P, 2, D]) for u in range(2)]
        q_T = [sb(f"qT{u}", [P, DB, PT]) for u in range(2)]
        k_T = [sb(f"kT{u}", [P, DB, PT]) for u in range(2)]
        keys = sb("keys", [P, 2, D])
        sim = sb("sim", [P, 2, P])
        row_max, neg_max = sb("row_max", [P, 2]), sb("neg_max", [P, 2])
        prob = sb("prob", [P, 2, P])
        own_sum, pad, total, inv = (sb(n, [P, 2]) for n in ("own_sum", "pad", "total", "inv"))
        probn, probT = sb("probn", [P, 2, P]), sb("probT", [P, 2, P])
        oT = sb("oT", [P, DB, PT])
        tl = Tail(sem, sb)
        M = ps("M", [P, 2, PT])
        S = ps("S", [P, 2, 2 * P])
        KB = ps("KB", [P, 2, D])
        PB = ps("PB", [P, 2, 2 * P])
        OB = ps("OB", [P, DB, PT])
        Y = ps("Y", [P, 2, D])
        XB = ps("XB", [P, DB, PT])
        names = ("weights_loaded q_done k_done q_ready k_ready s_done keyT_done keys_ready sim_done max_done "
                 "neg_done exp_done pad_done total_done inv_done probn_done pT_done pT_ready o_done o_ready xb_ready")
        (weights_loaded, q_done, k_done, q_ready, k_ready, s_done, keyT_done, keys_ready, sim_done, max_done,
         neg_done, exp_done, pad_done, total_done, inv_done, probn_done, pT_done, pT_ready, o_done, o_ready,
         xb_ready) = (sem(n) for n in names.split())
        block = ctx.enter_context(nc.Block())

        @block.sync
        def _(sp):
            for dst, src in ((w_qk, w_qkv[:, :, 0:2 * D]), (w_o, w_out), (b_o, b_out.to_broadcast([P, D]))):
                sp.dma_start(dst[:], src).then_inc(weights_loaded, 16)

        @block.gpsimd
        def _(pool):
            def add_bias(p, u):
                pool.tensor_tensor(xb[u][:], mem.x[:, pair_tiles(p), :],
                                   b_o[:].unsqueeze(1).to_broadcast([P, 2, D]), ALU.add).then_inc(xb_ready, 1)

            def step(p, k, u, first, last):
                if not first:
                    tail_rstd(pool, mem, tl, p - 1)
                    tail_store_x(pool, mem, tl, p - 1)
                if not last:
                    after(pool, tl.r_done, p)
                    add_bias(p + 1, 1 - u)

            pool.wait_ge(weights_loaded, 16 * 3)
            add_bias(0, 0)
            over_pairs(pool, step)
            tail_rstd(pool, mem, tl, NP - 1)
            tail_store_x(pool, mem, tl, NP - 1)

        @block.scalar
        def _(act):
            def copy_q(p, u):
                after(act, q_done, p + 1)
                act.activation(q_T[u][:], M[:], ACT.Copy).then_inc(q_ready, 1)

            def copy_k(p, u):
                after(act, k_done, p + 1)
                act.activation(k_T[u][:], M[:], ACT.Copy).then_inc(k_ready, 1)

            def softmax(p):
                after(act, neg_done, p + 1)
                after(act, total_done, p)
                for j in range(2):
                    act.activation(prob[:, j, :], sim[:, j, :], ACT.Exp, bias=neg_max[:, j:j + 1],
                                   scale=WIN_SCALE, accum_out=own_sum[:, j:j + 1]).then_inc(exp_done, 1)
                act.activation(pad[:], neg_max[:], ACT.Exp).then_inc(pad_done, 1)

            def step(p, k, u, first, last):
                after(act, keyT_done, p + 1)
                act.activation(keys[:], KB[:], ACT.Copy).then_inc(keys_ready, 1)
                softmax(p)
                if not last:
                    copy_q(p + 1, 1 - u)
                if not first:
                    tail_store_xT(act, mem, tl, p - 1, XB[:])
                after(act, pT_done, p + 1)
                act.activation(probT[:], PB[:, :, 0:P], ACT.Copy).then_inc(pT_ready, 1)
                if not last:
                    copy_k(p + 1, 1 - u)
                after(act, o_done, p + 1)
                act.activation(oT[:], OB[:], ACT.Copy).then_inc(o_ready, 1)

            copy_q(0, 0)
            copy_k(0, 0)
            over_pairs(act, step)
            tail_store_xT(act, mem, tl, NP - 1, XB[:])

        @block.vector
        def _(dve):
            def shift(p):
                after(dve, s_done, p + 1)
                after(dve, exp_done, 2 * p)
                dve.tensor_tensor(sim[:], S[:, :, 0:P], mem.causal.unsqueeze(1).to_broadcast([P, 2, P]), ALU.add)\
                    .then_inc(sim_done, 1)
                after(dve, sim_done, p + 1)
                dve.tensor_reduce(row_max[:], sim[:], AX.X, ALU.max).then_inc(max_done, 1)
                after(dve, max_done, p + 1)
                after(dve, pad_done, p)
                dve.tensor_scalar(neg_max[:], row_max[:], 0.0, -WIN_SCALE, ALU.max, ALU.mult)\
                    .then_inc(neg_done, 1)

            def normalize(p):
                after(dve, exp_done, 2 * p + 2)
                after(dve, pad_done, p + 1)
                dve.scalar_tensor_tensor(total[:], pad[:], float(P), own_sum[:], ALU.mult, ALU.add)\
                    .then_inc(total_done, 1)
                after(dve, total_done, p + 1)
                dve.reciprocal(inv[:], total[:]).then_inc(inv_done, 1)
                after(dve, inv_done, p + 1)
                for j in range(2):
                    dve.tensor_scalar(probn[:, j, :], prob[:, j, :], inv[:, j:j + 1], None, ALU.mult)\
                        .then_inc(probn_done, 1)

            def residual(p, u):
                after(dve, xb_ready, p + 1)
                tail_residual(dve, tl, p, Y[:], xb[u][:])
                tail_stats(dve, tl, p, tl.r)

            def step(p, k, u, first, last):
                shift(p)
                if not first:
                    residual(p - 1, 1 - u)
                normalize(p)
                if not first:
                    tail_apply(dve, tl, p - 1, tl.r, tl.x_stored)

            over_pairs(dve, step)
            residual(NP - 1, 1)
            tail_apply(dve, tl, NP - 1, tl.r, tl.x_stored)

        @block.tensor
        def _(pe):
            def proj_q(p):
                project_T(pe, M, w_q, lambda db: mem.xT[:, db, pair_tokens(p)]).then_inc(q_done, 1)

            def proj_k(p):
                after(pe, q_ready, p + 1)
                project_T(pe, M, w_k, lambda db: mem.xT[:, db, pair_tokens(p)]).then_inc(k_done, 1)

            def step(p, k, u, first, last):
                after(pe, k_ready, p + 1)
                after(pe, sim_done, p)
                for j in range(2):
                    for db in range(DB):
                        last_s = pe.matmul(S[:, j, 0:P], q_T[u][:, db, j * P:(j + 1) * P],
                                           k_T[u][:, db, j * P:(j + 1) * P],
                                           start=(db == 0), stop=(db == DB - 1))
                last_s.then_inc(s_done, 1)
                after(pe, keys_ready, p)
                for j in range(2):
                    for db in range(DB):
                        last_k = pe.transpose(KB[:, j, db * P:(db + 1) * P], k_T[u][:, db, j * P:(j + 1) * P],
                                              mem.ident)
                last_k.then_inc(keyT_done, 1)
                if not first:
                    after(pe, o_ready, p)
                    project(pe, Y, oT, w_o).then_inc(tl.y_done, 1)
                if not last:
                    proj_q(p + 1)
                if not first:
                    tail_transpose(pe, mem, tl, p - 1, XB)
                after(pe, probn_done, 2 * p + 2)
                for j in range(2):
                    last_p = pe.transpose(PB[:, j, 0:P], probn[:, j, :], mem.ident)
                last_p.then_inc(pT_done, 1)
                if not last:
                    proj_k(p + 1)
                after(pe, keys_ready, p + 1)
                after(pe, pT_ready, p + 1)
                for db in range(DB):
                    for j in range(2):
                        last_o = pe.matmul(OB[:, db, j * P:(j + 1) * P], keys[:, j, db * P:(db + 1) * P],
                                           probT[:, j, :], start=True, stop=True)
                last_o.then_inc(o_done, 1)

            pe.wait_ge(weights_loaded, 16 * 3)
            proj_q(0)
            proj_k(0)
            over_pairs(pe, step)
            pe.wait_ge(o_ready, NP)
            project(pe, Y, oT, w_o).then_inc(tl.y_done, 1)
            tail_transpose(pe, mem, tl, NP - 1, XB)



def by_block(ap):
    return ap.rearrange("(b p) n -> p b n", p=P)


def row(ap):
    return ap.rearrange("(a n) -> a n", a=1)


def constants():
    r, c = np.arange(P)[:, None], np.arange(P)[None, :]
    return {
        "ident": r == c,
        "ones": np.ones((P, P)),
        "earlier": r < c,
        "causal": np.where(c <= r, 0.0, MASKED),
        "even_rows": r // DH % 2 == 0,
        "odd_rows": r // DH % 2 == 1,
        "neg_half": np.full((P, 2), -0.5),
        "eps": np.full((P, 2), EPS),
        "zeros32": np.zeros((P, NB)),
        "rising8": np.broadcast_to(E - np.arange(E), (P, E)),
        "lower8": np.broadcast_to((np.arange(E)[None, :] < np.arange(E)[:, None]).reshape(1, E * E), (P, E * E)),
    }


def constant_columns():
    at, found = 0, {}
    for name, value in constants().items():
        found[name] = (at, value.shape[1])
        at += value.shape[1]
    return found, at


def decoder(nc, a, out):
    with ExitStack() as ctx:
        columns, n_columns = constant_columns()
        mem = Mem()
        mem.x = ctx.enter_context(nc.sbuf_tensor("x", [P, NB, D], F32))
        mem.xT = ctx.enter_context(nc.sbuf_tensor("xT", [P, DB, T], F32))
        mem.gates = ctx.enter_context(nc.sbuf_tensor("gates", [P, NB, E], F32))
        const = ctx.enter_context(nc.sbuf_tensor("const", [P, n_columns], F32))

        def constant(name):
            at, size = columns[name]
            return const[:, at:at + size]

        mem.ident, mem.ones, mem.earlier, mem.causal = (constant(n) for n in ("ident", "ones", "earlier", "causal"))
        mem.even_rows, mem.odd_rows = constant("even_rows"), constant("odd_rows")
        mem.neg_half, mem.zeros32, mem.rising8 = constant("neg_half"), constant("zeros32"), constant("rising8")
        mem.eps = constant("eps")
        mem.lower8 = constant("lower8").rearrange("p (e o) -> p e o", e=E)
        mem.load_constants = lambda sp, loaded: sp.dma_start(const[:], a["const"]).then_inc(loaded, 16)

        ctxT = by_block(a["ctxT"])
        gated_attention(nc, mem, a["x"].rearrange("b p d -> p b d"), by_block(a["xT"]),
                        *(by_block(a[f"L0_attn_{n}"]) for n in ("Wq", "Wk", "Wv", "Wo", "Wg")),
                        a["L0_attn_bg"].rearrange("(h a) -> h a", a=1),
                        a["diagonals"].rearrange("p (h t) -> p h t", h=HH),
                        a["head_rows"].rearrange("p (h t) -> p h t", h=H))

        def context_layer(tag):
            weights = (by_block(a[f"{tag}_xattn_{n}"]) for n in ("Wq", "Wk", "Wv", "Wo"))
            cross_attention(nc, mem, f"{tag}x", ctxT, *weights, a[f"{tag}_xattn_bq"],
                            a[f"{tag}_xattn_bk"], row(a[f"{tag}_xattn_bv"]), row(a[f"{tag}_xattn_bo"]))

        def expert_layer(tag, w_up, w_down, width, gelu):
            experts(nc, mem, tag, w_up.rearrange("e (b p) h -> p b e h", p=P),
                    w_down.rearrange("e (b p) d -> p b e d", p=P), width, gelu)

        context_layer("L0")
        router(nc, mem, "r0", by_block(a["L0_ffn_router_w"]), top_experts)
        expert_layer("L0", a["L0_ffn_up_w"], a["L0_ffn_down_w"], 4 * D, ACT.Gelu_apprx_tanh)
        norm_after_experts(nc, mem, "n0", None)
        window_attention(nc, mem, by_block(a["L1_attn_w_qkv"]), by_block(a["L1_attn_w_out"]),
                         row(a["L1_attn_b_out"]))
        context_layer("L1")
        router(nc, mem, "r1", by_block(a["L1_ffn_Wg"]), selected_expert)
        expert_layer("L1", a["L1_ffn_W1"], a["L1_ffn_W2"], 2 * D, ACT.Gelu)
        norm_after_experts(nc, mem, "n1", out.rearrange("b p d -> p b d"))



def kernel(**inputs):
    import concourse.bacc as bacc
    from concourse.bass_utils import run_bass_kernel_spmd

    arrays = {k: np.asarray(v) for k, v in inputs.items()}
    arrays["xT"] = arrays["x"].reshape(T, D).T
    arrays["ctxT"] = arrays.pop("ctx_1024").reshape(T, D).T
    for name in ("L0_attn_Wq", "L0_attn_Wk", "L0_attn_Wv", "L0_attn_Wo", "L0_attn_Wg",
                 "L0_xattn_Wq", "L0_xattn_Wk", "L0_xattn_Wv", "L0_xattn_Wo"):
        arrays[name] = arrays[name].T
    for name in ("L0_xattn_bq", "L0_xattn_bk", "L1_xattn_bq", "L1_xattn_bk"):
        arrays[name] = arrays[name].reshape(DB, P).T
    eye = np.eye(P, dtype=np.float32)
    arrays["const"] = np.concatenate(list(constants().values()), axis=1).astype(np.float32)
    arrays["diagonals"] = np.tile(eye, (1, HH))
    arrays["head_rows"] = np.repeat(np.eye(H, dtype=np.float32), P, axis=1)
    arrays = {k: np.ascontiguousarray(v) for k, v in arrays.items()}

    nc = bacc.Bacc("TRN2", target_bir_lowering=False, num_devices=1)
    aps = {k: nc.dram_tensor(f"in_{k}", v.shape, mybir.dt.from_np(v.dtype), kind="ExternalInput").ap()
           for k, v in arrays.items()}
    out = nc.dram_tensor("out", (NB, P, D), F32, kind="ExternalOutput").ap()
    decoder(nc, aps, out)
    r = run_bass_kernel_spmd(nc, [{f"in_{k}": v for k, v in arrays.items()}], core_ids=[0])
    return r.results[0]["out"]
```

```python
import numpy as np
import concourse.bass as bass
from concourse import mybir
from contextlib import ExitStack

F32 = mybir.dt.float32
F16 = mybir.dt.float16
U32 = mybir.dt.uint32
ALU = mybir.AluOpType
ACT = mybir.ActivationFunctionType
AX = mybir.AxisListType

P = 128
D = 256
DB = D // P
NB = 32
T = NB * P
NP = NB // 2
PT = 2 * P
H = 16
DH = D // H
HH = H // 2
E = 8
TOPK = 4
CAP = T // E
EPS = 1e-5
RT = 256
BANK = 512
HEAD_SCALE = float(DH) ** -0.5
WIN_SCALE = float(D) ** -0.5
MASKED = -3.0e38


def after(eng, sem, count):
    if isinstance(count, int) and count <= 0:
        return
    eng.wait_ge(sem, count)


def over_pairs(eng, step):
    step(0, 0, 0, True, False)
    with eng.Fori(0, (NP - 2) // 2) as i:
        step(2 * i + 1, i, 1, False, False)
        step(2 * i + 2, i + 1, 0, False, False)
    step(NP - 1, NP // 2 - 1, 1, False, True)


def pair_tokens(p):
    return bass.ds(p * PT, PT)


def pair_tiles(p):
    return bass.ds(p * 2, 2)


class Mem:
    pass


def open_stage(nc, ctx, tag):
    sems = []

    def sem(name):
        sems.append(nc.alloc_semaphore(f"{tag}_{name}"))
        return sems[-1]

    def clear():
        nc.clear_and_free_semaphores(sems)
        nc.all_engine_barrier()

    ctx.callback(clear)

    def sb(name, shape, dt=F32):
        return ctx.enter_context(nc.sbuf_tensor(f"{tag}_{name}", shape, dt))

    def ps(name, shape):
        size = int(np.prod(shape[1:]))
        whole = ctx.enter_context(nc.psum_tensor(f"{tag}_{name}", [P, -(-size // BANK) * BANK], F32))
        flat = whole[:, 0:size]
        if len(shape) == 2:
            return flat
        inner = {f"n{i}": n for i, n in enumerate(shape[1:])}
        return flat.rearrange(f"p ({' '.join(inner)}) -> p {' '.join(inner)}", **inner)

    return sem, sb, ps



class Tail:

    def __init__(self, sem, sb):
        self.r = sb("r", [P, 2, D])
        self.stats = sb("stats", [P, 2, 6])
        self.moments = sb("moments", [P, 2, 2])
        self.vare = sb("vare", [P, 2])
        self.rstd = sb("rstd", [P, 2])
        self.xn = sb("xn", [P, 2, D])
        self.y_done = sem("y_done")
        self.r_done = sem("r_done")
        self.moments_done = sem("moments_done")
        self.vare_done = sem("vare_done")
        self.rstd_done = sem("rstd_done")
        self.xn_done = sem("xn_done")
        self.x_stored = sem("x_stored")
        self.xT_done = sem("xT_done")
        self.xT_high = sem("xT_high")
        self.xT_low = sem("xT_low")


def tail_residual(dve, tl, p, y, xb):
    after(dve, tl.y_done, p + 1)
    dve.tensor_tensor(tl.r[:], y, xb, ALU.add).then_inc(tl.r_done, 1)
    after(dve, tl.r_done, p + 1)


def tail_stats(dve, tl, p, r):
    for j in range(2):
        dve.bn_stats(tl.stats[:, j, :], r[:, j, :])
    dve.drain()
    for j in range(2):
        dve.bn_aggr(tl.moments[:, j, :], tl.stats[:, j, :]).then_inc(tl.moments_done, 1)


def tail_rstd(pool, mem, tl, p):
    after(pool, tl.moments_done, 2 * p + 2)
    pool.tensor_tensor(tl.vare[:], tl.moments[:, :, 1], mem.eps, ALU.add)\
        .then_inc(tl.vare_done, 1)
    after(pool, tl.vare_done, p + 1)
    pool.tensor_tensor(tl.rstd[:], tl.vare[:], mem.neg_half, ALU.pow).then_inc(tl.rstd_done, 1)


def tail_apply(dve, tl, p, r, xn_used):
    after(dve, tl.rstd_done, p + 1)
    after(dve, tl.moments_done, 2 * p + 2)
    after(dve, xn_used, p)
    for j in range(2):
        dve.tensor_scalar(tl.xn[:, j, :], r[:, j, :], tl.moments[:, j, 0:1], tl.rstd[:, j:j + 1],
                          ALU.subtract, ALU.mult).then_inc(tl.xn_done, 1)


def tail_store_x(pool, mem, tl, p):
    after(pool, tl.xn_done, 2 * p + 2)
    pool.tensor_copy(mem.x[:, pair_tiles(p), :], tl.xn[:]).then_inc(tl.x_stored, 1)


def tail_transpose(pe, mem, tl, p, bank):
    after(pe, tl.xn_done, 2 * p + 2)
    for db in range(DB):
        for j in range(2):
            last = pe.transpose(bank[:, db, j * P:(j + 1) * P], tl.xn[:, j, db * P:(db + 1) * P],
                                mem.ident)
    last.then_inc(tl.xT_done, 1)


def tail_xT_high(act, mem, tl, p, bank):
    after(act, tl.xT_done, p + 1)
    act.activation(mem.xT.hi[:, :, pair_tokens(p)], bank, ACT.Copy).then_inc(tl.xT_high, 1)


def tail_xT_low(dve, mem, tl, p, bank):
    after(dve, tl.xT_high, p + 1)
    dve.tensor_tensor(mem.xT.lo[:, :, pair_tokens(p)], bank, mem.xT.hi[:, :, pair_tokens(p)], ALU.subtract)\
        .then_inc(tl.xT_low, 1)



class Parts:
    def __init__(self, hi, lo):
        self.hi, self.lo = hi, lo


def parts(sb, name, shape):
    return Parts(sb(f"{name}_hi", shape, F16), sb(f"{name}_lo", shape, F16))


def product(pe, out, stationary, moving, start=True, stop=True):
    s_hi, s_lo = stationary
    m_hi, m_lo = moving
    pe.matmul(out, s_hi, m_hi, start=start, stop=False)
    pe.matmul(out, s_hi, m_lo, start=False, stop=False)
    return pe.matmul(out, s_lo, m_hi, start=False, stop=stop)


def project_T(pe, bank, w, moving):
    for m in range(DB):
        f = slice(m * P, (m + 1) * P)
        for db in range(DB):
            last = product(pe, bank[:, m, :], (w.hi[:, db, f], w.lo[:, db, f]), moving(db),
                           start=(db == 0), stop=(db == DB - 1))
    return last


def project(pe, bank, featT, w):
    for j in range(2):
        tok = slice(j * P, (j + 1) * P)
        for db in range(DB):
            last = product(pe, bank[:, j, :], (featT.hi[:, db, tok], featT.lo[:, db, tok]),
                           (w.hi[:, db, :], w.lo[:, db, :]), start=(db == 0), stop=(db == DB - 1))
    return last


def blocks_of(x):
    return lambda db: (x.hi[:, db, :], x.lo[:, db, :])


def blocks_at(x, tokens):
    return lambda db: (x.hi[:, db, tokens], x.lo[:, db, tokens])


def over_pair(column):
    return column.unsqueeze(2).to_broadcast([P, DB, PT])


class Weights:

    def __init__(self, sem, sb, shapes):
        self.raw = [sb(f"w{n}_raw", shape) for n, shape in enumerate(shapes)]
        self.cut = [parts(sb, f"w{n}", shape) for n, shape in enumerate(shapes)]
        self.loaded = [sem(f"w{n}_loaded") for n in range(len(shapes))]
        self.hi_done, self.lo_done = sem("w_hi_done"), sem("w_lo_done")

    def load(self, sp, n, source):
        sp.dma_start(self.raw[n][:], source).then_inc(self.loaded[n], 16)

    def high(self, act, n):
        act.wait_ge(self.loaded[n], 16)
        act.activation(self.cut[n].hi[:], self.raw[n][:], ACT.Copy).then_inc(self.hi_done, 1)

    def low(self, pool, n):
        pool.wait_ge(self.hi_done, n + 1)
        pool.tensor_tensor(self.cut[n].lo[:], self.raw[n][:], self.cut[n].hi[:], ALU.subtract)\
            .then_inc(self.lo_done, 1)


def mask_heads(eng, mem, masked, part, done):
    for h in range(HH):
        last = eng.tensor_scalar(masked[:, h, :, :], part[:], mem.head_mask[:, h:h + 1], 1.0, ALU.mult, ALU.mult)
    last.then_inc(done, 1)


def four_heads(masked, a, blk, tok):
    return masked[:, 4 * a:4 * a + 4, blk, tok]



GROWS = 96


def gated_attention(nc, mem, rows_in, x, xT0, wq, wk, wv, wo, wg, bg, diagonals_in, head_rows_in):
    with ExitStack() as ctx:
        sem, sb, ps = open_stage(nc, ctx, "ga")
        WQ, WK, WV, WG, WO = range(5)
        w = Weights(sem, sb, [[P, DB, D]] * 3 + [[P, DB, GROWS], [P, DB, D]])
        b_g, half_bg = sb("bg", [GROWS, 1]), sb("half_bg", [GROWS, 1])
        head_rows = sb("head_rows", [GROWS, H, P], F16)
        diagonals = sb("diagonals", [P, HH, P])
        xt = [sb(f"xt{u}", [P, DB, PT]) for u in range(2)]
        xc = parts(sb, "xc", [P, DB, PT])
        xb = [sb(f"xb{u}", [P, 2, D]) for u in range(2)]
        qexp, kexp = sb("qexp", [P, DB, PT]), sb("kexp", [P, DB, PT])
        qrelu, krelu = sb("qrelu", [P, DB, PT]), sb("krelu", [P, DB, PT])
        qfeat, kfeat = sb("qfeat", [P, DB, PT]), sb("kfeat", [P, DB, PT])
        q_cut = parts(sb, "q", [P, DB, PT])
        q_heads = [parts(sb, f"q_heads{u}", [P, HH, DB, PT]) for u in range(2)]
        k_T = [parts(sb, f"kT{u}", [P, DB, PT]) for u in range(2)]
        v_cut = [parts(sb, f"v{u}", [P, 2, D]) for u in range(2)]
        gtanh, gate = sb("gtanh", [GROWS, 2, P]), sb("gate", [GROWS, 2, P])
        gate_hi = sb("gate_hi", [GROWS, 2, P], F16)
        gate_parts = [sb(f"gate_parts{u}", [GROWS, 2, P], F16) for u in range(2)]
        decay = [sb(f"decay{n}", [P, HH, P]) for n in range(2)]
        att = [sb(f"att{n}", [P, HH, P]) for n in range(2)]
        att_cut = [parts(sb, f"attc{n}", [P, HH, P]) for n in range(2)]
        ctxn = sb("ctxn", [P, 2, D])
        ctxT = parts(sb, "ctxT", [P, DB, PT])
        zero = sb("zero", [P, D])
        tl = Tail(sem, sb)

        GB = ps("GB", [P, HH, P])
        S = [ps(f"S{n}", [P, HH, P]) for n in range(2)]
        O = ps("O", [P, 512])
        M = ps("M", [P, 2, PT])

        consts_loaded = sem("consts_loaded")
        xt_loaded = [sem(f"xt_loaded{u}") for u in range(2)]
        xb_loaded = [sem(f"xb_loaded{u}") for u in range(2)]
        half_bg_done, x_high, x_low = sem("half_bg_done"), sem("x_high"), sem("x_low")
        q_done, k_done, v_done, g_done = (sem(n) for n in ("q_done", "k_done", "v_done", "g_done"))
        qexp_done, kexp_done, gtanh_done = sem("qexp_done"), sem("kexp_done"), sem("gtanh_done")
        qrelu_done, qfeat_done, q_high, q_low = (sem(n) for n in ("qrelu_done", "qfeat_done", "q_high", "q_low"))
        heads_high, heads_low = sem("heads_high"), sem("heads_low")
        krelu_done, kfeat_done, k_high, k_low = (sem(n) for n in ("krelu_done", "kfeat_done", "k_high", "k_low"))
        v_high, v_low = sem("v_high"), sem("v_low")
        gate_done, gate0_done, gate_cast, g_ready = (sem(n) for n in ("gate_done", "gate0_done", "gate_cast", "g_ready"))
        gb_done, decay_done = sem("gb_done"), sem("decay_done")
        s_done, att_done, att_high, att_low = (sem(n) for n in ("s_done", "att_done", "att_high", "att_low"))
        o_done, ctx_ready = sem("o_done"), sem("ctx_ready")
        ctxT_done, ctxT_high, ctxT_low = sem("ctxT_done"), sem("ctxT_high"), sem("ctxT_low")
        zeroed, cleared = sem("zeroed"), sem("cleared")
        consts_all = 16 * 5

        block = ctx.enter_context(nc.Block())

        @block.sync
        def _(sp):
            def step(p, k, u, first, last):
                after(sp, x_low, p)
                sp.dma_start(xt[u][:], xT0[:, :, pair_tokens(p)]).then_inc(xt_loaded[u], 16)
                if first:
                    w.load(sp, WQ, wq)
                    w.load(sp, WK, wk)
                    sp.dma_start(b_g[:], bg).then_inc(consts_loaded, 16)
                    mem.load_constants(sp, consts_loaded)
                    w.load(sp, WV, wv)
                    w.load(sp, WG, wg)
                    sp.dma_start(head_rows[:], head_rows_in).then_inc(consts_loaded, 16)
                    sp.dma_start(diagonals[:], diagonals_in).then_inc(consts_loaded, 16)
                    w.load(sp, WO, wo)
                after(sp, tl.r_done, p)
                sp.dma_start(xb[u][:], x[:, pair_tiles(p), :]).then_inc(xb_loaded[u], 16)

            over_pairs(sp, step)
            sp.wait_ge(cleared, 16)

        @block.gpsimd
        def _(pool):
            def x_lo(p, k, u):
                after(pool, x_high, p + 1)
                pool.tensor_tensor(xc.lo[:], xt[u][:], xc.hi[:], ALU.subtract).then_inc(x_low, 1)

            def q_lo(p, u):
                after(pool, q_high, p + 1)
                pool.tensor_tensor(q_cut.lo[:], qfeat[:], q_cut.hi[:], ALU.subtract).then_inc(q_low, 1)
                pool.drain()
                mask_heads(pool, mem, q_heads[u].lo, q_cut.lo, heads_low)

            def k_lo(p, u):
                after(pool, k_high, p + 1)
                pool.tensor_tensor(k_T[u].lo[:], kfeat[:], k_T[u].hi[:], ALU.subtract).then_inc(k_low, 1)

            def att_lo(p, n):
                after(pool, att_high, 4 * p + n + 1)
                pool.tensor_tensor(att_cut[n % 2].lo[:], att[n % 2][:], att_cut[n % 2].hi[:], ALU.subtract)\
                    .then_inc(att_low, 1)

            def step(p, k, u, first, last):
                att_lo(p, 0)
                att_lo(p, 1)
                if not first:
                    tail_rstd(pool, mem, tl, p - 1)
                if not last:
                    x_lo(p + 1, k + u, 1 - u)
                att_lo(p, 2)
                if not first:
                    tail_store_x(pool, mem, tl, p - 1)
                att_lo(p, 3)
                if not last:
                    q_lo(p + 1, 1 - u)
                    k_lo(p + 1, 1 - u)

            pool.memset(zero[:], 0.0).then_inc(zeroed, 1)
            w.low(pool, WQ)
            x_lo(0, 0, 0)
            w.low(pool, WK)
            w.low(pool, WV)
            w.low(pool, WG)
            pool.wait_ge(consts_loaded, consts_all)
            q_lo(0, 0)
            k_lo(0, 0)
            w.low(pool, WO)
            over_pairs(pool, step)
            tail_rstd(pool, mem, tl, NP - 1)
            tail_store_x(pool, mem, tl, NP - 1)

        @block.scalar
        def _(act):
            def x_hi(p, k, u):
                act.wait_ge(xt_loaded[u], 16 * (k + 1))
                after(act, g_done, p)
                act.activation(xc.hi[:], xt[u][:], ACT.Copy).then_inc(x_high, 1)

            def exp_q(p):
                after(act, q_done, p + 1)
                act.activation(qexp[:], M[:], ACT.Exp, scale=HEAD_SCALE).then_inc(qexp_done, 1)

            def exp_k(p):
                after(act, k_done, p + 1)
                act.activation(kexp[:], M[:], ACT.Exp).then_inc(kexp_done, 1)

            def k_hi(p, u):
                after(act, kfeat_done, p + 1)
                act.activation(k_T[u].hi[:], kfeat[:], ACT.Copy).then_inc(k_high, 1)

            def v_hi(p, u):
                after(act, v_done, p + 1)
                act.activation(v_cut[u].hi[:], M[:], ACT.Copy).then_inc(v_high, 1)

            def tanh_g(p):
                after(act, g_done, p + 1)
                act.activation(gtanh[:].rearrange("g j t -> g (j t)"), M[0:GROWS, 0, :], ACT.Tanh,
                               bias=half_bg[:], scale=0.5).then_inc(gtanh_done, 1)

            def att_hi(p, n):
                after(act, att_done, 4 * p + n + 1)
                act.activation(att_cut[n % 2].hi[:], att[n % 2][:], ACT.Copy).then_inc(att_high, 1)

            def copy_o(p, j):
                after(act, o_done, 2 * p + j + 1)
                act.activation(ctxn[:, j, :], O[:, 0:D], ACT.Copy).then_inc(ctx_ready, 1)

            def ctxT_hi(p):
                after(act, ctxT_done, p + 1)
                act.activation(ctxT.hi[:], M[:], ACT.Copy).then_inc(ctxT_high, 1)

            def step(p, k, u, first, last):
                if not first:
                    ctxT_hi(p - 1)
                att_hi(p, 0)
                if not last:
                    x_hi(p + 1, k + u, 1 - u)
                att_hi(p, 1)
                if not first:
                    tail_xT_high(act, mem, tl, p - 1, M[:])
                att_hi(p, 2)
                if not last:
                    exp_q(p + 1)
                copy_o(p, 0)
                att_hi(p, 3)
                if not last:
                    exp_k(p + 1)
                    k_hi(p + 1, 1 - u)
                    v_hi(p + 1, 1 - u)
                copy_o(p, 1)
                if not last:
                    tanh_g(p + 1)

            w.high(act, WQ)
            x_hi(0, 0, 0)
            w.high(act, WK)
            exp_q(0)
            act.wait_ge(zeroed, 1)
            act.dma_start(rows_in.rearrange("(n p) d -> p n d", p=P),
                          zero[:].unsqueeze(1).to_broadcast([P, rows_in.shape[0] // P, D])).then_inc(cleared, 16)
            w.high(act, WV)
            exp_k(0)
            k_hi(0, 0)
            w.high(act, WG)
            v_hi(0, 0)
            act.wait_ge(half_bg_done, 1)
            tanh_g(0)
            w.high(act, WO)
            over_pairs(act, step)
            ctxT_hi(NP - 1)
            tail_xT_high(act, mem, tl, NP - 1, M[:])

        @block.vector
        def _(dve):
            def feature_q(p, u):
                after(dve, qexp_done, p + 1)
                dve.tensor_scalar(qrelu[:], M[:], HEAD_SCALE, 0.0, ALU.mult, ALU.max)\
                    .then_inc(qrelu_done, 1)
                after(dve, qrelu_done, p + 1)
                after(dve, heads_low, p)
                dve.scalar_tensor_tensor(qfeat[:], qexp[:], 1.0, qrelu[:], ALU.min, ALU.add)\
                    .then_inc(qfeat_done, 1)
                after(dve, qfeat_done, p + 1)
                dve.tensor_copy(q_cut.hi[:], qfeat[:]).then_inc(q_high, 1)
                after(dve, q_high, p + 1)
                mask_heads(dve, mem, q_heads[u].hi, q_cut.hi, heads_high)

            def feature_k(p, u):
                after(dve, kexp_done, p + 1)
                dve.tensor_scalar(krelu[:], M[:], 0.0, None, ALU.max).then_inc(krelu_done, 1)
                after(dve, krelu_done, p + 1)
                after(dve, k_low, p)
                dve.scalar_tensor_tensor(kfeat[:], kexp[:], 1.0, krelu[:], ALU.min, ALU.add)\
                    .then_inc(kfeat_done, 1)

            def v_lo(p, u):
                after(dve, v_high, p + 1)
                dve.tensor_tensor(v_cut[u].lo[:], M[:], v_cut[u].hi[:], ALU.subtract).then_inc(v_low, 1)

            def gates(p, u):
                after(dve, gtanh_done, p + 1)
                dve.tensor_scalar(gate[:], gtanh[:], 0.5, 0.5, ALU.mult, ALU.add).then_inc(gate_done, 1)
                after(dve, gate_done, p + 1)
                dve.memset(gate[:, :, 0:1], 0.0).then_inc(gate0_done, 1)
                after(dve, gate0_done, p + 1)
                dve.tensor_copy(gate_parts[u][0:32, :, :], gate[0:32, :, :])
                dve.tensor_copy(gate_hi[32:64, :, :], gate[32:64, :, :])
                dve.tensor_copy(gate_hi[64:96, :, :], gate[64:96, :, :]).then_inc(gate_cast, 1)
                after(dve, gate_cast, p + 1)
                for rows in (slice(32, 64), slice(64, 96)):
                    last = dve.tensor_tensor(gate_parts[u][rows, :, :], gate[rows, :, :], gate_hi[rows, :, :],
                                             ALU.subtract)
                last.then_inc(g_ready, 1)
                after(dve, g_ready, p + 1)

            def half(p, n):
                h = 4 * p + n
                after(dve, att_done, h - 1)
                after(dve, gb_done, h + 1)
                dve.tensor_tensor_scan(decay[n % 2][:].rearrange("p h t -> p (h t)"),
                                       GB[:].rearrange("p h t -> p (h t)"),
                                       diagonals[:].rearrange("p h t -> p (h t)"),
                                       0.0, ALU.mult, ALU.add).then_inc(decay_done, 1)
                after(dve, decay_done, h + 1)
                after(dve, s_done, h + 1)
                dve.tensor_tensor(att[n % 2][:], S[n % 2][:], decay[n % 2][:], ALU.mult).then_inc(att_done, 1)

            def ctxT_lo(p):
                after(dve, ctxT_high, p + 1)
                dve.tensor_tensor(ctxT.lo[:], M[:], ctxT.hi[:], ALU.subtract).then_inc(ctxT_low, 1)

            def step(p, k, u, first, last):
                half(p, 0)
                if not first:
                    ctxT_lo(p - 1)
                half(p, 1)
                if not first:
                    dve.wait_ge(xb_loaded[1 - u], 16 * (k + u))
                    tail_residual(dve, tl, p - 1, M[:], xb[1 - u][:])
                    tail_stats(dve, tl, p - 1, tl.r)
                half(p, 2)
                if not first:
                    tail_apply(dve, tl, p - 1, tl.r, tl.x_stored)
                    tail_xT_low(dve, mem, tl, p - 1, M[:])
                if not last:
                    feature_q(p + 1, 1 - u)
                half(p, 3)
                if not last:
                    feature_k(p + 1, 1 - u)
                    v_lo(p + 1, 1 - u)
                    gates(p + 1, 1 - u)

            dve.wait_ge(consts_loaded, consts_all)
            dve.tensor_scalar(half_bg[:], b_g[:], 0.5, None, ALU.mult).then_inc(half_bg_done, 1)
            feature_q(0, 0)
            feature_k(0, 0)
            v_lo(0, 0)
            gates(0, 0)
            over_pairs(dve, step)
            ctxT_lo(NP - 1)
            dve.wait_ge(xb_loaded[1], 16 * (NP // 2))
            tail_residual(dve, tl, NP - 1, M[:], xb[1][:])
            tail_stats(dve, tl, NP - 1, tl.r)
            tail_apply(dve, tl, NP - 1, tl.r, tl.x_stored)
            tail_xT_low(dve, mem, tl, NP - 1, M[:])

        @block.tensor
        def _(pe):
            def proj_q(p):
                after(pe, x_high, p + 1)
                after(pe, x_low, p + 1)
                project_T(pe, M, w.cut[WQ], blocks_of(xc)).then_inc(q_done, 1)

            def proj_k(p):
                after(pe, qfeat_done, p + 1)
                project_T(pe, M, w.cut[WK], blocks_of(xc)).then_inc(k_done, 1)

            def proj_v(p):
                after(pe, kfeat_done, p + 1)
                project(pe, M, xc, w.cut[WV]).then_inc(v_done, 1)

            def proj_g(p):
                after(pe, v_low, p + 1)
                for db in range(DB):
                    wg_ = w.cut[WG]
                    last = product(pe, M[0:GROWS, 0, :], (wg_.hi[:, db, :], wg_.lo[:, db, :]),
                                   (xc.hi[:, db, :], xc.lo[:, db, :]), start=(db == 0), stop=(db == DB - 1))
                last.then_inc(g_done, 1)

            def spread_gates(p, n, u):
                h = 4 * p + n
                after(pe, g_ready, p + 1)
                after(pe, decay_done, h)
                for s in range(HH):
                    last = pe.matmul(GB[:, s, :], head_rows[:, HH * (n % 2) + s, :],
                                     gate_parts[u][:, n // 2, :], start=True, stop=True)
                last.then_inc(gb_done, 1)

            def scores(p, n, u):
                h = 4 * p + n
                blk, tok = n % 2, slice((n // 2) * P, (n // 2 + 1) * P)
                after(pe, heads_high, p + 1)
                after(pe, heads_low, p + 1)
                after(pe, k_low, p + 1)
                after(pe, att_done, h - 1)
                for a in range(2):
                    last = product(pe, S[n % 2][:, 4 * a:4 * a + 4, :],
                                   (k_T[u].hi[:, blk, tok], k_T[u].lo[:, blk, tok]),
                                   (four_heads(q_heads[u].hi, a, blk, tok), four_heads(q_heads[u].lo, a, blk, tok)))
                last.then_inc(s_done, 1)

            def values(p, n, u):
                h = 4 * p + n
                blk, j = n % 2, n // 2
                after(pe, att_high, h + 1)
                after(pe, att_low, h + 1)
                after(pe, v_low, p + 1)
                after(pe, ctx_ready, 2 * p + j)
                cut, v = att_cut[n % 2], v_cut[u]
                for s in range(HH):
                    f = slice((HH * blk + s) * DH, (HH * blk + s + 1) * DH)
                    last = product(pe, O[:, f], (cut.hi[:, s, :], cut.lo[:, s, :]), (v.hi[:, j, f], v.lo[:, j, f]))
                if blk:
                    last.then_inc(o_done, 1)

            def transpose_ctx(p):
                after(pe, ctx_ready, 2 * p + 2)
                for db in range(DB):
                    for j in range(2):
                        last = pe.transpose(M[:, db, j * P:(j + 1) * P], ctxn[:, j, db * P:(db + 1) * P],
                                            mem.ident)
                last.then_inc(ctxT_done, 1)

            def output(p):
                after(pe, ctxT_low, p + 1)
                project(pe, M, ctxT, w.cut[WO]).then_inc(tl.y_done, 1)

            def step(p, k, u, first, last):
                spread_gates(p, 0, u)
                scores(p, 0, u)
                if not first:
                    after(pe, gtanh_done, p + 1)
                    transpose_ctx(p - 1)
                spread_gates(p, 1, u)
                scores(p, 1, u)
                if not first:
                    output(p - 1)
                values(p, 0, u)
                spread_gates(p, 2, u)
                scores(p, 2, u)
                if not first:
                    tail_transpose(pe, mem, tl, p - 1, M)
                values(p, 1, u)
                if not last:
                    if not first:
                        after(pe, tl.xT_low, p)
                    proj_q(p + 1)
                spread_gates(p, 3, u)
                scores(p, 3, u)
                if not last:
                    proj_k(p + 1)
                values(p, 2, u)
                if not last:
                    proj_v(p + 1)
                values(p, 3, u)
                if not last:
                    proj_g(p + 1)

            pe.wait_ge(consts_loaded, consts_all)
            pe.wait_ge(w.lo_done, WQ + 1)
            proj_q(0)
            pe.wait_ge(w.lo_done, WK + 1)
            proj_k(0)
            pe.wait_ge(w.lo_done, WV + 1)
            proj_v(0)
            pe.wait_ge(w.lo_done, WG + 1)
            proj_g(0)
            pe.wait_ge(w.lo_done, WO + 1)
            over_pairs(pe, step)
            pe.wait_ge(tl.xT_low, NP - 1)
            transpose_ctx(NP - 1)
            output(NP - 1)
            tail_transpose(pe, mem, tl, NP - 1, M)



def cross_attention(nc, mem, tag, ctxT_in, wq, wk, wv, wo, bq, bk, bv, bo):
    with ExitStack() as ctx:
        sem, sb, ps = open_stage(nc, ctx, tag)
        WQ, WK, WV, WO = range(4)
        w = Weights(sem, sb, [[P, DB, D]] * 4)
        b_q, b_k = sb("bq", [P, DB]), sb("bk", [P, DB])
        b_v, b_o = sb("bv", [P, D]), sb("bo", [P, D])
        ct = [sb(f"ct{u}", [P, DB, PT]) for u in range(2)]
        cc = parts(sb, "cc", [P, DB, PT])
        xb = [sb(f"xb{u}", [P, 2, D]) for u in range(2)]
        q32 = sb("q32", [P, DB, PT])
        q_cut = parts(sb, "q", [P, DB, PT])
        q_heads = [parts(sb, f"q_heads{u}", [P, HH, DB, PT]) for u in range(2)]
        k_T = [parts(sb, f"kT{u}", [P, DB, PT]) for u in range(2)]
        v32 = sb("v32", [P, 2, H, DH])
        v_cut = [parts(sb, f"v{u}", [P, 2, H, DH + 1]) for u in range(2)]
        neg_max = [sb(f"neg_max{n}", [P, HH], F16) for n in range(2)]
        prob = [sb(f"prob{n}", [P, HH, P]) for n in range(2)]
        prob_cut = [parts(sb, f"probc{n}", [P, HH, P]) for n in range(2)]
        inv = sb("inv", [P, 2, H])
        ctxn = sb("ctxn", [P, 2, D])
        ctxT = parts(sb, "ctxT", [P, DB, PT])
        tl = Tail(sem, sb)

        A = ps("A", [P, HH, P])
        S = [ps(f"S{n}", [P, HH, P]) for n in range(2)]
        O = ps("O", [P, H, 32])
        M = ps("M", [P, 2, PT])

        bias_loaded = sem("bias_loaded")
        ct_loaded = [sem(f"ct_loaded{u}") for u in range(2)]
        ct_high, ct_low, ones_ready, xb_ready = (sem(n) for n in ("ct_high", "ct_low", "ones_ready", "xb_ready"))
        q_done, k_done, v_done = (sem(n) for n in ("q_done", "k_done", "v_done"))
        q32_done, q_high, q_low, heads_high, heads_low = (
            sem(n) for n in ("q32_done", "q_high", "q_low", "heads_high", "heads_low"))
        k_high, k_low, v32_done, v_high, v_low = (sem(n) for n in ("k_high", "k_low", "v32_done", "v_high", "v_low"))
        a_done, max_done, s_done, exp_done = (sem(n) for n in ("a_done", "max_done", "s_done", "exp_done"))
        exp_high, low_even, low_odd = sem("exp_high"), sem("low_even"), sem("low_odd")
        o_done, inv_done, ctx_ready = sem("o_done"), sem("inv_done"), sem("ctx_ready")
        ctxT_done, ctxT_high, ctxT_low = sem("ctxT_done"), sem("ctxT_high"), sem("ctxT_low")

        block = ctx.enter_context(nc.Block())

        @block.sync
        def _(sp):
            def step(p, k, u, first, last):
                after(sp, ct_low, p)
                sp.dma_start(ct[u][:], ctxT_in[:, :, pair_tokens(p)]).then_inc(ct_loaded[u], 16)
                if first:
                    for n, source in ((WV, wv), (WO, wo)):
                        w.load(sp, n, source)

            for dst, src in ((b_q, bq), (b_k, bk), (b_v, bv.to_broadcast([P, D])), (b_o, bo.to_broadcast([P, D]))):
                sp.dma_start(dst[:], src).then_inc(bias_loaded, 16)
            for n, source in ((WQ, wq), (WK, wk)):
                w.load(sp, n, source)
            over_pairs(sp, step)

        def prob_lo(eng, p, n, done):
            after(eng, exp_high, 4 * p + n + 1)
            eng.tensor_tensor(prob_cut[n % 2].lo[:], prob[n % 2][:], prob_cut[n % 2].hi[:], ALU.subtract)\
                .then_inc(done, 1)

        @block.gpsimd
        def _(pool):
            def add_bias(p, u):
                pool.tensor_tensor(xb[u][:], mem.x[:, pair_tiles(p), :],
                                   b_o[:].unsqueeze(1).to_broadcast([P, 2, D]), ALU.add).then_inc(xb_ready, 1)

            def ct_lo(p, u):
                after(pool, ct_high, p + 1)
                pool.tensor_tensor(cc.lo[:], ct[u][:], cc.hi[:], ALU.subtract).then_inc(ct_low, 1)

            def q_lo(p, u):
                after(pool, q_high, p + 1)
                pool.tensor_tensor(q_cut.lo[:], q32[:], q_cut.hi[:], ALU.subtract).then_inc(q_low, 1)
                pool.drain()
                mask_heads(pool, mem, q_heads[u].lo, q_cut.lo, heads_low)

            def v_lo(p, u):
                after(pool, v_high, p + 1)
                pool.tensor_tensor(v_cut[u].lo[:, :, :, 0:DH], v32[:], v_cut[u].hi[:, :, :, 0:DH], ALU.subtract)\
                    .then_inc(v_low, 1)

            def step(p, k, u, first, last):
                prob_lo(pool, p, 1, low_odd)
                if not first:
                    tail_rstd(pool, mem, tl, p - 1)
                if not last:
                    ct_lo(p + 1, 1 - u)
                if not first:
                    tail_store_x(pool, mem, tl, p - 1)
                prob_lo(pool, p, 3, low_odd)
                if not last:
                    q_lo(p + 1, 1 - u)
                    v_lo(p + 1, 1 - u)
                    after(pool, tl.r_done, p)
                    add_bias(p + 1, 1 - u)

            for u in range(2):
                pool.memset(v_cut[u].hi[:, :, :, DH:DH + 1], 1.0).then_inc(ones_ready, 1)
                pool.memset(v_cut[u].lo[:, :, :, DH:DH + 1], 0.0).then_inc(ones_ready, 1)
            w.low(pool, WQ)
            w.low(pool, WK)
            ct_lo(0, 0)
            w.low(pool, WV)
            q_lo(0, 0)
            v_lo(0, 0)
            w.low(pool, WO)
            pool.wait_ge(bias_loaded, 16 * 4)
            add_bias(0, 0)
            over_pairs(pool, step)
            tail_rstd(pool, mem, tl, NP - 1)
            tail_store_x(pool, mem, tl, NP - 1)

        @block.scalar
        def _(act):
            def ct_hi(p, k, u):
                act.wait_ge(ct_loaded[u], 16 * (k + 1))
                after(act, v_done, p)
                act.activation(cc.hi[:], ct[u][:], ACT.Copy).then_inc(ct_high, 1)

            def copy_q(p):
                after(act, q_done, p + 1)
                after(act, heads_low, p)
                for m in range(DB):
                    act.activation(q32[:, m, :], M[:, m, :], ACT.Identity, bias=b_q[:, m:m + 1])\
                        .then_inc(q32_done, 1)

            def k_hi(p, u):
                after(act, k_done, p + 1)
                for m in range(DB):
                    act.activation(k_T[u].hi[:, m, :], M[:, m, :], ACT.Identity, bias=b_k[:, m:m + 1])\
                        .then_inc(k_high, 1)

            def v_hi(p, u):
                after(act, v32_done, p + 1)
                act.activation(v_cut[u].hi[:, :, :, 0:DH], v32[:], ACT.Copy).then_inc(v_high, 1)

            def exp(p, n):
                after(act, s_done, 4 * p + n + 1)
                act.activation(prob[n % 2][:], S[n % 2][:], ACT.Exp, scale=HEAD_SCALE).then_inc(exp_done, 1)
                act.activation(prob_cut[n % 2].hi[:], S[n % 2][:], ACT.Exp, scale=HEAD_SCALE)\
                    .then_inc(exp_high, 1)

            def ctxT_hi(p):
                after(act, ctxT_done, p + 1)
                act.activation(ctxT.hi[:], M[:], ACT.Copy).then_inc(ctxT_high, 1)

            def step(p, k, u, first, last):
                if not first:
                    ctxT_hi(p - 1)
                exp(p, 0)
                if not last:
                    ct_hi(p + 1, k + u, 1 - u)
                exp(p, 1)
                if not first:
                    tail_xT_high(act, mem, tl, p - 1, M[:])
                exp(p, 2)
                if not last:
                    copy_q(p + 1)
                exp(p, 3)
                if not last:
                    k_hi(p + 1, 1 - u)
                    v_hi(p + 1, 1 - u)

            w.high(act, WQ)
            w.high(act, WK)
            ct_hi(0, 0, 0)
            act.wait_ge(bias_loaded, 16 * 4)
            copy_q(0)
            w.high(act, WV)
            k_hi(0, 0)
            v_hi(0, 0)
            w.high(act, WO)
            over_pairs(act, step)
            ctxT_hi(NP - 1)
            tail_xT_high(act, mem, tl, NP - 1, M[:])

        @block.vector
        def _(dve):
            def maximum(p, n):
                h = 4 * p + n
                after(dve, a_done, h + 1)
                dve.tensor_reduce(neg_max[n % 2][:], A[:], AX.X, ALU.max, negate=True).then_inc(max_done, 1)

            def q_hi(p, u):
                after(dve, q32_done, 2 * p + 2)
                dve.tensor_copy(q_cut.hi[:], q32[:]).then_inc(q_high, 1)
                after(dve, q_high, p + 1)
                mask_heads(dve, mem, q_heads[u].hi, q_cut.hi, heads_high)

            def k_lo(p, u):
                after(dve, k_high, 2 * p + 2)
                for m in range(DB):
                    dve.scalar_tensor_tensor(k_T[u].lo[:, m, :], M[:, m, :], b_k[:, m:m + 1],
                                             k_T[u].hi[:, m, :], ALU.add, ALU.subtract).then_inc(k_low, 1)

            def add_bv(p):
                after(dve, v_done, p + 1)
                after(dve, v_low, p)
                dve.tensor_tensor(v32[:], M[:].rearrange("p j (h d) -> p j h d", h=H),
                                  b_v[:].rearrange("p (h d) -> p h d", h=H).unsqueeze(1)
                                  .to_broadcast([P, 2, H, DH]), ALU.add).then_inc(v32_done, 1)

            def normalize(p, j):
                after(dve, o_done, 2 * p + j + 1)
                dve.reciprocal(inv[:, j, :], O[:, :, DH]).then_inc(inv_done, 1)
                after(dve, inv_done, 2 * p + j + 1)
                dve.tensor_tensor(ctxn[:, j, :].rearrange("p (h d) -> p h d", h=H), O[:, :, 0:DH],
                                  inv[:, j, :].unsqueeze(2).to_broadcast([P, H, DH]), ALU.mult)\
                    .then_inc(ctx_ready, 1)

            def ctxT_lo(p):
                after(dve, ctxT_high, p + 1)
                dve.tensor_tensor(ctxT.lo[:], M[:], ctxT.hi[:], ALU.subtract).then_inc(ctxT_low, 1)

            def residual(p, u):
                after(dve, xb_ready, p + 1)
                tail_residual(dve, tl, p, M[:], xb[u][:])
                tail_stats(dve, tl, p, tl.r)

            def step(p, k, u, first, last):
                maximum(p, 0)
                if not first:
                    ctxT_lo(p - 1)
                maximum(p, 1)
                if not first:
                    residual(p - 1, 1 - u)
                prob_lo(dve, p, 0, low_even)
                maximum(p, 2)
                if not first:
                    tail_apply(dve, tl, p - 1, tl.r, tl.x_stored)
                    tail_xT_low(dve, mem, tl, p - 1, M[:])
                prob_lo(dve, p, 2, low_even)
                maximum(p, 3)
                normalize(p, 0)
                if not last:
                    q_hi(p + 1, 1 - u)
                    k_lo(p + 1, 1 - u)
                    add_bv(p + 1)
                normalize(p, 1)

            dve.wait_ge(bias_loaded, 16 * 4)
            q_hi(0, 0)
            k_lo(0, 0)
            add_bv(0)
            over_pairs(dve, step)
            ctxT_lo(NP - 1)
            residual(NP - 1, 1)
            tail_apply(dve, tl, NP - 1, tl.r, tl.x_stored)
            tail_xT_low(dve, mem, tl, NP - 1, M[:])

        @block.tensor
        def _(pe):
            def proj_q(p):
                project_T(pe, M, w.cut[WQ], blocks_at(mem.xT, pair_tokens(p))).then_inc(q_done, 1)

            def proj_k(p):
                after(pe, ct_low, p + 1)
                after(pe, q32_done, 2 * p + 2)
                project_T(pe, M, w.cut[WK], blocks_of(cc)).then_inc(k_done, 1)

            def proj_v(p):
                after(pe, k_low, 2 * p + 2)
                project(pe, M, cc, w.cut[WV]).then_inc(v_done, 1)

            def first_scores(p, n, u):
                blk, tok = n % 2, slice((n // 2) * P, (n // 2 + 1) * P)
                after(pe, heads_high, p + 1)
                after(pe, k_high, 2 * p + 2)
                after(pe, max_done, 4 * p + n)
                for s in range(HH):
                    last = pe.matmul(A[:, s, :], q_heads[u].hi[:, s, blk, tok], k_T[u].hi[:, blk, tok],
                                     start=True, stop=True)
                last.then_inc(a_done, 1)

            def scores(p, n, u):
                blk, tok = n % 2, slice((n // 2) * P, (n // 2 + 1) * P)
                after(pe, heads_low, p + 1)
                after(pe, k_low, 2 * p + 2)
                after(pe, exp_high, 4 * p + n - 1)
                for a in range(2):
                    product(pe, S[n % 2][:, 4 * a:4 * a + 4, :],
                            (k_T[u].hi[:, blk, tok], k_T[u].lo[:, blk, tok]),
                            (four_heads(q_heads[u].hi, a, blk, tok), four_heads(q_heads[u].lo, a, blk, tok)))

            def subtract_maximum(p, n):
                after(pe, max_done, 4 * p + n + 1)
                for s in range(HH):
                    last = pe.matmul(S[n % 2][:, s, :], neg_max[n % 2][:, s:s + 1].to_broadcast([P, P]),
                                     mem.ident16[:], start=False, stop=True, skip_group_check=True)
                last.then_inc(s_done, 1)

            def values(p, n, u):
                blk, j = n % 2, n // 2
                after(pe, low_odd if blk else low_even, 2 * p + j + 1)
                after(pe, v_low, p + 1)
                after(pe, ctx_ready, 2 * p + j)
                cut, v = prob_cut[n % 2], v_cut[u]
                for s in range(HH):
                    h = HH * blk + s
                    last = product(pe, O[:, h, 0:DH + 1], (cut.hi[:, s, :], cut.lo[:, s, :]),
                                   (v.hi[:, j, h, :], v.lo[:, j, h, :]))
                if blk:
                    last.then_inc(o_done, 1)

            def transpose_ctx(p):
                after(pe, ctx_ready, 2 * p + 2)
                for db in range(DB):
                    for j in range(2):
                        last = pe.transpose(M[:, db, j * P:(j + 1) * P], ctxn[:, j, db * P:(db + 1) * P],
                                            mem.ident)
                last.then_inc(ctxT_done, 1)

            def output(p):
                after(pe, ctxT_low, p + 1)
                project(pe, M, ctxT, w.cut[WO]).then_inc(tl.y_done, 1)

            def step(p, k, u, first, last):
                first_scores(p, 0, u)
                scores(p, 0, u)
                if not first:
                    after(pe, v32_done, p + 1)
                    transpose_ctx(p - 1)
                subtract_maximum(p, 0)
                first_scores(p, 1, u)
                scores(p, 1, u)
                if not first:
                    output(p - 1)
                subtract_maximum(p, 1)
                first_scores(p, 2, u)
                values(p, 0, u)
                scores(p, 2, u)
                if not first:
                    tail_transpose(pe, mem, tl, p - 1, M)
                subtract_maximum(p, 2)
                values(p, 1, u)
                if not last:
                    if not first:
                        after(pe, tl.xT_low, p)
                    proj_q(p + 1)
                first_scores(p, 3, u)
                scores(p, 3, u)
                subtract_maximum(p, 3)
                if not last:
                    proj_k(p + 1)
                values(p, 2, u)
                if not last:
                    proj_v(p + 1)
                values(p, 3, u)

            pe.wait_ge(ones_ready, 4)
            pe.wait_ge(w.lo_done, WQ + 1)
            proj_q(0)
            pe.wait_ge(w.lo_done, WK + 1)
            proj_k(0)
            pe.wait_ge(w.lo_done, WV + 1)
            proj_v(0)
            pe.wait_ge(w.lo_done, WO + 1)
            over_pairs(pe, step)
            pe.wait_ge(tl.xT_low, NP - 1)
            transpose_ctx(NP - 1)
            output(NP - 1)
            tail_transpose(pe, mem, tl, NP - 1, M)



def most_tiles(k):
    return (k * T + E * (RT - 1)) // RT


class Routed:

    def __init__(self, nc, ctx, tag, k, rows_in, rows_out):
        def sb(name, shape, dt):
            return ctx.enter_context(nc.sbuf_tensor(f"{tag}_{name}", shape, dt))

        self.k, self.tiles = k, most_tiles(k)
        self.slot = sb("slot", [P, k, NB], U32)
        self.gate = sb("gate", [P, k, NB], F32)
        self.expert = sb("expert", [P, self.tiles], U32)
        self.rows_in, self.rows_out = rows_in, rows_out


class SlotNumbers:

    def __init__(self, sb, routed):
        self.routed = routed
        self.in_tile, self.slot_of, self.own = (sb(n, [P, NB, E]) for n in ("tile_rows", "slot_of", "own_slot"))
        self.rows, self.start, self.end = (sb(n, [P, E]) for n in ("rows", "start", "end"))
        self.padded, self.slot = sb("padded", [P, E], U32), sb("slot_f", [P, NB])
        self.passed, self.expert = sb("passed", [P, routed.tiles, E]), sb("expert_f", [P, routed.tiles])

    def starts(self, dve, link, mem, BEFORE, TILES):
        tiles = self.routed.tiles
        link(dve.tensor_copy(self.in_tile[:], TILES[:]))
        for e in range(E):
            last = dve.tensor_tensor_scan(self.slot_of[:, :, e], self.in_tile[:, :, e], mem.zeros32, 0.0,
                                          ALU.add, ALU.add)
        link(last)
        link(dve.tensor_scalar(self.rows[:], self.slot_of[:, NB - 1, :], float(RT - 1), None, ALU.add))
        link(dve.tensor_copy(self.padded[:], self.rows[:]))
        link(dve.tensor_scalar(self.padded[:], self.padded[:], ~(RT - 1) & 0xffffffff, None, ALU.bitwise_and))
        link(dve.tensor_copy(self.rows[:], self.padded[:]))
        link(dve.tensor_tensor_scan(self.end[:], self.rows[:], mem.zeros32[:, 0:E], 0.0, ALU.add, ALU.add))
        link(dve.tensor_tensor(self.start[:], self.end[:], self.rows[:], ALU.subtract))
        link(dve.tensor_tensor(self.slot_of[:], self.slot_of[:], self.in_tile[:], ALU.subtract))
        link(dve.tensor_tensor(self.slot_of[:], self.slot_of[:], BEFORE[:], ALU.add))
        link(dve.tensor_tensor(self.slot_of[:], self.slot_of[:],
                               self.start[:].unsqueeze(1).to_broadcast([P, NB, E]), ALU.add))
        link(dve.tensor_tensor(self.passed[:], mem.tile_start[:, 0:tiles].unsqueeze(2).to_broadcast([P, tiles, E]),
                               self.end[:].unsqueeze(1).to_broadcast([P, tiles, E]), ALU.is_ge))
        link(dve.tensor_reduce(self.expert[:], self.passed[:], AX.X, ALU.add))
        link(dve.tensor_scalar(self.routed.expert[:], self.expert[:], float(E - 1), None, ALU.min))

    def slots(self, dve, link, marks, values, k, slot_ready):
        link(dve.tensor_tensor(self.own[:], values, marks, ALU.mult))
        link(dve.tensor_reduce(self.routed.gate[:, k, :], self.own[:], AX.X, ALU.add))
        link(dve.tensor_tensor(self.own[:], self.slot_of[:], marks, ALU.mult))
        link(dve.tensor_reduce(self.slot[:], self.own[:], AX.X, ALU.add))
        dve.tensor_copy(self.routed.slot[:, k, :], self.slot[:]).then_inc(slot_ready, 1)
        dve.wait_ge(slot_ready, k + 1)


def router(nc, mem, tag, w_router, decide, routed, x_kept):
    with ExitStack() as ctx:
        sem, sb, ps = open_stage(nc, ctx, tag)
        CHUNK, NCH = 4 * P, T // (4 * P)
        w = Weights(sem, sb, [[P, DB, E]])
        logitsT = [sb(f"logitsT{a}", [E, CHUNK]) for a in range(2)]
        LT = [ps(f"LT{a}", [P, CHUNK]) for a in range(2)]
        L = ps("L", [P, NB, E])
        lt_done, lt_ready, l_done = sem("lt_done"), sem("lt_ready"), sem("l_done")
        slot_ready, sent, kept = sem("slot_ready"), sem("sent"), sem("kept")
        rest = decide(mem, sem, sb, ps, L, l_done, routed, slot_ready)
        block = ctx.enter_context(nc.Block())

        @block.sync
        def _(sp):
            w.load(sp, 0, w_router)
            sp.dma_start(x_kept, mem.x[:]).then_inc(kept, 16)
            sp.wait_ge(kept, 16)

        @block.gpsimd
        def _(pool):
            w.low(pool, 0)
            for k in range(routed.k):
                pool.wait_ge(slot_ready, k + 1)
                for b in range(NB):
                    pool.indirect_dma_start(routed.rows_in,
                                            bass.IndirectOffsetOnAxis(routed.slot[:, k, b:b + 1], 0),
                                            mem.x[:, b, :], None).then_inc(sent, 16)
            pool.wait_ge(sent, 16 * NB * routed.k)

        @block.tensor
        def _(pe):
            pe.wait_ge(w.lo_done, 1)
            for c in range(NCH + 1):
                if c < NCH:
                    after(pe, lt_ready, c - 1)
                    for db in range(DB):
                        x = blocks_at(mem.xT, slice(c * CHUNK, (c + 1) * CHUNK))(db)
                        last = product(pe, LT[c % 2][0:E, :], (w.cut[0].hi[:, db, :], w.cut[0].lo[:, db, :]), x,
                                       start=(db == 0), stop=(db == DB - 1))
                    last.then_inc(lt_done, 1)
                if c:
                    pe.wait_ge(lt_ready, c)
                    for j in range(4):
                        last = pe.transpose(L[:, 4 * (c - 1) + j, :], logitsT[(c - 1) % 2][:, j * P:(j + 1) * P],
                                            mem.ident[0:E, 0:E])
            last.then_inc(l_done, 1)
            rest["tensor"](pe)

        @block.scalar
        def _(act):
            w.high(act, 0)
            for c in range(NCH):
                act.wait_ge(lt_done, c + 1)
                act.activation(logitsT[c % 2][:], LT[c % 2][0:E, :], ACT.Copy).then_inc(lt_ready, 1)
            rest["scalar"](act)

        @block.vector
        def _(dve):
            rest["vector"](dve)


def over_experts(ap):
    return ap.unsqueeze(2).to_broadcast([P, NB, E])


class Softmax:

    def __init__(self, sem, sb, L, l_done):
        self.L, self.l_done = L, l_done
        self.top, self.total, self.inv = sb("top", [P, NB]), sb("total", [P, NB]), sb("inv", [P, NB])
        self.z, self.e, self.p = sb("z", [P, NB, E]), sb("e", [P, NB, E]), sb("p", [P, NB, E])
        self.z_done, self.e_done = sem("z_done"), sem("e_done")

    def scalar(self, act):
        act.wait_ge(self.z_done, 1)
        act.activation(self.e[:], self.z[:], ACT.Exp).then_inc(self.e_done, 1)

    def vector(self, dve, link):
        dve.wait_ge(self.l_done, 1)
        link(dve.tensor_reduce(self.top[:], self.L[:], AX.X, ALU.max))
        dve.tensor_tensor(self.z[:], self.L[:], over_experts(self.top[:]), ALU.subtract)\
            .then_inc(self.z_done, 1)
        dve.wait_ge(self.e_done, 1)
        link(dve.tensor_reduce(self.total[:], self.e[:], AX.X, ALU.add))
        link(dve.reciprocal(self.inv[:], self.total[:]))
        link(dve.tensor_tensor(self.p[:], self.e[:], over_experts(self.inv[:]), ALU.mult))


def chained(dve, sem):
    count = [0]

    def link(instruction):
        count[0] += 1
        instruction.then_inc(sem, 1)
        dve.wait_ge(sem, count[0])

    return link


def count_rows(pe, mem, marks, BEFORE, TILES):
    flat = marks[:].rearrange("p b e -> p (b e)")
    pe.matmul(BEFORE[:].rearrange("p b e -> p (b e)"), mem.earlier, flat, start=True, stop=True)
    return pe.matmul(TILES[:].rearrange("p b e -> p (b e)"), mem.ones, flat, start=True, stop=True)


def top_experts(mem, sem, sb, ps, L, l_done, routed, slot_ready):
    soft = Softmax(sem, sb, L, l_done)
    above, equal = sb("above", [P, NB, E, E]), sb("equal", [P, NB, E, E])
    rank, chosen, kept = sb("rank", [P, NB, E]), sb("chosen", [P, NB, E]), sb("kept", [P, NB, E])
    kept_sum, kept_inv = sb("kept_sum", [P, NB]), sb("kept_inv", [P, NB])
    gates, marks = sb("gates", [P, NB, E]), sb("marks", [P, NB, E])
    numbers = SlotNumbers(sb, routed)
    BEFORE, TILES = ps("BEFORE", [P, NB, E]), ps("TILES", [P, NB, E])
    chain, chosen_done, counted = sem("chain"), sem("chosen_done"), sem("counted")

    def tensor(pe):
        pe.wait_ge(chosen_done, 1)
        count_rows(pe, mem, chosen, BEFORE, TILES).then_inc(counted, 1)

    def vector(dve):
        link = chained(dve, chain)
        soft.vector(dve, link)
        others = soft.p[:].unsqueeze(2).to_broadcast([P, NB, E, E])
        own = soft.p[:].unsqueeze(3).to_broadcast([P, NB, E, E])
        before = mem.lower8.unsqueeze(1).to_broadcast([P, NB, E, E])
        dve.tensor_tensor(above[:], others, own, ALU.is_gt)
        link(dve.tensor_tensor(equal[:], others, own, ALU.is_equal))
        link(dve.tensor_tensor(equal[:], equal[:], before, ALU.mult))
        link(dve.tensor_tensor(above[:], above[:], equal[:], ALU.add))
        link(dve.tensor_reduce(rank[:], above[:], AX.X, ALU.add))
        dve.tensor_scalar(chosen[:], rank[:], float(TOPK), None, ALU.is_lt).then_inc(chosen_done, 1)
        dve.wait_ge(chosen_done, 1)
        link(dve.tensor_tensor(kept[:], soft.p[:], chosen[:], ALU.mult))
        link(dve.tensor_reduce(kept_sum[:], kept[:], AX.X, ALU.add))
        link(dve.reciprocal(kept_inv[:], kept_sum[:]))
        link(dve.tensor_tensor(gates[:], kept[:], over_experts(kept_inv[:]), ALU.mult))
        dve.wait_ge(counted, 1)
        numbers.starts(dve, link, mem, BEFORE, TILES)
        for k in range(TOPK):
            link(dve.tensor_scalar(marks[:], rank[:], float(k), None, ALU.is_equal))
            numbers.slots(dve, link, marks[:], gates[:], k, slot_ready)

    return {"tensor": tensor, "scalar": soft.scalar, "vector": vector}


BITS = 30


def selected_expert(mem, sem, sb, ps, L, l_done, routed, slot_ready):
    soft = Softmax(sem, sb, L, l_done)
    bit, cand, thr = (sb(n, [P, E], U32) for n in ("bit", "cand", "thr"))
    enough = sb("enough", [P, E], U32)
    flags, part = sb("flags", [P, E, NB]), sb("part", [P, E])
    above, equal, first = (sb(n, [P, NB, E]) for n in ("above", "equal", "first"))
    in_tile, upto, value, marks = (sb(n, [P, NB, E]) for n in ("in_tile", "upto", "value", "marks"))
    some, best = sb("some", [P, NB]), sb("best", [P, NB])
    need = sb("need", [P, E])
    numbers = SlotNumbers(sb, routed)
    TOT = ps("TOT", [P, E])
    BEFORE = ps("BEFORE", [P, NB, E])
    TILES = ps("TILES", [P, NB, E])
    chain, thr_done = sem("chain"), sem("thr_done")
    part_done, tot_done, bit_done = sem("part_done"), sem("tot_done"), sem("bit_done")
    marks_done, marks_tot = sem("marks_done"), sem("marks_tot")
    cand_done, flags_done, enough_done = sem("cand_done"), sem("flags_done"), sem("enough_done")
    above_done, above_tot, equal_done, equal_tot = (sem(n) for n in ("above_done", "above_tot", "equal_done", "equal_tot"))

    def tensor(pe):
        with pe.Fori(0, BITS) as i:
            pe.wait_ge(part_done, i + 1)
            pe.matmul(TOT[:], mem.ones, part[:], start=True, stop=True).then_inc(tot_done, 1)
        pe.wait_ge(above_done, 1)
        pe.matmul(TOT[:], mem.ones, part[:], start=True, stop=True).then_inc(above_tot, 1)
        pe.wait_ge(equal_done, 1)
        count_rows(pe, mem, equal, BEFORE, TILES).then_inc(equal_tot, 1)
        pe.wait_ge(marks_done, 1)
        count_rows(pe, mem, marks, BEFORE, TILES).then_inc(marks_tot, 1)

    def vector(dve):
        link = chained(dve, chain)
        soft.vector(dve, link)
        by_expert = soft.p[:].rearrange("p b e -> p e b")
        thr_f = thr[:].bitcast(F32)
        dve.memset(thr[:], 0)
        link(dve.memset(bit[:], 1 << (BITS - 1)))
        with dve.Fori(0, BITS) as i:
            dve.tensor_tensor(cand[:], thr[:], bit[:], ALU.bitwise_or).then_inc(cand_done, 1)
            dve.wait_ge(cand_done, i + 1)
            dve.tensor_tensor(flags[:], by_expert, cand[:].bitcast(F32).unsqueeze(2).to_broadcast([P, E, NB]),
                              ALU.is_ge).then_inc(flags_done, 1)
            dve.wait_ge(flags_done, i + 1)
            dve.tensor_reduce(part[:], flags[:], AX.X, ALU.add).then_inc(part_done, 1)
            dve.wait_ge(tot_done, i + 1)
            dve.tensor_scalar(enough[:], TOT[:], float(CAP), None, ALU.is_ge).then_inc(enough_done, 1)
            dve.wait_ge(enough_done, i + 1)
            dve.tensor_scalar(bit[:], bit[:], 1, None, ALU.logical_shift_right).then_inc(bit_done, 1)
            dve.copy_predicated(thr[:], enough[:], cand[:]).then_inc(thr_done, 1)
            dve.wait_ge(bit_done, i + 1)
            dve.wait_ge(thr_done, i + 1)
        thr_b = thr_f.unsqueeze(1).to_broadcast([P, NB, E])
        link(dve.tensor_tensor(above[:], soft.p[:], thr_b, ALU.is_gt))
        dve.tensor_reduce(part[:], above[:].rearrange("p b e -> p e b"), AX.X, ALU.add).then_inc(above_done, 1)
        dve.tensor_tensor(equal[:], soft.p[:], thr_b, ALU.is_equal).then_inc(equal_done, 1)
        dve.wait_ge(above_tot, 1)
        link(dve.tensor_scalar(need[:], TOT[:], -1.0, float(CAP), ALU.mult, ALU.add))
        dve.wait_ge(equal_tot, 1)
        link(dve.tensor_copy(in_tile[:], TILES[:]))
        dve.wait_ge(equal_done, 1)
        for e in range(E):
            last = dve.tensor_tensor_scan(upto[:, :, e], in_tile[:, :, e], mem.zeros32, 0.0, ALU.add, ALU.add)
        link(last)
        link(dve.tensor_tensor(upto[:], upto[:], in_tile[:], ALU.subtract))
        link(dve.tensor_tensor(upto[:], BEFORE[:], upto[:], ALU.add))
        link(dve.tensor_tensor(first[:], upto[:], need[:].unsqueeze(1).to_broadcast([P, NB, E]), ALU.is_lt))
        link(dve.tensor_tensor(first[:], first[:], equal[:], ALU.mult))
        link(dve.tensor_tensor(above[:], above[:], first[:], ALU.add))
        link(dve.tensor_reduce(some[:], above[:], AX.X, ALU.max))
        link(dve.tensor_scalar(above[:], above[:], 1.0, 4.0, ALU.subtract, ALU.mult))
        link(dve.tensor_tensor(above[:], above[:], over_experts(some[:]), ALU.mult))
        link(dve.tensor_tensor(value[:], soft.p[:], above[:], ALU.add))
        link(dve.tensor_reduce(best[:], value[:], AX.X, ALU.max))
        link(dve.tensor_tensor(marks[:], value[:], over_experts(best[:]), ALU.is_equal))
        link(dve.tensor_tensor(marks[:], marks[:], mem.rising8.unsqueeze(1).to_broadcast([P, NB, E]), ALU.mult))
        link(dve.tensor_reduce(best[:], marks[:], AX.X, ALU.max))
        dve.tensor_tensor(marks[:], marks[:], over_experts(best[:]), ALU.is_equal).then_inc(marks_done, 1)
        dve.wait_ge(marks_done, 1)
        dve.wait_ge(marks_tot, 1)
        numbers.starts(dve, link, mem, BEFORE, TILES)
        numbers.slots(dve, link, marks[:], soft.p[:], 0, slot_ready)

    return {"tensor": tensor, "scalar": soft.scalar, "vector": vector}



CUT = 1024


def sorted_experts(nc, mem, routed, tag, w_up, w_down, width, gelu):
    with ExitStack() as ctx:
        sem, sb, ps = open_stage(nc, ctx, tag)
        MB = width // P
        G = MB // 2
        NT, TB = routed.tiles, RT // P
        up, down = parts(sb, "up", [P, DB, E, width]), parts(sb, "down", [P, MB, E, D])
        raw = [sb(f"raw{a}", [P, CUT]) for a in range(2)]
        rows = [sb(f"rows{u}", [P, TB, D]) for u in range(2)]
        xT = [parts(sb, f"xT{u}", [P, DB, RT]) for u in range(2)]
        h32 = [sb(f"h{g}", [P, 2, RT]) for g in range(2)]
        hT = [parts(sb, f"hT{u}", [P, MB, RT]) for u in range(2)]
        y = [sb(f"y{u}", [P, TB, D]) for u in range(2)]
        XB = [ps(f"XB{u}", [P, DB, RT]) for u in range(2)]
        HB = [ps(f"HB{g}", [P, 2, RT]) for g in range(4)]
        YB = ps("YB", [P, TB, 512])
        raw_loaded, cut_high, cut_done = [sem(f"raw_loaded{a}") for a in range(2)], sem("cut_high"), sem("cut_done")
        rows_loaded = [sem(f"rows_loaded{u}") for u in range(2)]
        xT_done, x_high, x_low = sem("xT_done"), sem("x_high"), sem("x_low")
        h_done, h_high, h_low = sem("h_done"), sem("h_high"), sem("h_low")
        y_done, y_ready, y_free = sem("y_done"), sem("y_ready"), [sem(f"y_free{u}") for u in range(2)]
        block = ctx.enter_context(nc.Block())
        assert NT % 2 == 1 and G % 2 == 0 and TB == 2

        jobs = [(cut, source, e, slice(b, b + CUT // size), size)
                for e in range(E) for cut, source, blocks, size in ((up, w_up, DB, width), (down, w_down, MB, D))
                for b in range(0, blocks, CUT // size)]
        JOBS = len(jobs) // E

        def over_tiles(eng, step):
            step(0, 0, 0, 3)
            step(1, 0, 1, 3)
            with eng.Fori(0, (NT - 5) // 2) as i:
                step(2 * i + 2, i + 1, 0, 3)
                step(2 * i + 3, i + 1, 1, 3)
            step(NT - 3, NT // 2 - 1, 0, 2)
            step(NT - 2, NT // 2 - 1, 1, 1)
            step(NT - 1, NT // 2, 0, 0)

        def tile_rows(source, s):
            return source[bass.ds(s * RT, RT), :].rearrange("(t p) d -> p t d", p=P)

        @block.gpsimd
        def _(pool):
            def blocks_of_raw(n):
                return raw[n % 2][:].rearrange("p (b c) -> p b c", c=jobs[n][4])

            def load(n):
                cut, source, e, blocks, size = jobs[n]
                after(pool, cut_done, n - 1)
                pool.dma_start(blocks_of_raw(n), source[:, blocks, e, :]).then_inc(raw_loaded[n % 2], 16)

            load(0)
            for n, (cut, source, e, blocks, size) in enumerate(jobs):
                if n + 1 < len(jobs):
                    load(n + 1)
                pool.wait_ge(raw_loaded[n % 2], 16 * (n // 2 + 1))
                pool.tensor_copy(cut.hi[:, blocks, e, :], blocks_of_raw(n)).then_inc(cut_high, 1)
                pool.wait_ge(cut_high, n + 1)
                pool.tensor_tensor(cut.lo[:, blocks, e, :], blocks_of_raw(n), cut.hi[:, blocks, e, :],
                                   ALU.subtract).then_inc(cut_done, 1)

        @block.sync
        def _(sp):
            def load(s, k, u):
                sp.dma_start(rows[u][:], tile_rows(routed.rows_in, s)).then_inc(rows_loaded[u], 16)

            def step(s, k, u, more):
                if more >= 3:
                    after(sp, xT_done, s + 2)
                    load(s + 3, k + 1 + u, 1 - u)
                after(sp, y_ready, s + 1)
                sp.dma_start(tile_rows(routed.rows_out, s), y[u][:]).then_inc(y_free[u], 16)

            load(0, 0, 0)
            load(1, 0, 1)
            sp.wait_ge(xT_done, 1)
            load(2, 1, 0)
            over_tiles(sp, step)
            sp.wait_ge(y_free[0], 16 * (NT // 2 + 2))
            sp.wait_ge(y_free[1], 16 * (NT // 2 + 1))

        @block.tensor
        def _(pe):
            def expert_of(s):
                return pe.value_load(routed.expert[0:1, bass.ds(s, 1)], min_val=0, max_val=E - 1)

            def of_expert(cut, blk, e, columns):
                return tuple(w[:, blk, bass.ds(e, 1), columns].rearrange("p o c -> p (o c)") for w in (cut.hi, cut.lo))

            def transpose(s, k, u):
                pe.wait_ge(rows_loaded[u], 16 * (k + 1))
                after(pe, x_low, s - 1)
                for db in range(DB):
                    for t in range(TB):
                        last = pe.transpose(XB[u][:, db, t * P:(t + 1) * P], rows[u][:, t, db * P:(db + 1) * P],
                                            mem.ident)
                last.then_inc(xT_done, 1)

            def hidden(s, u):
                e = expert_of(s)
                pe.wait_ge(cut_done, JOBS * e + JOBS)
                after(pe, x_low, s + 1)
                for g in range(G):
                    bank = HB[(G * u + g) % 4]
                    after(pe, h_high, G * s + g - 3)
                    for m in (2 * g, 2 * g + 1):
                        for db in range(DB):
                            last = product(pe, bank[:, m % 2, :], of_expert(up, db, e, slice(m * P, (m + 1) * P)),
                                           (xT[u].hi[:, db, :], xT[u].lo[:, db, :]),
                                           start=(db == 0), stop=(db == DB - 1))
                    last.then_inc(h_done, 1)

            def output(s, u):
                e = expert_of(s)
                after(pe, h_low, G * s + G)
                after(pe, y_ready, s)
                for m in range(MB):
                    w = of_expert(down, m, e, slice(0, D))
                    for t in range(TB):
                        tok = slice(t * P, (t + 1) * P)
                        last = product(pe, YB[:, t, 0:D], (hT[u].hi[:, m, tok], hT[u].lo[:, m, tok]), w,
                                       start=(m == 0), stop=(m == MB - 1))
                last.then_inc(y_done, 1)

            def step(s, k, u, more):
                if more >= 2:
                    transpose(s + 2, k + 1, u)
                if more >= 1:
                    hidden(s + 1, 1 - u)
                output(s, u)

            transpose(0, 0, 0)
            transpose(1, 0, 1)
            hidden(0, 0)
            over_tiles(pe, step)

        @block.scalar
        def _(act):
            def x_hi(s, u):
                after(act, xT_done, s + 1)
                after(act, h_done, G * (s - 1))
                act.activation(xT[u].hi[:], XB[u][:], ACT.Copy).then_inc(x_high, 1)

            def h_hi(s, u):
                after(act, y_done, s - 1)
                for g in range(G):
                    bank = HB[(G * u + g) % 4]
                    after(act, h_done, G * s + g + 1)
                    after(act, h_low, G * s + g - 1)
                    act.activation(h32[g % 2][:], bank[:], gelu)
                    act.activation(hT[u].hi[:, 2 * g:2 * g + 2, :], bank[:], gelu).then_inc(h_high, 1)

            def step(s, k, u, more):
                if more >= 2:
                    x_hi(s + 2, u)
                if more >= 1:
                    h_hi(s + 1, 1 - u)

            x_hi(0, 0)
            x_hi(1, 1)
            h_hi(0, 0)
            over_tiles(act, step)

        @block.vector
        def _(dve):
            def x_lo(s, u):
                after(dve, x_high, s + 1)
                dve.tensor_tensor(xT[u].lo[:], XB[u][:], xT[u].hi[:], ALU.subtract).then_inc(x_low, 1)

            def h_lo(s, u):
                for g in range(G):
                    after(dve, h_high, G * s + g + 1)
                    high = hT[u].hi[:, 2 * g:2 * g + 2, :]
                    dve.tensor_tensor(hT[u].lo[:, 2 * g:2 * g + 2, :], h32[g % 2][:], high, ALU.subtract)\
                        .then_inc(h_low, 1)

            def step(s, k, u, more):
                if more >= 2:
                    x_lo(s + 2, u)
                if more >= 1:
                    h_lo(s + 1, 1 - u)
                after(dve, y_done, s + 1)
                dve.wait_ge(y_free[u], 16 * (k + 1))
                dve.tensor_copy(y[u][:], YB[:, :, 0:D]).then_inc(y_ready, 1)

            for u in range(2):
                dve.sem_inc(y_free[u], 16)
            x_lo(0, 0)
            x_lo(1, 1)
            h_lo(0, 0)
            over_tiles(dve, step)


def norm_of_sorted(nc, mem, routed, tag, x_kept, out):
    with ExitStack() as ctx:
        sem, sb, ps = open_stage(nc, ctx, tag)
        K = routed.k
        tl = Tail(sem, sb)
        x = [sb(f"x{u}", [P, 2, D]) for u in range(2)]
        index = [sb(f"index{u}", [P, K, 2], U32) for u in range(2)]
        y = [sb(f"y{u}", [P, K, 2, D]) for u in range(2)]
        M = ps("M", [P, 2, PT])
        x_loaded, fetched = [sem(f"x_loaded{u}") for u in range(2)], [sem(f"fetched{u}") for u in range(2)]
        r_added, r_complete, out_stored = sem("r_added"), sem("r_complete"), sem("out_stored")
        block = ctx.enter_context(nc.Block())

        @block.gpsimd
        def _(pool):
            def fetch(p, u):
                pool.tensor_copy(index[u][:], routed.slot[:, :, pair_tiles(p)])
                pool.drain()
                for k in range(K):
                    for j in range(2):
                        pool.indirect_dma_start(y[u][:, k, j, :], None, routed.rows_out,
                                                bass.IndirectOffsetOnAxis(index[u][:, k, j:j + 1], 0))\
                            .then_inc(fetched[u], 16)

            fetch(0, 0)
            fetch(1, 1)
            with pool.Fori(0, NP // 2 - 1) as i:
                for u in range(2):
                    tail_rstd(pool, mem, tl, 2 * i + u)
                    pool.wait_ge(r_complete, 2 * i + u + 1)
                    fetch(2 * i + 2 + u, u)
            tail_rstd(pool, mem, tl, NP - 2)
            tail_rstd(pool, mem, tl, NP - 1)

        @block.vector
        def _(dve):
            def step(p, q, u, first, last):
                dve.wait_ge(x_loaded[u], 16 * (q + 1))
                dve.wait_ge(fetched[u], 32 * K * (q + 1))
                after(dve, tl.xn_done, 2 * p)
                for k in range(K):
                    if k:
                        after(dve, r_added, (K - 1) * p + k)
                    for j in range(2):
                        tile = bass.ds(2 * p + j, 1)
                        so_far = tl.r[:, j, :] if k else x[u][:, j, :]
                        done = r_added if k < K - 1 else r_complete
                        added = dve.scalar_tensor_tensor(tl.r[:, j, :], y[u][:, k, j, :], routed.gate[:, k, tile],
                                                         so_far, ALU.mult, ALU.add)
                    added.then_inc(done, 1)
                after(dve, r_complete, p + 1)
                tail_stats(dve, tl, p, tl.r)
                if out is None and not first:
                    tail_xT_low(dve, mem, tl, p - 1, M[:])
                    after(dve, tl.xT_done, p)
                tail_apply(dve, tl, p, tl.r, tl.x_stored)

            over_pairs(dve, step)
            if out is None:
                tail_xT_low(dve, mem, tl, NP - 1, M[:])

        @block.sync
        def _(sp):
            def step(p, k, u, first, last):
                after(sp, r_complete, p - 1)
                sp.dma_start(x[u][:], x_kept[:, pair_tiles(p), :]).then_inc(x_loaded[u], 16)
                if out is not None and not first:
                    store(p - 1)

            def store(p):
                after(sp, tl.xn_done, 2 * p + 2)
                sp.dma_start(out[:, pair_tiles(p), :], tl.xn[:]).then_inc(out_stored, 16)
                after(sp, out_stored, 16 * (p + 1))
                sp.sem_inc(tl.x_stored, 1)

            step(0, 0, 0, True, False)
            step(1, 0, 1, False, False)
            with sp.Fori(0, (NP - 2) // 2) as i:
                step(2 * i + 2, i + 1, 0, False, False)
                step(2 * i + 3, i + 1, 1, False, False)
            if out is not None:
                store(NP - 1)

        if out is None:
            @block.tensor
            def _(pe):
                over_pairs(pe, lambda p, k, u, first, last: tail_transpose(pe, mem, tl, p, M))

            @block.scalar
            def _(act):
                def step(p, k, u, first, last):
                    after(act, tl.xn_done, 2 * p + 2)
                    act.activation(mem.x[:, pair_tiles(p), :], tl.xn[:], ACT.Copy).then_inc(tl.x_stored, 1)
                    tail_xT_high(act, mem, tl, p, M[:])

                over_pairs(act, step)



def window_attention(nc, mem, w_qkv, w_out, b_out):
    with ExitStack() as ctx:
        sem, sb, ps = open_stage(nc, ctx, "wa")
        WQ, WK, WO = range(3)
        w = Weights(sem, sb, [[P, DB, D]] * 3)
        b_o = sb("bo", [P, D])
        xb = [sb(f"xb{u}", [P, 2, D]) for u in range(2)]
        q_T = parts(sb, "qT", [P, DB, PT])
        k_T = parts(sb, "kT", [P, DB, PT])
        keys = [parts(sb, f"keys{u}", [P, 2, D]) for u in range(2)]
        sim = sb("sim", [P, 2, P])
        row_max, neg_max = sb("row_max", [P, 2]), sb("neg_max", [P, 2])
        prob = sb("prob", [P, 2, P])
        own_sum, pad, total, inv = (sb(n, [P, 2]) for n in ("own_sum", "pad", "total", "inv"))
        probn, probT = sb("probn", [P, 2, P]), parts(sb, "probT", [P, 2, P])
        oT = parts(sb, "oT", [P, DB, PT])
        tl = Tail(sem, sb)
        Q, K = ps("Q", [P, DB, PT]), ps("K", [P, DB, PT])
        S = ps("S", [P, 2, 2 * P])
        KEYS = ps("KEYS", [P, 2, D])
        PB = ps("PB", [P, 2, 2 * P])
        OB = ps("OB", [P, DB, PT])
        Y = ps("Y", [P, 2, D])
        XB = ps("XB", [P, DB, PT])
        names = ("bias_loaded q_done q_high q_low k_done k_high k_low keys_done keys_high keys_low s_done sim_done "
                 "max_done neg_done exp_done pad_done total_done inv_done probn_done pT_done pT_high pT_low o_done "
                 "o_high o_low xb_ready")
        (bias_loaded, q_done, q_high, q_low, k_done, k_high, k_low, keys_done, keys_high, keys_low, s_done, sim_done,
         max_done, neg_done, exp_done, pad_done, total_done, inv_done, probn_done, pT_done, pT_high, pT_low, o_done,
         o_high, o_low, xb_ready) = (sem(n) for n in names.split())
        block = ctx.enter_context(nc.Block())

        @block.sync
        def _(sp):
            w.load(sp, WQ, w_qkv[:, :, 0:D])
            w.load(sp, WK, w_qkv[:, :, D:2 * D])
            sp.dma_start(b_o[:], b_out.to_broadcast([P, D])).then_inc(bias_loaded, 16)
            w.load(sp, WO, w_out)

        @block.gpsimd
        def _(pool):
            def add_bias(p, u):
                pool.tensor_tensor(xb[u][:], mem.x[:, pair_tiles(p), :],
                                   b_o[:].unsqueeze(1).to_broadcast([P, 2, D]), ALU.add).then_inc(xb_ready, 1)

            def step(p, k, u, first, last):
                if not first:
                    tail_rstd(pool, mem, tl, p - 1)
                    tail_store_x(pool, mem, tl, p - 1)
                if not last:
                    after(pool, tl.r_done, p)
                    add_bias(p + 1, 1 - u)

            for n in (WQ, WK, WO):
                w.low(pool, n)
            pool.wait_ge(bias_loaded, 16)
            add_bias(0, 0)
            over_pairs(pool, step)
            tail_rstd(pool, mem, tl, NP - 1)
            tail_store_x(pool, mem, tl, NP - 1)

        @block.scalar
        def _(act):
            def high(p, part, source, done, high_done):
                after(act, done, p + 1)
                act.activation(part.hi[:], source, ACT.Copy).then_inc(high_done, 1)

            def softmax(p):
                after(act, neg_done, p + 1)
                after(act, total_done, p)
                for j in range(2):
                    act.activation(prob[:, j, :], sim[:, j, :], ACT.Exp, bias=neg_max[:, j:j + 1],
                                   scale=WIN_SCALE, accum_out=own_sum[:, j:j + 1]).then_inc(exp_done, 1)
                act.activation(pad[:], neg_max[:], ACT.Exp).then_inc(pad_done, 1)

            def step(p, k, u, first, last):
                softmax(p)
                if not last:
                    high(p + 1, q_T, Q[:], q_done, q_high)
                    high(p + 1, k_T, K[:], k_done, k_high)
                high(p, probT, PB[:, :, 0:P], pT_done, pT_high)
                if not last:
                    high(p + 1, keys[1 - u], KEYS[:], keys_done, keys_high)
                if not first:
                    tail_xT_high(act, mem, tl, p - 1, XB[:])
                high(p, oT, OB[:], o_done, o_high)

            for n in (WQ, WK, WO):
                w.high(act, n)
            high(0, q_T, Q[:], q_done, q_high)
            high(0, k_T, K[:], k_done, k_high)
            high(0, keys[0], KEYS[:], keys_done, keys_high)
            over_pairs(act, step)
            tail_xT_high(act, mem, tl, NP - 1, XB[:])

        @block.vector
        def _(dve):
            def low(p, part, source, high_done, low_done):
                after(dve, high_done, p + 1)
                dve.tensor_tensor(part.lo[:], source, part.hi[:], ALU.subtract).then_inc(low_done, 1)

            def shift(p):
                after(dve, s_done, p + 1)
                after(dve, exp_done, 2 * p)
                dve.tensor_tensor(sim[:], S[:, :, 0:P], mem.causal.unsqueeze(1).to_broadcast([P, 2, P]), ALU.add)\
                    .then_inc(sim_done, 1)
                after(dve, sim_done, p + 1)
                dve.tensor_reduce(row_max[:], sim[:], AX.X, ALU.max).then_inc(max_done, 1)
                after(dve, max_done, p + 1)
                after(dve, pad_done, p)
                dve.tensor_scalar(neg_max[:], row_max[:], 0.0, -WIN_SCALE, ALU.max, ALU.mult)\
                    .then_inc(neg_done, 1)

            def normalize(p):
                after(dve, exp_done, 2 * p + 2)
                after(dve, pad_done, p + 1)
                dve.scalar_tensor_tensor(total[:], pad[:], float(P), own_sum[:], ALU.mult, ALU.add)\
                    .then_inc(total_done, 1)
                after(dve, total_done, p + 1)
                dve.reciprocal(inv[:], total[:]).then_inc(inv_done, 1)
                after(dve, inv_done, p + 1)
                for j in range(2):
                    dve.tensor_scalar(probn[:, j, :], prob[:, j, :], inv[:, j:j + 1], None, ALU.mult)\
                        .then_inc(probn_done, 1)

            def residual(p, u):
                after(dve, xb_ready, p + 1)
                tail_residual(dve, tl, p, Y[:], xb[u][:])
                tail_stats(dve, tl, p, tl.r)

            def step(p, k, u, first, last):
                shift(p)
                normalize(p)
                if not first:
                    residual(p - 1, 1 - u)
                if not last:
                    low(p + 1, q_T, Q[:], q_high, q_low)
                    low(p + 1, k_T, K[:], k_high, k_low)
                low(p, probT, PB[:, :, 0:P], pT_high, pT_low)
                if not first:
                    tail_apply(dve, tl, p - 1, tl.r, tl.x_stored)
                if not last:
                    low(p + 1, keys[1 - u], KEYS[:], keys_high, keys_low)
                low(p, oT, OB[:], o_high, o_low)
                if not first:
                    tail_xT_low(dve, mem, tl, p - 1, XB[:])

            low(0, q_T, Q[:], q_high, q_low)
            low(0, k_T, K[:], k_high, k_low)
            low(0, keys[0], KEYS[:], keys_high, keys_low)
            over_pairs(dve, step)
            residual(NP - 1, 1)
            tail_apply(dve, tl, NP - 1, tl.r, tl.x_stored)
            tail_xT_low(dve, mem, tl, NP - 1, XB[:])

        @block.tensor
        def _(pe):
            def proj_q(p):
                after(pe, q_low, p)
                project_T(pe, Q, w.cut[WQ], blocks_at(mem.xT, pair_tokens(p))).then_inc(q_done, 1)

            def proj_k(p):
                after(pe, k_low, p)
                project_T(pe, K, w.cut[WK], blocks_at(mem.xT, pair_tokens(p))).then_inc(k_done, 1)

            def proj_keys(p, u):
                after(pe, keys_low, p)
                wk = w.cut[WK]
                for j in range(2):
                    for db in range(DB):
                        tok = bass.ds(p * PT + j * P, P)
                        last = product(pe, KEYS[:, j, :], (mem.xT.hi[:, db, tok], mem.xT.lo[:, db, tok]),
                                       (wk.hi[:, db, :], wk.lo[:, db, :]), start=(db == 0), stop=(db == DB - 1))
                last.then_inc(keys_done, 1)

            def scores(p):
                after(pe, q_low, p + 1)
                after(pe, k_low, p + 1)
                after(pe, sim_done, p)
                for j in range(2):
                    for db in range(DB):
                        tok = slice(j * P, (j + 1) * P)
                        last = product(pe, S[:, j, 0:P], (q_T.hi[:, db, tok], q_T.lo[:, db, tok]),
                                       (k_T.hi[:, db, tok], k_T.lo[:, db, tok]),
                                       start=(db == 0), stop=(db == DB - 1))
                last.then_inc(s_done, 1)

            def step(p, k, u, first, last):
                scores(p)
                if not first:
                    after(pe, o_low, p)
                    project(pe, Y, oT, w.cut[WO]).then_inc(tl.y_done, 1)
                if not last:
                    proj_q(p + 1)
                    proj_k(p + 1)
                after(pe, probn_done, 2 * p + 2)
                after(pe, pT_low, p)
                for j in range(2):
                    last_p = pe.transpose(PB[:, j, 0:P], probn[:, j, :], mem.ident)
                last_p.then_inc(pT_done, 1)
                if not first:
                    tail_transpose(pe, mem, tl, p - 1, XB)
                if not last:
                    proj_keys(p + 1, 1 - u)
                after(pe, keys_low, p + 1)
                after(pe, pT_low, p + 1)
                for db in range(DB):
                    for j in range(2):
                        f = slice(db * P, (db + 1) * P)
                        last_o = product(pe, OB[:, db, j * P:(j + 1) * P],
                                         (keys[u].hi[:, j, f], keys[u].lo[:, j, f]),
                                         (probT.hi[:, j, :], probT.lo[:, j, :]))
                last_o.then_inc(o_done, 1)

            pe.wait_ge(w.lo_done, WQ + 1)
            proj_q(0)
            pe.wait_ge(w.lo_done, WK + 1)
            proj_k(0)
            proj_keys(0, 0)
            pe.wait_ge(w.lo_done, WO + 1)
            over_pairs(pe, step)
            pe.wait_ge(o_low, NP)
            project(pe, Y, oT, w.cut[WO]).then_inc(tl.y_done, 1)
            tail_transpose(pe, mem, tl, NP - 1, XB)



def by_block(ap):
    return ap.rearrange("(b p) n -> p b n", p=P)


def row(ap):
    return ap.rearrange("(a n) -> a n", a=1)


def constants():
    r, c = np.arange(P)[:, None], np.arange(P)[None, :]
    return {
        "ident": r == c,
        "ones": np.ones((P, P)),
        "earlier": r < c,
        "causal": np.where(c <= r, 0.0, MASKED),
        "head_mask": np.arange(P)[:, None] // DH == np.arange(HH)[None, :],
        "neg_half": np.full((P, 2), -0.5),
        "eps": np.full((P, 2), EPS),
        "zeros32": np.zeros((P, NB)),
        "rising8": np.broadcast_to(E - np.arange(E), (P, E)),
        "tile_start": np.broadcast_to(RT * np.arange(most_tiles(TOPK)), (P, most_tiles(TOPK))),
        "lower8": np.broadcast_to((np.arange(E)[None, :] < np.arange(E)[:, None]).reshape(1, E * E), (P, E * E)),
    }


def constant_columns():
    at, found = 0, {}
    for name, value in constants().items():
        found[name] = (at, value.shape[1])
        at += value.shape[1]
    return found, at


def open_residents(nc, ctx, mem, tag):
    mem.x = ctx.enter_context(nc.sbuf_tensor(f"{tag}_x", [P, NB, D], F32))
    mem.xT = Parts(*(ctx.enter_context(nc.sbuf_tensor(f"{tag}_xT_{n}", [P, DB, T], F16)) for n in ("hi", "lo")))


def decoder(nc, a, out):
    with ExitStack() as ctx:
        columns, n_columns = constant_columns()
        mem = Mem()
        mem.ident16 = ctx.enter_context(nc.sbuf_tensor("ident16", [P, P], F16))
        const = ctx.enter_context(nc.sbuf_tensor("const", [P, n_columns], F32))

        def constant(name):
            at, size = columns[name]
            return const[:, at:at + size]

        mem.ident, mem.ones, mem.earlier, mem.causal = (constant(n) for n in ("ident", "ones", "earlier", "causal"))
        mem.head_mask = constant("head_mask")
        mem.neg_half, mem.zeros32, mem.rising8 = constant("neg_half"), constant("zeros32"), constant("rising8")
        mem.eps, mem.tile_start = constant("eps"), constant("tile_start")
        mem.lower8 = constant("lower8").rearrange("p (e o) -> p e o", e=E)

        def load_constants(sp, loaded):
            sp.dma_start(const[:], a["const"]).then_inc(loaded, 16)
            sp.dma_start(mem.ident16[:], a["ident16"]).then_inc(loaded, 16)

        mem.load_constants = load_constants

        ctxT = by_block(a["ctxT"])
        x_kept = nc.dram_tensor("x_kept", (T, D), F32).ap().rearrange("(b p) d -> p b d", p=P)
        rows_in, rows_out = (nc.dram_tensor(n, (most_tiles(TOPK) * RT, D), F32).ap() for n in ("rows_in", "rows_out"))
        routed = [Routed(nc, ctx, f"L{n}", k, rows_in, rows_out) for n, k in enumerate((TOPK, 1))]

        def context_layer(tag):
            weights = (by_block(a[f"{tag}_xattn_{n}"]) for n in ("Wq", "Wk", "Wv", "Wo"))
            cross_attention(nc, mem, f"{tag}x", ctxT, *weights, a[f"{tag}_xattn_bq"],
                            a[f"{tag}_xattn_bk"], row(a[f"{tag}_xattn_bv"]), row(a[f"{tag}_xattn_bo"]))

        def expert_layer(n, w_up, w_down, width, gelu):
            sorted_experts(nc, mem, routed[n], f"L{n}", w_up.rearrange("e (b p) h -> p b e h", p=P),
                           w_down.rearrange("e (b p) d -> p b e d", p=P), width, gelu)

        with ExitStack() as residents:
            open_residents(nc, residents, mem, "L0")
            gated_attention(nc, mem, rows_in, a["x"].rearrange("b p d -> p b d"), by_block(a["xT"]),
                            *(by_block(a[f"L0_attn_{n}"]) for n in ("Wq", "Wk", "Wv", "Wo", "Wg")),
                            a["L0_attn_bg"],
                            a["diagonals"].rearrange("p (h t) -> p h t", h=HH),
                            a["head_rows"].rearrange("p (h t) -> p h t", h=H))
            context_layer("L0")
            router(nc, mem, "r0", by_block(a["L0_ffn_router_w"]), top_experts, routed[0], x_kept)
        expert_layer(0, a["L0_ffn_up_w"], a["L0_ffn_down_w"], 4 * D, ACT.Gelu_apprx_tanh)
        with ExitStack() as residents:
            open_residents(nc, residents, mem, "L1")
            norm_of_sorted(nc, mem, routed[0], "n0", x_kept, None)
            window_attention(nc, mem, by_block(a["L1_attn_w_qkv"]), by_block(a["L1_attn_w_out"]),
                             row(a["L1_attn_b_out"]))
            context_layer("L1")
            router(nc, mem, "r1", by_block(a["L1_ffn_Wg"]), selected_expert, routed[1], x_kept)
        expert_layer(1, a["L1_ffn_W1"], a["L1_ffn_W2"], 2 * D, ACT.Gelu)
        norm_of_sorted(nc, mem, routed[1], "n1", x_kept, out.rearrange("b p d -> p b d"))



def kernel(**inputs):
    import concourse.bacc as bacc
    from concourse.bass_utils import run_bass_kernel_spmd

    arrays = {k: np.asarray(v) for k, v in inputs.items()}
    arrays["xT"] = arrays["x"].reshape(T, D).T
    arrays["ctxT"] = arrays.pop("ctx_1024").reshape(T, D).T
    for name in ("L0_attn_Wq", "L0_attn_Wk", "L0_attn_Wv", "L0_attn_Wo", "L0_attn_Wg",
                 "L0_xattn_Wq", "L0_xattn_Wk", "L0_xattn_Wv", "L0_xattn_Wo"):
        arrays[name] = arrays[name].T
    for name in ("L0_xattn_bq", "L0_xattn_bk", "L1_xattn_bq", "L1_xattn_bk"):
        arrays[name] = arrays[name].reshape(DB, P).T
    gate_w, gate_b = np.zeros((D, GROWS), np.float32), np.zeros((GROWS, 1), np.float32)
    for at in (0, 32):
        gate_w[:, at:at + H] = arrays["L0_attn_Wg"]
        gate_b[at:at + H, 0] = arrays["L0_attn_bg"]
    arrays["L0_attn_Wg"], arrays["L0_attn_bg"] = gate_w, gate_b
    eye = np.eye(P, dtype=np.float32)
    arrays["const"] = np.concatenate(list(constants().values()), axis=1).astype(np.float32)
    arrays["diagonals"] = np.tile(eye, (1, HH))
    arrays["ident16"] = eye.astype(np.float16)
    head_rows = np.zeros((GROWS, H, P), np.float16)
    for at in (0, 32):
        head_rows[at + np.arange(H), np.arange(H), :] = 1
    arrays["head_rows"] = head_rows.reshape(GROWS, H * P)
    arrays = {k: np.ascontiguousarray(v) for k, v in arrays.items()}

    nc = bacc.Bacc("TRN2", target_bir_lowering=False, num_devices=1)
    aps = {k: nc.dram_tensor(f"in_{k}", v.shape, mybir.dt.from_np(v.dtype), kind="ExternalInput").ap()
           for k, v in arrays.items()}
    out = nc.dram_tensor("out", (NB, P, D), F32, kind="ExternalOutput").ap()
    decoder(nc, aps, out)
    r = run_bass_kernel_spmd(nc, [{f"in_{k}": v for k, v in arrays.items()}], core_ids=[0])
    return r.results[0]["out"]
```

```python
import numpy as np
import concourse.bass as bass
from concourse import mybir
from contextlib import ExitStack

F32 = mybir.dt.float32
F16 = mybir.dt.float16
U32 = mybir.dt.uint32
ALU = mybir.AluOpType
ACT = mybir.ActivationFunctionType
AX = mybir.AxisListType

P = 128
D = 256
DB = D // P
NB = 32
T = NB * P
NP = NB // 2
PT = 2 * P
H = 16
DH = D // H
HH = H // 2
E = 8
TOPK = 4
CAP = T // E
EPS = 1e-5
RT = 256
BANK = 512
HEAD_SCALE = float(DH) ** -0.5
WIN_SCALE = float(D) ** -0.5
MASKED = -3.0e38


def after(eng, sem, count):
    if isinstance(count, int) and count <= 0:
        return
    eng.wait_ge(sem, count)


def over_pairs(eng, step):
    step(0, 0, 0, True, False)
    with eng.Fori(0, (NP - 2) // 2) as i:
        step(2 * i + 1, i, 1, False, False)
        step(2 * i + 2, i + 1, 0, False, False)
    step(NP - 1, NP // 2 - 1, 1, False, True)


def over_pairs_deep(eng, step):
    step(0, 0, 0, 0, 2)
    step(1, 0, 1, 1, 2)
    with eng.Fori(0, (NP - 4) // 2) as i:
        step(2 * i + 2, i + 1, 0, 2, 2)
        step(2 * i + 3, i + 1, 1, 2, 2)
    step(NP - 2, NP // 2 - 1, 0, 2, 1)
    step(NP - 1, NP // 2 - 1, 1, 2, 0)


def pair_tokens(p):
    return bass.ds(p * PT, PT)


def pair_tiles(p):
    return bass.ds(p * 2, 2)


class Mem:
    pass


def open_stage(nc, ctx, tag):
    sems = []

    def sem(name):
        sems.append(nc.alloc_semaphore(f"{tag}_{name}"))
        return sems[-1]

    def clear():
        nc.clear_and_free_semaphores(sems)
        nc.all_engine_barrier()

    ctx.callback(clear)

    def sb(name, shape, dt=F32):
        return ctx.enter_context(nc.sbuf_tensor(f"{tag}_{name}", shape, dt))

    def ps(name, shape):
        size = int(np.prod(shape[1:]))
        whole = ctx.enter_context(nc.psum_tensor(f"{tag}_{name}", [P, -(-size // BANK) * BANK], F32))
        flat = whole[:, 0:size]
        if len(shape) == 2:
            return flat
        inner = {f"n{i}": n for i, n in enumerate(shape[1:])}
        return flat.rearrange(f"p ({' '.join(inner)}) -> p {' '.join(inner)}", **inner)

    return sem, sb, ps



class Tail:

    def __init__(self, sem, sb):
        self.r = sb("r", [P, 2, D])
        self.stats = sb("stats", [P, 2, 6])
        self.moments = sb("moments", [P, 2, 2])
        self.vare = sb("vare", [P, 2])
        self.rstd = sb("rstd", [P, 2])
        self.xn = sb("xn", [P, 2, D])
        self.y_done = sem("y_done")
        self.r_done = sem("r_done")
        self.moments_done = sem("moments_done")
        self.vare_done = sem("vare_done")
        self.rstd_done = sem("rstd_done")
        self.xn_done = sem("xn_done")
        self.x_stored = sem("x_stored")
        self.xT_done = sem("xT_done")
        self.xT_high = sem("xT_high")
        self.xT_low = sem("xT_low")


def tail_residual(dve, tl, p, y, xb):
    after(dve, tl.y_done, p + 1)
    dve.tensor_tensor(tl.r[:], y, xb, ALU.add).then_inc(tl.r_done, 1)
    after(dve, tl.r_done, p + 1)


def tail_stats(dve, tl, p, r):
    for j in range(2):
        dve.bn_stats(tl.stats[:, j, :], r[:, j, :])
    dve.drain()
    for j in range(2):
        dve.bn_aggr(tl.moments[:, j, :], tl.stats[:, j, :]).then_inc(tl.moments_done, 1)


def tail_rstd(pool, mem, tl, p):
    after(pool, tl.moments_done, 2 * p + 2)
    pool.tensor_tensor(tl.vare[:], tl.moments[:, :, 1], mem.eps, ALU.add)\
        .then_inc(tl.vare_done, 1)
    after(pool, tl.vare_done, p + 1)
    pool.tensor_tensor(tl.rstd[:], tl.vare[:], mem.neg_half, ALU.pow).then_inc(tl.rstd_done, 1)


def tail_apply(dve, tl, p, r, xn_used):
    after(dve, tl.rstd_done, p + 1)
    after(dve, tl.moments_done, 2 * p + 2)
    after(dve, xn_used, p)
    for j in range(2):
        dve.tensor_scalar(tl.xn[:, j, :], r[:, j, :], tl.moments[:, j, 0:1], tl.rstd[:, j:j + 1],
                          ALU.subtract, ALU.mult).then_inc(tl.xn_done, 1)


def tail_copy_x(act, mem, tl, p):
    after(act, tl.xn_done, 2 * p + 2)
    act.activation(mem.x[:, pair_tiles(p), :], tl.xn[:], ACT.Copy).then_inc(tl.x_stored, 1)


def tail_transpose(pe, mem, tl, p, bank):
    after(pe, tl.xn_done, 2 * p + 2)
    for db in range(DB):
        for j in range(2):
            last = pe.transpose(bank[:, db, j * P:(j + 1) * P], tl.xn[:, j, db * P:(db + 1) * P],
                                mem.ident)
    last.then_inc(tl.xT_done, 1)


def tail_xT_high(act, mem, tl, p, bank):
    after(act, tl.xT_done, p + 1)
    act.activation(mem.xT.hi[:, :, pair_tokens(p)], bank, ACT.Copy).then_inc(tl.xT_high, 1)


def tail_xT_low(dve, mem, tl, p, bank):
    after(dve, tl.xT_high, p + 1)
    dve.tensor_tensor(mem.xT.lo[:, :, pair_tokens(p)], bank, mem.xT.hi[:, :, pair_tokens(p)], ALU.subtract)\
        .then_inc(tl.xT_low, 1)



class Parts:
    def __init__(self, hi, lo):
        self.hi, self.lo = hi, lo


def parts(sb, name, shape):
    return Parts(sb(f"{name}_hi", shape, F16), sb(f"{name}_lo", shape, F16))


def product(pe, out, stationary, moving, start=True, stop=True):
    s_hi, s_lo = stationary
    m_hi, m_lo = moving
    pe.matmul(out, s_hi, m_hi, start=start, stop=False)
    pe.matmul(out, s_hi, m_lo, start=False, stop=False)
    return pe.matmul(out, s_lo, m_hi, start=False, stop=stop)


def project_T(pe, bank, w, moving):
    for m in range(DB):
        f = slice(m * P, (m + 1) * P)
        for db in range(DB):
            last = product(pe, bank[:, m, :], (w.hi[:, db, f], w.lo[:, db, f]), moving(db),
                           start=(db == 0), stop=(db == DB - 1))
    return last


def project(pe, bank, featT, w):
    for j in range(2):
        tok = slice(j * P, (j + 1) * P)
        for db in range(DB):
            last = product(pe, bank[:, j, :], (featT.hi[:, db, tok], featT.lo[:, db, tok]),
                           (w.hi[:, db, :], w.lo[:, db, :]), start=(db == 0), stop=(db == DB - 1))
    return last


def blocks_of(x):
    return lambda db: (x.hi[:, db, :], x.lo[:, db, :])


def blocks_at(x, tokens):
    return lambda db: (x.hi[:, db, tokens], x.lo[:, db, tokens])


class Weights:

    def __init__(self, sem, sb, shapes):
        self.raw = [sb(f"w{n}_raw", shape) for n, shape in enumerate(shapes)]
        self.cut = [parts(sb, f"w{n}", shape) for n, shape in enumerate(shapes)]
        self.loaded = [sem(f"w{n}_loaded") for n in range(len(shapes))]
        self.hi_done, self.lo_done = sem("w_hi_done"), sem("w_lo_done")

    def load(self, sp, n, source):
        sp.dma_start(self.raw[n][:], source).then_inc(self.loaded[n], 16)

    def high(self, act, n):
        act.wait_ge(self.loaded[n], 16)
        act.activation(self.cut[n].hi[:], self.raw[n][:], ACT.Copy).then_inc(self.hi_done, 1)

    def low(self, pool, n):
        pool.wait_ge(self.hi_done, n + 1)
        pool.tensor_tensor(self.cut[n].lo[:], self.raw[n][:], self.cut[n].hi[:], ALU.subtract)\
            .then_inc(self.lo_done, 1)


def mask_heads(eng, mem, masked, part, done):
    for h in range(HH):
        last = eng.tensor_scalar(masked[:, h, :, :], part[:], mem.head_mask[:, h:h + 1], 1.0, ALU.mult, ALU.mult)
    last.then_inc(done, 1)


def four_heads(masked, a, blk, tok):
    return masked[:, 4 * a:4 * a + 4, blk, tok]



GROWS = 96


def gated_attention(nc, mem, rows_in, x, xT0, wq, wk, wv, wo, wg, bg, diagonals_in, head_rows_in):
    with ExitStack() as ctx:
        sem, sb, ps = open_stage(nc, ctx, "ga")
        WQ, WK, WV, WG, WO = range(5)
        w = Weights(sem, sb, [[P, DB, D]] * 3 + [[P, DB, GROWS], [P, DB, D]])
        b_g, half_bg = sb("bg", [GROWS, 1]), sb("half_bg", [GROWS, 1])
        head_rows = sb("head_rows", [GROWS, H, P], F16)
        diagonals = sb("diagonals", [P, HH, P])
        xt = [sb(f"xt{u}", [P, DB, PT]) for u in range(2)]
        xc = [parts(sb, f"xc{u}", [P, DB, PT]) for u in range(2)]
        xb = [sb(f"xb{u}", [P, 2, D]) for u in range(2)]
        qexp, kexp = sb("qexp", [P, DB, PT]), sb("kexp", [P, DB, PT])
        qrelu, krelu = sb("qrelu", [P, DB, PT]), sb("krelu", [P, DB, PT])
        qfeat, kfeat = sb("qfeat", [P, DB, PT]), sb("kfeat", [P, DB, PT])
        q_cut = parts(sb, "q", [P, DB, PT])
        q_heads = [parts(sb, f"q_heads{u}", [P, HH, DB, PT]) for u in range(2)]
        k_T = [parts(sb, f"kT{u}", [P, DB, PT]) for u in range(2)]
        v_cut = [parts(sb, f"v{u}", [P, 2, D]) for u in range(2)]
        gtanh, gate = sb("gtanh", [GROWS, 2, P]), sb("gate", [GROWS, 2, P])
        gate_hi = sb("gate_hi", [GROWS, 2, P], F16)
        gate_parts = [sb(f"gate_parts{u}", [GROWS, 2, P], F16) for u in range(2)]
        decay = [sb(f"decay{n}", [P, HH, P]) for n in range(2)]
        att = [sb(f"att{n}", [P, HH, P]) for n in range(2)]
        att_cut = [parts(sb, f"attc{n}", [P, HH, P]) for n in range(2)]
        ctxn = sb("ctxn", [P, 2, D])
        ctxT = parts(sb, "ctxT", [P, DB, PT])
        zero = sb("zero", [P, D])
        tl = Tail(sem, sb)

        GB = ps("GB", [P, HH, P])
        S = ps("S", [P, HH, P])
        O = ps("O", [P, 512])
        MQ = ps("MQ", [P, 2, PT])
        MK = ps("MK", [P, 2, PT])
        MT = ps("MT", [P, 2, PT])

        consts_loaded = sem("consts_loaded")
        xt_loaded = [sem(f"xt_loaded{u}") for u in range(2)]
        xb_loaded = [sem(f"xb_loaded{u}") for u in range(2)]
        half_bg_done, x_high, x_low = sem("half_bg_done"), sem("x_high"), sem("x_low")
        q_done, k_done, v_done, g_done = (sem(n) for n in ("q_done", "k_done", "v_done", "g_done"))
        qexp_done, kexp_done, gtanh_done = sem("qexp_done"), sem("kexp_done"), sem("gtanh_done")
        qrelu_done, qfeat_done, q_high, q_low = (sem(n) for n in ("qrelu_done", "qfeat_done", "q_high", "q_low"))
        heads_high, heads_low = sem("heads_high"), sem("heads_low")
        krelu_done, kfeat_done, k_high, k_low = (sem(n) for n in ("krelu_done", "kfeat_done", "k_high", "k_low"))
        v_high, v_low = sem("v_high"), sem("v_low")
        gate_done, gate0_done, gate_cast, g_ready = (sem(n) for n in ("gate_done", "gate0_done", "gate_cast", "g_ready"))
        gb_done, decay_done = sem("gb_done"), sem("decay_done")
        s_done, att_done, att_high, att_low = (sem(n) for n in ("s_done", "att_done", "att_high", "att_low"))
        o_done, ctx_ready = sem("o_done"), sem("ctx_ready")
        ctxT_done, ctxT_high, ctxT_low = sem("ctxT_done"), sem("ctxT_high"), sem("ctxT_low")
        zeroed, cleared = sem("zeroed"), sem("cleared")
        consts_all = 16 * 5

        block = ctx.enter_context(nc.Block())

        @block.sync
        def _(sp):
            def load_xt(p, k, u):
                after(sp, x_low, p - 1)
                sp.dma_start(xt[u][:], xT0[:, :, pair_tokens(p)]).then_inc(xt_loaded[u], 16)

            def step(p, k, u, before, more):
                after(sp, tl.r_done, p - 1)
                sp.dma_start(xb[u][:], x[:, pair_tiles(p), :]).then_inc(xb_loaded[u], 16)
                if more >= 2:
                    load_xt(p + 2, k + 1, u)

            load_xt(0, 0, 0)
            w.load(sp, WQ, wq)
            w.load(sp, WK, wk)
            sp.dma_start(b_g[:], bg).then_inc(consts_loaded, 16)
            mem.load_constants(sp, consts_loaded)
            w.load(sp, WV, wv)
            w.load(sp, WG, wg)
            sp.dma_start(head_rows[:], head_rows_in).then_inc(consts_loaded, 16)
            sp.dma_start(diagonals[:], diagonals_in).then_inc(consts_loaded, 16)
            load_xt(1, 0, 1)
            w.load(sp, WO, wo)
            over_pairs_deep(sp, step)
            sp.wait_ge(cleared, 16)

        @block.gpsimd
        def _(pool):
            def x_lo(p, u):
                after(pool, x_high, p + 1)
                pool.tensor_tensor(xc[u].lo[:], xt[u][:], xc[u].hi[:], ALU.subtract).then_inc(x_low, 1)

            def q_lo(p, u):
                after(pool, q_high, p + 1)
                pool.tensor_tensor(q_cut.lo[:], qfeat[:], q_cut.hi[:], ALU.subtract).then_inc(q_low, 1)

            def split_q(p, u):
                pool.drain()
                mask_heads(pool, mem, q_heads[u].lo, q_cut.lo, heads_low)

            def k_lo(p, u):
                after(pool, k_high, p + 1)
                pool.tensor_tensor(k_T[u].lo[:], kfeat[:], k_T[u].hi[:], ALU.subtract).then_inc(k_low, 1)

            def att_lo(p, n):
                after(pool, att_high, 4 * p + n + 1)
                pool.tensor_tensor(att_cut[n % 2].lo[:], att[n % 2][:], att_cut[n % 2].hi[:], ALU.subtract)\
                    .then_inc(att_low, 1)

            def step(p, k, u, before, more):
                att_lo(p, 0)
                if more:
                    q_lo(p + 1, 1 - u)
                att_lo(p, 1)
                if more:
                    k_lo(p + 1, 1 - u)
                att_lo(p, 2)
                if more:
                    split_q(p + 1, 1 - u)
                if more >= 2:
                    x_lo(p + 2, u)
                if before:
                    tail_rstd(pool, mem, tl, p - 1)
                att_lo(p, 3)

            pool.memset(zero[:], 0.0).then_inc(zeroed, 1)
            w.low(pool, WQ)
            x_lo(0, 0)
            w.low(pool, WK)
            w.low(pool, WV)
            w.low(pool, WG)
            pool.wait_ge(consts_loaded, consts_all)
            q_lo(0, 0)
            split_q(0, 0)
            k_lo(0, 0)
            w.low(pool, WO)
            x_lo(1, 1)
            over_pairs_deep(pool, step)
            tail_rstd(pool, mem, tl, NP - 1)

        @block.scalar
        def _(act):
            def x_hi(p, k, u):
                act.wait_ge(xt_loaded[u], 16 * (k + 1))
                after(act, v_done, p - 1)
                act.activation(xc[u].hi[:], xt[u][:], ACT.Copy).then_inc(x_high, 1)

            def exp_q(p):
                after(act, q_done, p + 1)
                act.activation(qexp[:], MQ[:], ACT.Exp, scale=HEAD_SCALE).then_inc(qexp_done, 1)

            def exp_k(p):
                after(act, k_done, p + 1)
                act.activation(kexp[:], MK[:], ACT.Exp).then_inc(kexp_done, 1)

            def k_hi(p, u):
                after(act, kfeat_done, p + 1)
                act.activation(k_T[u].hi[:], kfeat[:], ACT.Copy).then_inc(k_high, 1)

            def v_hi(p, u):
                after(act, v_done, p + 1)
                act.activation(v_cut[u].hi[:], MQ[:], ACT.Copy).then_inc(v_high, 1)

            def tanh_g(p):
                after(act, g_done, p + 1)
                act.activation(gtanh[:].rearrange("g j t -> g (j t)"), MK[0:GROWS, 0, :], ACT.Tanh,
                               bias=half_bg[:], scale=0.5).then_inc(gtanh_done, 1)

            def att_hi(p, n):
                after(act, att_done, 4 * p + n + 1)
                act.activation(att_cut[n % 2].hi[:], att[n % 2][:], ACT.Copy).then_inc(att_high, 1)

            def copy_o(p, j):
                after(act, o_done, 2 * p + j + 1)
                act.activation(ctxn[:, j, :], O[:, 0:D], ACT.Copy).then_inc(ctx_ready, 1)

            def ctxT_hi(p):
                after(act, ctxT_done, p + 1)
                act.activation(ctxT.hi[:], MT[:], ACT.Copy).then_inc(ctxT_high, 1)

            def step(p, k, u, before, more):
                att_hi(p, 0)
                if before:
                    copy_o(p - 1, 1)
                if more:
                    exp_q(p + 1)
                if before >= 2:
                    tail_copy_x(act, mem, tl, p - 2)
                att_hi(p, 1)
                if more:
                    exp_k(p + 1)
                if before >= 2:
                    tail_xT_high(act, mem, tl, p - 2, MT[:])
                if before:
                    ctxT_hi(p - 1)
                if more:
                    k_hi(p + 1, 1 - u)
                    tanh_g(p + 1)
                copy_o(p, 0)
                att_hi(p, 2)
                if more:
                    v_hi(p + 1, 1 - u)
                att_hi(p, 3)
                if more >= 2:
                    x_hi(p + 2, k + 1, u)

            w.high(act, WQ)
            x_hi(0, 0, 0)
            w.high(act, WK)
            exp_q(0)
            act.wait_ge(zeroed, 1)
            act.dma_start(rows_in.rearrange("(n p) d -> p n d", p=P),
                          zero[:].unsqueeze(1).to_broadcast([P, rows_in.shape[0] // P, D])).then_inc(cleared, 16)
            w.high(act, WV)
            exp_k(0)
            k_hi(0, 0)
            w.high(act, WG)
            act.wait_ge(half_bg_done, 1)
            tanh_g(0)
            v_hi(0, 0)
            w.high(act, WO)
            x_hi(1, 0, 1)
            over_pairs_deep(act, step)
            copy_o(NP - 1, 1)
            tail_copy_x(act, mem, tl, NP - 2)
            tail_xT_high(act, mem, tl, NP - 2, MT[:])
            ctxT_hi(NP - 1)
            tail_copy_x(act, mem, tl, NP - 1)
            tail_xT_high(act, mem, tl, NP - 1, MT[:])

        @block.vector
        def _(dve):
            def feature_q(p, u):
                after(dve, qexp_done, p + 1)
                dve.tensor_scalar(qrelu[:], MQ[:], HEAD_SCALE, 0.0, ALU.mult, ALU.max)\
                    .then_inc(qrelu_done, 1)
                after(dve, qrelu_done, p + 1)
                after(dve, heads_low, p)
                dve.scalar_tensor_tensor(qfeat[:], qexp[:], 1.0, qrelu[:], ALU.min, ALU.add)\
                    .then_inc(qfeat_done, 1)
                after(dve, qfeat_done, p + 1)
                dve.tensor_copy(q_cut.hi[:], qfeat[:]).then_inc(q_high, 1)
                after(dve, q_high, p + 1)
                mask_heads(dve, mem, q_heads[u].hi, q_cut.hi, heads_high)

            def feature_k(p, u):
                after(dve, kexp_done, p + 1)
                dve.tensor_scalar(krelu[:], MK[:], 0.0, None, ALU.max).then_inc(krelu_done, 1)
                after(dve, krelu_done, p + 1)
                after(dve, k_low, p)
                dve.scalar_tensor_tensor(kfeat[:], kexp[:], 1.0, krelu[:], ALU.min, ALU.add)\
                    .then_inc(kfeat_done, 1)

            def v_lo(p, u):
                after(dve, v_high, p + 1)
                dve.tensor_tensor(v_cut[u].lo[:], MQ[:], v_cut[u].hi[:], ALU.subtract).then_inc(v_low, 1)

            def gates(p, u):
                after(dve, gtanh_done, p + 1)
                dve.tensor_scalar(gate[:], gtanh[:], 0.5, 0.5, ALU.mult, ALU.add).then_inc(gate_done, 1)
                after(dve, gate_done, p + 1)
                dve.memset(gate[:, :, 0:1], 0.0).then_inc(gate0_done, 1)
                after(dve, gate0_done, p + 1)
                dve.tensor_copy(gate_parts[u][0:32, :, :], gate[0:32, :, :])
                dve.tensor_copy(gate_hi[32:64, :, :], gate[32:64, :, :])
                dve.tensor_copy(gate_hi[64:96, :, :], gate[64:96, :, :]).then_inc(gate_cast, 1)
                after(dve, gate_cast, p + 1)
                for rows in (slice(32, 64), slice(64, 96)):
                    last = dve.tensor_tensor(gate_parts[u][rows, :, :], gate[rows, :, :], gate_hi[rows, :, :],
                                             ALU.subtract)
                last.then_inc(g_ready, 1)
                after(dve, g_ready, p + 1)

            def half(p, n):
                h = 4 * p + n
                after(dve, att_done, h - 1)
                after(dve, gb_done, h + 1)
                dve.tensor_tensor_scan(decay[n % 2][:].rearrange("p h t -> p (h t)"),
                                       GB[:].rearrange("p h t -> p (h t)"),
                                       diagonals[:].rearrange("p h t -> p (h t)"),
                                       0.0, ALU.mult, ALU.add).then_inc(decay_done, 1)
                after(dve, decay_done, h + 1)
                after(dve, s_done, h + 1)
                dve.tensor_tensor(att[n % 2][:], S[:], decay[n % 2][:], ALU.mult).then_inc(att_done, 1)

            def ctxT_lo(p):
                after(dve, ctxT_high, p + 1)
                dve.tensor_tensor(ctxT.lo[:], MT[:], ctxT.hi[:], ALU.subtract).then_inc(ctxT_low, 1)

            def residual(p, k, u):
                dve.wait_ge(xb_loaded[u], 16 * (k + 1))
                tail_residual(dve, tl, p, MT[:], xb[u][:])
                tail_stats(dve, tl, p, tl.r)

            def step(p, k, u, before, more):
                half(p, 0)
                if before >= 2:
                    tail_apply(dve, tl, p - 2, tl.r, tl.x_stored)
                half(p, 1)
                if more:
                    feature_q(p + 1, 1 - u)
                if before >= 2:
                    tail_xT_low(dve, mem, tl, p - 2, MT[:])
                if more:
                    feature_k(p + 1, 1 - u)
                half(p, 2)
                half(p, 3)
                if before:
                    ctxT_lo(p - 1)
                if more:
                    gates(p + 1, 1 - u)
                    v_lo(p + 1, 1 - u)
                if before:
                    residual(p - 1, k + u - 1, 1 - u)

            dve.wait_ge(consts_loaded, consts_all)
            dve.tensor_scalar(half_bg[:], b_g[:], 0.5, None, ALU.mult).then_inc(half_bg_done, 1)
            feature_q(0, 0)
            feature_k(0, 0)
            gates(0, 0)
            v_lo(0, 0)
            over_pairs_deep(dve, step)
            tail_apply(dve, tl, NP - 2, tl.r, tl.x_stored)
            tail_xT_low(dve, mem, tl, NP - 2, MT[:])
            ctxT_lo(NP - 1)
            residual(NP - 1, NP // 2 - 1, 1)
            tail_apply(dve, tl, NP - 1, tl.r, tl.x_stored)
            tail_xT_low(dve, mem, tl, NP - 1, MT[:])

        @block.tensor
        def _(pe):
            def proj_q(p, u):
                after(pe, x_high, p + 1)
                after(pe, x_low, p + 1)
                after(pe, v_low, p)
                project_T(pe, MQ, w.cut[WQ], blocks_of(xc[u])).then_inc(q_done, 1)

            def proj_k(p, u):
                after(pe, gtanh_done, p)
                project_T(pe, MK, w.cut[WK], blocks_of(xc[u])).then_inc(k_done, 1)

            def proj_v(p, u):
                after(pe, qfeat_done, p + 1)
                project(pe, MQ, xc[u], w.cut[WV]).then_inc(v_done, 1)

            def proj_g(p, u):
                after(pe, kfeat_done, p + 1)
                for db in range(DB):
                    wg_ = w.cut[WG]
                    last = product(pe, MK[0:GROWS, 0, :], (wg_.hi[:, db, :], wg_.lo[:, db, :]),
                                   (xc[u].hi[:, db, :], xc[u].lo[:, db, :]), start=(db == 0), stop=(db == DB - 1))
                last.then_inc(g_done, 1)

            def spread_gates(p, n, u):
                h = 4 * p + n
                after(pe, g_ready, p + 1)
                after(pe, decay_done, h)
                for s in range(HH):
                    last = pe.matmul(GB[:, s, :], head_rows[:, HH * (n % 2) + s, :],
                                     gate_parts[u][:, n // 2, :], start=True, stop=True)
                last.then_inc(gb_done, 1)

            def scores(p, n, u):
                h = 4 * p + n
                blk, tok = n % 2, slice((n // 2) * P, (n // 2 + 1) * P)
                after(pe, heads_high, p + 1)
                after(pe, heads_low, p + 1)
                after(pe, k_low, p + 1)
                after(pe, att_done, h)
                for a in range(2):
                    last = product(pe, S[:, 4 * a:4 * a + 4, :],
                                   (k_T[u].hi[:, blk, tok], k_T[u].lo[:, blk, tok]),
                                   (four_heads(q_heads[u].hi, a, blk, tok), four_heads(q_heads[u].lo, a, blk, tok)))
                last.then_inc(s_done, 1)

            def values(p, n, u):
                h = 4 * p + n
                blk, j = n % 2, n // 2
                after(pe, att_high, h + 1)
                after(pe, att_low, h + 1)
                after(pe, v_low, p + 1)
                after(pe, ctx_ready, 2 * p + j)
                cut, v = att_cut[n % 2], v_cut[u]
                for s in range(HH):
                    f = slice((HH * blk + s) * DH, (HH * blk + s + 1) * DH)
                    last = product(pe, O[:, f], (cut.hi[:, s, :], cut.lo[:, s, :]), (v.hi[:, j, f], v.lo[:, j, f]))
                if blk:
                    last.then_inc(o_done, 1)

            def transpose_ctx(p):
                after(pe, ctx_ready, 2 * p + 2)
                after(pe, tl.xT_low, p)
                for db in range(DB):
                    for j in range(2):
                        last = pe.transpose(MT[:, db, j * P:(j + 1) * P], ctxn[:, j, db * P:(db + 1) * P],
                                            mem.ident)
                last.then_inc(ctxT_done, 1)

            def output(p):
                after(pe, ctxT_low, p + 1)
                project(pe, MT, ctxT, w.cut[WO]).then_inc(tl.y_done, 1)

            def step(p, k, u, before, more):
                spread_gates(p, 0, u)
                scores(p, 0, u)
                spread_gates(p, 1, u)
                if more:
                    proj_q(p + 1, 1 - u)
                if before:
                    values(p - 1, 3, 1 - u)
                scores(p, 1, u)
                if before >= 2:
                    tail_transpose(pe, mem, tl, p - 2, MT)
                values(p, 0, u)
                spread_gates(p, 2, u)
                if more:
                    proj_k(p + 1, 1 - u)
                scores(p, 2, u)
                if before:
                    transpose_ctx(p - 1)
                values(p, 1, u)
                if more:
                    proj_g(p + 1, 1 - u)
                spread_gates(p, 3, u)
                scores(p, 3, u)
                values(p, 2, u)
                if more:
                    proj_v(p + 1, 1 - u)
                if before:
                    output(p - 1)

            pe.wait_ge(consts_loaded, consts_all)
            pe.wait_ge(w.lo_done, WQ + 1)
            proj_q(0, 0)
            pe.wait_ge(w.lo_done, WK + 1)
            proj_k(0, 0)
            pe.wait_ge(w.lo_done, WG + 1)
            proj_g(0, 0)
            proj_v(0, 0)
            pe.wait_ge(w.lo_done, WO + 1)
            over_pairs_deep(pe, step)
            values(NP - 1, 3, 1)
            tail_transpose(pe, mem, tl, NP - 2, MT)
            transpose_ctx(NP - 1)
            output(NP - 1)
            tail_transpose(pe, mem, tl, NP - 1, MT)



def cross_attention(nc, mem, tag, ctxT_in, wq, wk, wv, wo, bq, bk, bv, bo):
    with ExitStack() as ctx:
        sem, sb, ps = open_stage(nc, ctx, tag)
        WQ, WK, WV, WO = range(4)
        w = Weights(sem, sb, [[P, DB, D]] * 4)
        b_q, b_k = sb("bq", [P, DB]), sb("bk", [P, DB])
        b_v, b_o = sb("bv", [P, D]), sb("bo", [P, D])
        ct = [sb(f"ct{u}", [P, DB, PT]) for u in range(2)]
        cc = [parts(sb, f"cc{u}", [P, DB, PT]) for u in range(2)]
        xb = [sb(f"xb{u}", [P, 2, D]) for u in range(2)]
        q32 = sb("q32", [P, DB, PT])
        q_cut = parts(sb, "q", [P, DB, PT])
        q_heads = [parts(sb, f"q_heads{u}", [P, HH, DB, PT]) for u in range(2)]
        k_T = [parts(sb, f"kT{u}", [P, DB, PT]) for u in range(2)]
        v32 = sb("v32", [P, 2, H, DH])
        v_cut = [parts(sb, f"v{u}", [P, 2, H, DH + 1]) for u in range(2)]
        neg_max = [sb(f"neg_max{n}", [P, HH], F16) for n in range(2)]
        prob = [sb(f"prob{n}", [P, HH, P]) for n in range(2)]
        prob_cut = [parts(sb, f"probc{n}", [P, HH, P]) for n in range(2)]
        inv = sb("inv", [P, 2, H])
        ctxn = sb("ctxn", [P, 2, D])
        ctxT = parts(sb, "ctxT", [P, DB, PT])
        tl = Tail(sem, sb)

        A = ps("A", [P, HH // 2, P])
        S = [ps(f"S{n}", [P, HH, P]) for n in range(2)]
        O = ps("O", [P, H, 32])
        MP = ps("MP", [P, 2, PT])
        MT = ps("MT", [P, 2, PT])

        bias_loaded = sem("bias_loaded")
        ct_loaded = [sem(f"ct_loaded{u}") for u in range(2)]
        ct_high, ct_low, ones_ready, xb_ready = (sem(n) for n in ("ct_high", "ct_low", "ones_ready", "xb_ready"))
        q_done, k_done, v_done = (sem(n) for n in ("q_done", "k_done", "v_done"))
        q32_done, q_high, q_low, heads_high, heads_low = (
            sem(n) for n in ("q32_done", "q_high", "q_low", "heads_high", "heads_low"))
        k_high, k_low, v32_done, v_high, v_low = (sem(n) for n in ("k_high", "k_low", "v32_done", "v_high", "v_low"))
        a_done, max_done, s_done, exp_done = (sem(n) for n in ("a_done", "max_done", "s_done", "exp_done"))
        exp_high, low_even, low_odd = sem("exp_high"), sem("low_even"), sem("low_odd")
        o_done, inv_done, ctx_ready = sem("o_done"), sem("inv_done"), sem("ctx_ready")
        ctxT_done, ctxT_high, ctxT_low = sem("ctxT_done"), sem("ctxT_high"), sem("ctxT_low")

        block = ctx.enter_context(nc.Block())

        @block.sync
        def _(sp):
            def load(p, k, u):
                after(sp, ct_low, p - 1)
                sp.dma_start(ct[u][:], ctxT_in[:, :, pair_tokens(p)]).then_inc(ct_loaded[u], 16)

            def step(p, k, u, before, more):
                if more >= 2:
                    load(p + 2, k + 1, u)

            for dst, src in ((b_q, bq), (b_k, bk), (b_v, bv.to_broadcast([P, D])), (b_o, bo.to_broadcast([P, D]))):
                sp.dma_start(dst[:], src).then_inc(bias_loaded, 16)
            w.load(sp, WQ, wq)
            w.load(sp, WK, wk)
            load(0, 0, 0)
            w.load(sp, WV, wv)
            w.load(sp, WO, wo)
            load(1, 0, 1)
            over_pairs_deep(sp, step)

        def prob_lo(eng, p, n, done):
            after(eng, exp_high, 4 * p + n + 1)
            eng.tensor_tensor(prob_cut[n % 2].lo[:], prob[n % 2][:], prob_cut[n % 2].hi[:], ALU.subtract)\
                .then_inc(done, 1)

        @block.gpsimd
        def _(pool):
            def add_bias(p, u):
                pool.tensor_tensor(xb[u][:], mem.x[:, pair_tiles(p), :],
                                   b_o[:].unsqueeze(1).to_broadcast([P, 2, D]), ALU.add).then_inc(xb_ready, 1)

            def ct_lo(p, u):
                after(pool, ct_high, p + 1)
                pool.tensor_tensor(cc[u].lo[:], ct[u][:], cc[u].hi[:], ALU.subtract).then_inc(ct_low, 1)

            def q_lo(p, u):
                after(pool, q_high, p + 1)
                pool.tensor_tensor(q_cut.lo[:], q32[:], q_cut.hi[:], ALU.subtract).then_inc(q_low, 1)

            def split_q(p, u):
                pool.drain()
                mask_heads(pool, mem, q_heads[u].lo, q_cut.lo, heads_low)

            def v_lo(p, u):
                after(pool, v_high, p + 1)
                pool.tensor_tensor(v_cut[u].lo[:, :, :, 0:DH], v32[:], v_cut[u].hi[:, :, :, 0:DH], ALU.subtract)\
                    .then_inc(v_low, 1)

            def step(p, k, u, before, more):
                if more:
                    q_lo(p + 1, 1 - u)
                prob_lo(pool, p, 1, low_odd)
                if more:
                    split_q(p + 1, 1 - u)
                if before:
                    tail_rstd(pool, mem, tl, p - 1)
                prob_lo(pool, p, 3, low_odd)
                if more:
                    v_lo(p + 1, 1 - u)
                    after(pool, tl.r_done, p)
                    add_bias(p + 1, 1 - u)
                if more >= 2:
                    ct_lo(p + 2, u)

            for u in range(2):
                pool.memset(v_cut[u].hi[:, :, :, DH:DH + 1], 1.0).then_inc(ones_ready, 1)
                pool.memset(v_cut[u].lo[:, :, :, DH:DH + 1], 0.0).then_inc(ones_ready, 1)
            w.low(pool, WQ)
            w.low(pool, WK)
            ct_lo(0, 0)
            w.low(pool, WV)
            q_lo(0, 0)
            split_q(0, 0)
            v_lo(0, 0)
            w.low(pool, WO)
            ct_lo(1, 1)
            pool.wait_ge(bias_loaded, 16 * 4)
            add_bias(0, 0)
            over_pairs_deep(pool, step)
            tail_rstd(pool, mem, tl, NP - 1)

        @block.scalar
        def _(act):
            def ct_hi(p, k, u):
                act.wait_ge(ct_loaded[u], 16 * (k + 1))
                after(act, v_done, p - 1)
                act.activation(cc[u].hi[:], ct[u][:], ACT.Copy).then_inc(ct_high, 1)

            def copy_q(p):
                after(act, q_done, p + 1)
                after(act, heads_low, p)
                for m in range(DB):
                    act.activation(q32[:, m, :], MP[:, m, :], ACT.Identity, bias=b_q[:, m:m + 1])\
                        .then_inc(q32_done, 1)

            def k_hi(p, u):
                after(act, k_done, p + 1)
                for m in range(DB):
                    act.activation(k_T[u].hi[:, m, :], MP[:, m, :], ACT.Identity, bias=b_k[:, m:m + 1])\
                        .then_inc(k_high, 1)

            def v_hi(p, u):
                after(act, v32_done, p + 1)
                act.activation(v_cut[u].hi[:, :, :, 0:DH], v32[:], ACT.Copy).then_inc(v_high, 1)

            def exp(p, n):
                after(act, s_done, 4 * p + n + 1)
                act.activation(prob[n % 2][:], S[n % 2][:], ACT.Exp, scale=HEAD_SCALE).then_inc(exp_done, 1)
                act.activation(prob_cut[n % 2].hi[:], S[n % 2][:], ACT.Exp, scale=HEAD_SCALE)\
                    .then_inc(exp_high, 1)

            def ctxT_hi(p):
                after(act, ctxT_done, p + 1)
                act.activation(ctxT.hi[:], MT[:], ACT.Copy).then_inc(ctxT_high, 1)

            def step(p, k, u, before, more):
                if more:
                    copy_q(p + 1)
                exp(p, 0)
                if before >= 2:
                    tail_copy_x(act, mem, tl, p - 2)
                    tail_xT_high(act, mem, tl, p - 2, MT[:])
                exp(p, 1)
                if more:
                    k_hi(p + 1, 1 - u)
                if before:
                    ctxT_hi(p - 1)
                exp(p, 2)
                exp(p, 3)
                if more:
                    v_hi(p + 1, 1 - u)
                if more >= 2:
                    ct_hi(p + 2, k + 1, u)

            w.high(act, WQ)
            w.high(act, WK)
            ct_hi(0, 0, 0)
            act.wait_ge(bias_loaded, 16 * 4)
            copy_q(0)
            w.high(act, WV)
            k_hi(0, 0)
            v_hi(0, 0)
            w.high(act, WO)
            ct_hi(1, 0, 1)
            over_pairs_deep(act, step)
            tail_copy_x(act, mem, tl, NP - 2)
            tail_xT_high(act, mem, tl, NP - 2, MT[:])
            ctxT_hi(NP - 1)
            tail_copy_x(act, mem, tl, NP - 1)
            tail_xT_high(act, mem, tl, NP - 1, MT[:])

        @block.vector
        def _(dve):
            def maximum(p, n):
                for a in range(2):
                    after(dve, a_done, 2 * (4 * p + n) + a + 1)
                    dve.tensor_reduce(neg_max[n % 2][:, 4 * a:4 * a + 4], A[:], AX.X, ALU.max, negate=True)\
                        .then_inc(max_done, 1)

            def q_hi(p, u):
                after(dve, q32_done, 2 * p + 2)
                dve.tensor_copy(q_cut.hi[:], q32[:]).then_inc(q_high, 1)
                after(dve, q_high, p + 1)
                mask_heads(dve, mem, q_heads[u].hi, q_cut.hi, heads_high)

            def k_lo(p, u):
                after(dve, k_high, 2 * p + 2)
                for m in range(DB):
                    dve.scalar_tensor_tensor(k_T[u].lo[:, m, :], MP[:, m, :], b_k[:, m:m + 1],
                                             k_T[u].hi[:, m, :], ALU.add, ALU.subtract).then_inc(k_low, 1)

            def add_bv(p):
                after(dve, v_done, p + 1)
                after(dve, v_low, p)
                dve.tensor_tensor(v32[:], MP[:].rearrange("p j (h d) -> p j h d", h=H),
                                  b_v[:].rearrange("p (h d) -> p h d", h=H).unsqueeze(1)
                                  .to_broadcast([P, 2, H, DH]), ALU.add).then_inc(v32_done, 1)

            def normalize(p, j):
                after(dve, o_done, 2 * p + j + 1)
                dve.reciprocal(inv[:, j, :], O[:, :, DH]).then_inc(inv_done, 1)
                after(dve, inv_done, 2 * p + j + 1)
                dve.tensor_tensor(ctxn[:, j, :].rearrange("p (h d) -> p h d", h=H), O[:, :, 0:DH],
                                  inv[:, j, :].unsqueeze(2).to_broadcast([P, H, DH]), ALU.mult)\
                    .then_inc(ctx_ready, 1)

            def ctxT_lo(p):
                after(dve, ctxT_high, p + 1)
                dve.tensor_tensor(ctxT.lo[:], MT[:], ctxT.hi[:], ALU.subtract).then_inc(ctxT_low, 1)

            def residual(p, u):
                after(dve, xb_ready, p + 1)
                tail_residual(dve, tl, p, MT[:], xb[u][:])
                tail_stats(dve, tl, p, tl.r)

            def step(p, k, u, before, more):
                maximum(p, 0)
                if before >= 2:
                    tail_apply(dve, tl, p - 2, tl.r, tl.x_stored)
                if more:
                    q_hi(p + 1, 1 - u)
                maximum(p, 1)
                if before:
                    normalize(p - 1, 1)
                prob_lo(dve, p, 0, low_even)
                if before >= 2:
                    tail_xT_low(dve, mem, tl, p - 2, MT[:])
                maximum(p, 2)
                if more:
                    k_lo(p + 1, 1 - u)
                if before:
                    ctxT_lo(p - 1)
                normalize(p, 0)
                maximum(p, 3)
                prob_lo(dve, p, 2, low_even)
                if more:
                    add_bv(p + 1)
                if before:
                    residual(p - 1, 1 - u)

            dve.wait_ge(bias_loaded, 16 * 4)
            q_hi(0, 0)
            k_lo(0, 0)
            add_bv(0)
            over_pairs_deep(dve, step)
            tail_apply(dve, tl, NP - 2, tl.r, tl.x_stored)
            normalize(NP - 1, 1)
            tail_xT_low(dve, mem, tl, NP - 2, MT[:])
            ctxT_lo(NP - 1)
            residual(NP - 1, 1)
            tail_apply(dve, tl, NP - 1, tl.r, tl.x_stored)
            tail_xT_low(dve, mem, tl, NP - 1, MT[:])

        @block.tensor
        def _(pe):
            def proj_q(p):
                after(pe, v32_done, p)
                project_T(pe, MP, w.cut[WQ], blocks_at(mem.xT, pair_tokens(p))).then_inc(q_done, 1)

            def proj_k(p, u):
                after(pe, ct_low, p + 1)
                after(pe, q32_done, 2 * p + 2)
                project_T(pe, MP, w.cut[WK], blocks_of(cc[u])).then_inc(k_done, 1)

            def proj_v(p, u):
                after(pe, k_low, 2 * p + 2)
                project(pe, MP, cc[u], w.cut[WV]).then_inc(v_done, 1)

            def first_scores(p, n, u, a):
                blk, tok = n % 2, slice((n // 2) * P, (n // 2 + 1) * P)
                after(pe, heads_high, p + 1)
                after(pe, k_high, 2 * p + 2)
                after(pe, max_done, 2 * (4 * p + n) + a)
                for s in range(4):
                    last = pe.matmul(A[:, s, :], q_heads[u].hi[:, 4 * a + s, blk, tok], k_T[u].hi[:, blk, tok],
                                     start=True, stop=True)
                last.then_inc(a_done, 1)

            def scores(p, n, u):
                blk, tok = n % 2, slice((n // 2) * P, (n // 2 + 1) * P)
                after(pe, heads_low, p + 1)
                after(pe, k_low, 2 * p + 2)
                after(pe, exp_high, 4 * p + n - 1)
                for a in range(2):
                    product(pe, S[n % 2][:, 4 * a:4 * a + 4, :],
                            (k_T[u].hi[:, blk, tok], k_T[u].lo[:, blk, tok]),
                            (four_heads(q_heads[u].hi, a, blk, tok), four_heads(q_heads[u].lo, a, blk, tok)))

            def subtract_maximum(p, n):
                after(pe, max_done, 2 * (4 * p + n) + 2)
                for s in range(HH):
                    last = pe.matmul(S[n % 2][:, s, :], neg_max[n % 2][:, s:s + 1].to_broadcast([P, P]),
                                     mem.ident16[:], start=False, stop=True, skip_group_check=True)
                last.then_inc(s_done, 1)

            def values(p, n, u):
                blk, j = n % 2, n // 2
                after(pe, low_odd if blk else low_even, 2 * p + j + 1)
                after(pe, v_low, p + 1)
                after(pe, ctx_ready, 2 * p + j)
                cut, v = prob_cut[n % 2], v_cut[u]
                for s in range(HH):
                    h = HH * blk + s
                    last = product(pe, O[:, h, 0:DH + 1], (cut.hi[:, s, :], cut.lo[:, s, :]),
                                   (v.hi[:, j, h, :], v.lo[:, j, h, :]))
                if blk:
                    last.then_inc(o_done, 1)

            def transpose_ctx(p):
                after(pe, ctx_ready, 2 * p + 2)
                after(pe, tl.xT_low, p)
                for db in range(DB):
                    for j in range(2):
                        last = pe.transpose(MT[:, db, j * P:(j + 1) * P], ctxn[:, j, db * P:(db + 1) * P],
                                            mem.ident)
                last.then_inc(ctxT_done, 1)

            def output(p):
                after(pe, ctxT_low, p + 1)
                project(pe, MT, ctxT, w.cut[WO]).then_inc(tl.y_done, 1)

            def both_scores(p, n, u):
                first_scores(p, n, u, 0)
                scores(p, n, u)
                first_scores(p, n, u, 1)

            def step(p, k, u, before, more):
                both_scores(p, 0, u)
                if more:
                    proj_q(p + 1)
                subtract_maximum(p, 0)
                if before:
                    values(p - 1, 3, 1 - u)
                if before >= 2:
                    tail_transpose(pe, mem, tl, p - 2, MT)
                both_scores(p, 1, u)
                if more:
                    proj_k(p + 1, 1 - u)
                subtract_maximum(p, 1)
                both_scores(p, 2, u)
                values(p, 0, u)
                if before:
                    transpose_ctx(p - 1)
                subtract_maximum(p, 2)
                values(p, 1, u)
                both_scores(p, 3, u)
                if more:
                    proj_v(p + 1, 1 - u)
                if before:
                    output(p - 1)
                subtract_maximum(p, 3)
                values(p, 2, u)

            pe.wait_ge(ones_ready, 4)
            pe.wait_ge(w.lo_done, WQ + 1)
            proj_q(0)
            pe.wait_ge(w.lo_done, WK + 1)
            proj_k(0, 0)
            pe.wait_ge(w.lo_done, WV + 1)
            proj_v(0, 0)
            pe.wait_ge(w.lo_done, WO + 1)
            over_pairs_deep(pe, step)
            values(NP - 1, 3, 1)
            tail_transpose(pe, mem, tl, NP - 2, MT)
            transpose_ctx(NP - 1)
            output(NP - 1)
            tail_transpose(pe, mem, tl, NP - 1, MT)



def most_tiles(k):
    return (k * T + E * (RT - 1)) // RT


class Routed:

    def __init__(self, nc, ctx, tag, k, rows_in, rows_out):
        def sb(name, shape, dt):
            return ctx.enter_context(nc.sbuf_tensor(f"{tag}_{name}", shape, dt))

        self.k, self.tiles = k, most_tiles(k)
        self.slot = sb("slot", [P, k, NB], U32)
        self.gate = sb("gate", [P, k, NB], F32)
        self.expert = sb("expert", [P, self.tiles], U32)
        self.rows_in, self.rows_out = rows_in, rows_out


class SlotNumbers:

    def __init__(self, sb, routed):
        self.routed = routed
        self.in_tile, self.slot_of, self.own = (sb(n, [P, NB, E]) for n in ("tile_rows", "slot_of", "own_slot"))
        self.rows, self.start, self.end = (sb(n, [P, E]) for n in ("rows", "start", "end"))
        self.padded, self.slot = sb("padded", [P, E], U32), sb("slot_f", [P, NB])
        self.passed, self.expert = sb("passed", [P, routed.tiles, E]), sb("expert_f", [P, routed.tiles])

    def starts(self, dve, link, mem, BEFORE, TILES):
        tiles = self.routed.tiles
        link(dve.tensor_copy(self.in_tile[:], TILES[:]))
        for e in range(E):
            last = dve.tensor_tensor_scan(self.slot_of[:, :, e], self.in_tile[:, :, e], mem.zeros32, 0.0,
                                          ALU.add, ALU.add)
        link(last)
        link(dve.tensor_scalar(self.rows[:], self.slot_of[:, NB - 1, :], float(RT - 1), None, ALU.add))
        link(dve.tensor_copy(self.padded[:], self.rows[:]))
        link(dve.tensor_scalar(self.padded[:], self.padded[:], ~(RT - 1) & 0xffffffff, None, ALU.bitwise_and))
        link(dve.tensor_copy(self.rows[:], self.padded[:]))
        link(dve.tensor_tensor_scan(self.end[:], self.rows[:], mem.zeros32[:, 0:E], 0.0, ALU.add, ALU.add))
        link(dve.tensor_tensor(self.start[:], self.end[:], self.rows[:], ALU.subtract))
        link(dve.tensor_tensor(self.slot_of[:], self.slot_of[:], self.in_tile[:], ALU.subtract))
        link(dve.tensor_tensor(self.slot_of[:], self.slot_of[:], BEFORE[:], ALU.add))
        link(dve.tensor_tensor(self.slot_of[:], self.slot_of[:],
                               self.start[:].unsqueeze(1).to_broadcast([P, NB, E]), ALU.add))
        link(dve.tensor_tensor(self.passed[:], mem.tile_start[:, 0:tiles].unsqueeze(2).to_broadcast([P, tiles, E]),
                               self.end[:].unsqueeze(1).to_broadcast([P, tiles, E]), ALU.is_ge))
        link(dve.tensor_reduce(self.expert[:], self.passed[:], AX.X, ALU.add))
        link(dve.tensor_scalar(self.routed.expert[:], self.expert[:], float(E - 1), None, ALU.min))

    def slots(self, dve, link, marks, values, k, slot_ready):
        link(dve.tensor_tensor(self.own[:], values, marks, ALU.mult))
        link(dve.tensor_reduce(self.routed.gate[:, k, :], self.own[:], AX.X, ALU.add))
        link(dve.tensor_tensor(self.own[:], self.slot_of[:], marks, ALU.mult))
        link(dve.tensor_reduce(self.slot[:], self.own[:], AX.X, ALU.add))
        dve.tensor_copy(self.routed.slot[:, k, :], self.slot[:]).then_inc(slot_ready, 1)
        dve.wait_ge(slot_ready, k + 1)


def router(nc, mem, tag, w_router, decide, routed, x_kept):
    with ExitStack() as ctx:
        sem, sb, ps = open_stage(nc, ctx, tag)
        CHUNK, NCH = 4 * P, T // (4 * P)
        w = Weights(sem, sb, [[P, DB, E]])
        logitsT = [sb(f"logitsT{a}", [E, CHUNK]) for a in range(2)]
        LT = [ps(f"LT{a}", [P, CHUNK]) for a in range(2)]
        L = ps("L", [P, NB, E])
        lt_done, lt_ready, l_done = sem("lt_done"), sem("lt_ready"), sem("l_done")
        slot_ready, sent, kept = sem("slot_ready"), sem("sent"), sem("kept")
        rest = decide(mem, sem, sb, ps, L, l_done, routed, slot_ready)
        block = ctx.enter_context(nc.Block())

        @block.sync
        def _(sp):
            w.load(sp, 0, w_router)
            sp.dma_start(x_kept, mem.x[:]).then_inc(kept, 16)
            sp.wait_ge(kept, 16)

        @block.gpsimd
        def _(pool):
            w.low(pool, 0)
            for k in range(routed.k):
                pool.wait_ge(slot_ready, k + 1)
                for b in range(NB):
                    pool.indirect_dma_start(routed.rows_in,
                                            bass.IndirectOffsetOnAxis(routed.slot[:, k, b:b + 1], 0),
                                            mem.x[:, b, :], None).then_inc(sent, 16)
            pool.wait_ge(sent, 16 * NB * routed.k)

        @block.tensor
        def _(pe):
            pe.wait_ge(w.lo_done, 1)
            for c in range(NCH + 1):
                if c < NCH:
                    after(pe, lt_ready, c - 1)
                    for db in range(DB):
                        x = blocks_at(mem.xT, slice(c * CHUNK, (c + 1) * CHUNK))(db)
                        last = product(pe, LT[c % 2][0:E, :], (w.cut[0].hi[:, db, :], w.cut[0].lo[:, db, :]), x,
                                       start=(db == 0), stop=(db == DB - 1))
                    last.then_inc(lt_done, 1)
                if c:
                    pe.wait_ge(lt_ready, c)
                    for j in range(4):
                        last = pe.transpose(L[:, 4 * (c - 1) + j, :], logitsT[(c - 1) % 2][:, j * P:(j + 1) * P],
                                            mem.ident[0:E, 0:E])
            last.then_inc(l_done, 1)
            rest["tensor"](pe)

        @block.scalar
        def _(act):
            w.high(act, 0)
            for c in range(NCH):
                act.wait_ge(lt_done, c + 1)
                act.activation(logitsT[c % 2][:], LT[c % 2][0:E, :], ACT.Copy).then_inc(lt_ready, 1)
            rest["scalar"](act)

        @block.vector
        def _(dve):
            rest["vector"](dve)


def over_experts(ap):
    return ap.unsqueeze(2).to_broadcast([P, NB, E])


class Softmax:

    def __init__(self, sem, sb, L, l_done):
        self.L, self.l_done = L, l_done
        self.top, self.total, self.inv = sb("top", [P, NB]), sb("total", [P, NB]), sb("inv", [P, NB])
        self.z, self.e, self.p = sb("z", [P, NB, E]), sb("e", [P, NB, E]), sb("p", [P, NB, E])
        self.z_done, self.e_done = sem("z_done"), sem("e_done")

    def scalar(self, act):
        act.wait_ge(self.z_done, 1)
        act.activation(self.e[:], self.z[:], ACT.Exp).then_inc(self.e_done, 1)

    def vector(self, dve, link):
        dve.wait_ge(self.l_done, 1)
        link(dve.tensor_reduce(self.top[:], self.L[:], AX.X, ALU.max))
        dve.tensor_tensor(self.z[:], self.L[:], over_experts(self.top[:]), ALU.subtract)\
            .then_inc(self.z_done, 1)
        dve.wait_ge(self.e_done, 1)
        link(dve.tensor_reduce(self.total[:], self.e[:], AX.X, ALU.add))
        link(dve.reciprocal(self.inv[:], self.total[:]))
        link(dve.tensor_tensor(self.p[:], self.e[:], over_experts(self.inv[:]), ALU.mult))


def chained(dve, sem):
    count = [0]

    def link(instruction):
        count[0] += 1
        instruction.then_inc(sem, 1)
        dve.wait_ge(sem, count[0])

    return link


def count_rows(pe, mem, marks, BEFORE, TILES):
    flat = marks[:].rearrange("p b e -> p (b e)")
    pe.matmul(BEFORE[:].rearrange("p b e -> p (b e)"), mem.earlier, flat, start=True, stop=True)
    return pe.matmul(TILES[:].rearrange("p b e -> p (b e)"), mem.ones, flat, start=True, stop=True)


def top_experts(mem, sem, sb, ps, L, l_done, routed, slot_ready):
    soft = Softmax(sem, sb, L, l_done)
    above, equal = sb("above", [P, NB, E, E]), sb("equal", [P, NB, E, E])
    rank, chosen, kept = sb("rank", [P, NB, E]), sb("chosen", [P, NB, E]), sb("kept", [P, NB, E])
    kept_sum, kept_inv = sb("kept_sum", [P, NB]), sb("kept_inv", [P, NB])
    gates, marks = sb("gates", [P, NB, E]), sb("marks", [P, NB, E])
    numbers = SlotNumbers(sb, routed)
    BEFORE, TILES = ps("BEFORE", [P, NB, E]), ps("TILES", [P, NB, E])
    chain, chosen_done, counted = sem("chain"), sem("chosen_done"), sem("counted")

    def tensor(pe):
        pe.wait_ge(chosen_done, 1)
        count_rows(pe, mem, chosen, BEFORE, TILES).then_inc(counted, 1)

    def vector(dve):
        link = chained(dve, chain)
        soft.vector(dve, link)
        others = soft.p[:].unsqueeze(2).to_broadcast([P, NB, E, E])
        own = soft.p[:].unsqueeze(3).to_broadcast([P, NB, E, E])
        before = mem.lower8.unsqueeze(1).to_broadcast([P, NB, E, E])
        dve.tensor_tensor(above[:], others, own, ALU.is_gt)
        link(dve.tensor_tensor(equal[:], others, own, ALU.is_equal))
        link(dve.tensor_tensor(equal[:], equal[:], before, ALU.mult))
        link(dve.tensor_tensor(above[:], above[:], equal[:], ALU.add))
        link(dve.tensor_reduce(rank[:], above[:], AX.X, ALU.add))
        dve.tensor_scalar(chosen[:], rank[:], float(TOPK), None, ALU.is_lt).then_inc(chosen_done, 1)
        dve.wait_ge(chosen_done, 1)
        link(dve.tensor_tensor(kept[:], soft.p[:], chosen[:], ALU.mult))
        link(dve.tensor_reduce(kept_sum[:], kept[:], AX.X, ALU.add))
        link(dve.reciprocal(kept_inv[:], kept_sum[:]))
        link(dve.tensor_tensor(gates[:], kept[:], over_experts(kept_inv[:]), ALU.mult))
        dve.wait_ge(counted, 1)
        numbers.starts(dve, link, mem, BEFORE, TILES)
        for k in range(TOPK):
            link(dve.tensor_scalar(marks[:], rank[:], float(k), None, ALU.is_equal))
            numbers.slots(dve, link, marks[:], gates[:], k, slot_ready)

    return {"tensor": tensor, "scalar": soft.scalar, "vector": vector}


BITS = 30


def selected_expert(mem, sem, sb, ps, L, l_done, routed, slot_ready):
    soft = Softmax(sem, sb, L, l_done)
    thr = sb("thr", [P, E], U32)
    bits, cand, enough = (sb(n, [P, 3, E], U32) for n in ("bits", "cand", "enough"))
    flags, part = sb("flags", [P, 3, E, NB]), sb("part", [P, 3, E])
    above, equal, first = (sb(n, [P, NB, E]) for n in ("above", "equal", "first"))
    in_tile, upto, value, marks = (sb(n, [P, NB, E]) for n in ("in_tile", "upto", "value", "marks"))
    some, best = sb("some", [P, NB]), sb("best", [P, NB])
    need = sb("need", [P, E])
    numbers = SlotNumbers(sb, routed)
    TOT = ps("TOT", [P, 3, E])
    BEFORE = ps("BEFORE", [P, NB, E])
    TILES = ps("TILES", [P, NB, E])
    chain = sem("chain")
    part_done, tot_done = sem("part_done"), sem("tot_done")
    marks_done, marks_tot = sem("marks_done"), sem("marks_tot")
    cand_done, flags_done, enough_done = sem("cand_done"), sem("flags_done"), sem("enough_done")
    above_done, above_tot, equal_done, equal_tot = (sem(n) for n in ("above_done", "above_tot", "equal_done", "equal_tot"))

    def tensor(pe):
        with pe.Fori(0, BITS // 2) as i:
            pe.wait_ge(part_done, i + 1)
            pe.matmul(TOT[:].rearrange("p c e -> p (c e)"), mem.ones, part[:].rearrange("p c e -> p (c e)"),
                      start=True, stop=True).then_inc(tot_done, 1)
        pe.wait_ge(above_done, 1)
        pe.matmul(TOT[:, 0, :], mem.ones, part[:, 0, :], start=True, stop=True).then_inc(above_tot, 1)
        pe.wait_ge(equal_done, 1)
        count_rows(pe, mem, equal, BEFORE, TILES).then_inc(equal_tot, 1)
        pe.wait_ge(marks_done, 1)
        count_rows(pe, mem, marks, BEFORE, TILES).then_inc(marks_tot, 1)

    def vector(dve):
        link = chained(dve, chain)
        soft.vector(dve, link)
        by_expert = soft.p[:].rearrange("p b e -> p e b")
        thr_f = thr[:].bitcast(F32)
        dve.memset(thr[:], 0)
        for c in range(3):
            last = dve.memset(bits[:, c, :], (c + 1) << (BITS - 2))
        link(last)
        values = by_expert.unsqueeze(1).to_broadcast([P, 3, E, NB])
        with dve.Fori(0, BITS // 2) as i:
            dve.tensor_tensor(cand[:], thr[:].unsqueeze(1).to_broadcast([P, 3, E]), bits[:], ALU.bitwise_or)\
                .then_inc(cand_done, 1)
            dve.wait_ge(cand_done, i + 1)
            dve.tensor_tensor(flags[:], values, cand[:].bitcast(F32).unsqueeze(3).to_broadcast([P, 3, E, NB]),
                              ALU.is_ge).then_inc(flags_done, 1)
            dve.wait_ge(flags_done, i + 1)
            dve.tensor_reduce(part[:], flags[:], AX.X, ALU.add).then_inc(part_done, 1)
            dve.wait_ge(tot_done, i + 1)
            dve.tensor_scalar(enough[:], TOT[:], float(CAP), None, ALU.is_ge).then_inc(enough_done, 1)
            dve.wait_ge(enough_done, i + 1)
            dve.tensor_scalar(bits[:], bits[:], 2, None, ALU.logical_shift_right)
            for c in range(3):
                dve.copy_predicated(thr[:], enough[:, c, :], cand[:, c, :])
                dve.drain()
        thr_b = thr_f.unsqueeze(1).to_broadcast([P, NB, E])
        link(dve.tensor_tensor(above[:], soft.p[:], thr_b, ALU.is_gt))
        dve.tensor_reduce(part[:, 0, :], above[:].rearrange("p b e -> p e b"), AX.X, ALU.add).then_inc(above_done, 1)
        dve.tensor_tensor(equal[:], soft.p[:], thr_b, ALU.is_equal).then_inc(equal_done, 1)
        dve.wait_ge(above_tot, 1)
        link(dve.tensor_scalar(need[:], TOT[:, 0, :], -1.0, float(CAP), ALU.mult, ALU.add))
        dve.wait_ge(equal_tot, 1)
        link(dve.tensor_copy(in_tile[:], TILES[:]))
        dve.wait_ge(equal_done, 1)
        for e in range(E):
            last = dve.tensor_tensor_scan(upto[:, :, e], in_tile[:, :, e], mem.zeros32, 0.0, ALU.add, ALU.add)
        link(last)
        link(dve.tensor_tensor(upto[:], upto[:], in_tile[:], ALU.subtract))
        link(dve.tensor_tensor(upto[:], BEFORE[:], upto[:], ALU.add))
        link(dve.tensor_tensor(first[:], upto[:], need[:].unsqueeze(1).to_broadcast([P, NB, E]), ALU.is_lt))
        link(dve.tensor_tensor(first[:], first[:], equal[:], ALU.mult))
        link(dve.tensor_tensor(above[:], above[:], first[:], ALU.add))
        link(dve.tensor_reduce(some[:], above[:], AX.X, ALU.max))
        link(dve.tensor_scalar(above[:], above[:], 1.0, 4.0, ALU.subtract, ALU.mult))
        link(dve.tensor_tensor(above[:], above[:], over_experts(some[:]), ALU.mult))
        link(dve.tensor_tensor(value[:], soft.p[:], above[:], ALU.add))
        link(dve.tensor_reduce(best[:], value[:], AX.X, ALU.max))
        link(dve.tensor_tensor(marks[:], value[:], over_experts(best[:]), ALU.is_equal))
        link(dve.tensor_tensor(marks[:], marks[:], mem.rising8.unsqueeze(1).to_broadcast([P, NB, E]), ALU.mult))
        link(dve.tensor_reduce(best[:], marks[:], AX.X, ALU.max))
        dve.tensor_tensor(marks[:], marks[:], over_experts(best[:]), ALU.is_equal).then_inc(marks_done, 1)
        dve.wait_ge(marks_done, 1)
        dve.wait_ge(marks_tot, 1)
        numbers.starts(dve, link, mem, BEFORE, TILES)
        numbers.slots(dve, link, marks[:], soft.p[:], 0, slot_ready)

    return {"tensor": tensor, "scalar": soft.scalar, "vector": vector}



CUT = 1024


def sorted_experts(nc, mem, routed, tag, w_up, w_down, width, gelu):
    with ExitStack() as ctx:
        sem, sb, ps = open_stage(nc, ctx, tag)
        MB = width // P
        G = MB // 2
        NT, TB = routed.tiles, RT // P
        up, down = parts(sb, "up", [P, DB, E, width]), parts(sb, "down", [P, MB, E, D])
        raw = [sb(f"raw{a}", [P, CUT]) for a in range(2)]
        rows = [sb(f"rows{u}", [P, TB, D]) for u in range(2)]
        xT = [parts(sb, f"xT{u}", [P, DB, RT]) for u in range(2)]
        h32 = [sb(f"h{g}", [P, 2, RT]) for g in range(2)]
        hT = [parts(sb, f"hT{u}", [P, MB, RT]) for u in range(2)]
        y = [sb(f"y{u}", [P, TB, D]) for u in range(2)]
        XB = [ps(f"XB{u}", [P, DB, RT]) for u in range(2)]
        HB = [ps(f"HB{g}", [P, 2, RT]) for g in range(4)]
        YB = ps("YB", [P, TB, 512])
        raw_loaded, cut_high, cut_done = [sem(f"raw_loaded{a}") for a in range(2)], sem("cut_high"), sem("cut_done")
        rows_loaded = [sem(f"rows_loaded{u}") for u in range(2)]
        xT_done, x_high, x_low = sem("xT_done"), sem("x_high"), sem("x_low")
        h_done, h_high, h_low = sem("h_done"), sem("h_high"), sem("h_low")
        y_done, y_ready, y_free = sem("y_done"), sem("y_ready"), [sem(f"y_free{u}") for u in range(2)]
        block = ctx.enter_context(nc.Block())
        assert NT % 2 == 1 and G % 2 == 0 and TB == 2

        jobs = [(cut, source, e, slice(b, b + CUT // size), size)
                for e in range(E) for cut, source, blocks, size in ((up, w_up, DB, width), (down, w_down, MB, D))
                for b in range(0, blocks, CUT // size)]
        JOBS = len(jobs) // E

        def over_tiles(eng, step):
            step(0, 0, 0, 3)
            step(1, 0, 1, 3)
            with eng.Fori(0, (NT - 5) // 2) as i:
                step(2 * i + 2, i + 1, 0, 3)
                step(2 * i + 3, i + 1, 1, 3)
            step(NT - 3, NT // 2 - 1, 0, 2)
            step(NT - 2, NT // 2 - 1, 1, 1)
            step(NT - 1, NT // 2, 0, 0)

        def tile_rows(source, s):
            return source[bass.ds(s * RT, RT), :].rearrange("(t p) d -> p t d", p=P)

        def blocks_of_raw(n):
            return raw[n % 2][:].rearrange("p (b c) -> p b c", c=jobs[n][4])

        def cut_low(eng, n):
            cut, source, e, blocks, size = jobs[n]
            eng.wait_ge(cut_high, n + 1)
            eng.tensor_tensor(cut.lo[:, blocks, e, :], blocks_of_raw(n), cut.hi[:, blocks, e, :],
                              ALU.subtract).then_inc(cut_done, 1)

        @block.gpsimd
        def _(pool):
            def load(n):
                cut, source, e, blocks, size = jobs[n]
                after(pool, cut_done, n - 1)
                pool.dma_start(blocks_of_raw(n), source[:, blocks, e, :]).then_inc(raw_loaded[n % 2], 16)

            load(0)
            for n, (cut, source, e, blocks, size) in enumerate(jobs):
                if n + 1 < len(jobs):
                    load(n + 1)
                if e == 0:
                    continue
                pool.wait_ge(cut_done, JOBS)
                pool.wait_ge(raw_loaded[n % 2], 16 * (n // 2 + 1))
                pool.tensor_copy(cut.hi[:, blocks, e, :], blocks_of_raw(n)).then_inc(cut_high, 1)
                cut_low(pool, n)

        @block.sync
        def _(sp):
            def load(s, k, u):
                sp.dma_start(rows[u][:], tile_rows(routed.rows_in, s)).then_inc(rows_loaded[u], 16)

            def step(s, k, u, more):
                if more >= 3:
                    after(sp, xT_done, s + 2)
                    load(s + 3, k + 1 + u, 1 - u)
                after(sp, y_ready, s + 1)
                sp.dma_start(tile_rows(routed.rows_out, s), y[u][:]).then_inc(y_free[u], 16)

            load(0, 0, 0)
            load(1, 0, 1)
            sp.wait_ge(xT_done, 1)
            load(2, 1, 0)
            over_tiles(sp, step)
            sp.wait_ge(y_free[0], 16 * (NT // 2 + 2))
            sp.wait_ge(y_free[1], 16 * (NT // 2 + 1))

        @block.tensor
        def _(pe):
            def expert_of(s):
                return pe.value_load(routed.expert[0:1, bass.ds(s, 1)], min_val=0, max_val=E - 1)

            def of_expert(cut, blk, e, columns):
                return tuple(w[:, blk, bass.ds(e, 1), columns].rearrange("p o c -> p (o c)") for w in (cut.hi, cut.lo))

            def transpose(s, k, u):
                pe.wait_ge(rows_loaded[u], 16 * (k + 1))
                after(pe, x_low, s - 1)
                for db in range(DB):
                    for t in range(TB):
                        last = pe.transpose(XB[u][:, db, t * P:(t + 1) * P], rows[u][:, t, db * P:(db + 1) * P],
                                            mem.ident)
                last.then_inc(xT_done, 1)

            def hidden(s, u):
                e = expert_of(s)
                pe.wait_ge(cut_done, JOBS * e + JOBS)
                after(pe, x_low, s + 1)
                for g in range(G):
                    bank = HB[(G * u + g) % 4]
                    after(pe, h_high, G * s + g - 3)
                    for m in (2 * g, 2 * g + 1):
                        for db in range(DB):
                            last = product(pe, bank[:, m % 2, :], of_expert(up, db, e, slice(m * P, (m + 1) * P)),
                                           (xT[u].hi[:, db, :], xT[u].lo[:, db, :]),
                                           start=(db == 0), stop=(db == DB - 1))
                    last.then_inc(h_done, 1)

            def output(s, u):
                e = expert_of(s)
                after(pe, h_low, G * s + G)
                after(pe, y_ready, s)
                for m in range(MB):
                    w = of_expert(down, m, e, slice(0, D))
                    for t in range(TB):
                        tok = slice(t * P, (t + 1) * P)
                        last = product(pe, YB[:, t, 0:D], (hT[u].hi[:, m, tok], hT[u].lo[:, m, tok]), w,
                                       start=(m == 0), stop=(m == MB - 1))
                last.then_inc(y_done, 1)

            def step(s, k, u, more):
                if more >= 2:
                    transpose(s + 2, k + 1, u)
                if more >= 1:
                    hidden(s + 1, 1 - u)
                output(s, u)

            transpose(0, 0, 0)
            transpose(1, 0, 1)
            hidden(0, 0)
            over_tiles(pe, step)

        @block.scalar
        def _(act):
            def x_hi(s, u):
                after(act, xT_done, s + 1)
                after(act, h_done, G * (s - 1))
                act.activation(xT[u].hi[:], XB[u][:], ACT.Copy).then_inc(x_high, 1)

            def h_hi(s, u):
                after(act, y_done, s - 1)
                for g in range(G):
                    bank = HB[(G * u + g) % 4]
                    after(act, h_done, G * s + g + 1)
                    after(act, h_low, G * s + g - 1)
                    act.activation(h32[g % 2][:], bank[:], gelu)
                    act.activation(hT[u].hi[:, 2 * g:2 * g + 2, :], bank[:], gelu).then_inc(h_high, 1)

            def step(s, k, u, more):
                if more >= 2:
                    x_hi(s + 2, u)
                if more >= 1:
                    h_hi(s + 1, 1 - u)

            for n in range(JOBS):
                cut, source, e, blocks, size = jobs[n]
                act.wait_ge(raw_loaded[n % 2], 16 * (n // 2 + 1))
                act.activation(cut.hi[:, blocks, e, :], blocks_of_raw(n), ACT.Copy).then_inc(cut_high, 1)
            x_hi(0, 0)
            x_hi(1, 1)
            h_hi(0, 0)
            over_tiles(act, step)

        @block.vector
        def _(dve):
            def x_lo(s, u):
                after(dve, x_high, s + 1)
                dve.tensor_tensor(xT[u].lo[:], XB[u][:], xT[u].hi[:], ALU.subtract).then_inc(x_low, 1)

            def h_lo(s, u):
                for g in range(G):
                    after(dve, h_high, G * s + g + 1)
                    high = hT[u].hi[:, 2 * g:2 * g + 2, :]
                    dve.tensor_tensor(hT[u].lo[:, 2 * g:2 * g + 2, :], h32[g % 2][:], high, ALU.subtract)\
                        .then_inc(h_low, 1)

            def step(s, k, u, more):
                if more >= 2:
                    x_lo(s + 2, u)
                if more >= 1:
                    h_lo(s + 1, 1 - u)
                after(dve, y_done, s + 1)
                dve.wait_ge(y_free[u], 16 * (k + 1))
                dve.tensor_copy(y[u][:], YB[:, :, 0:D]).then_inc(y_ready, 1)

            for u in range(2):
                dve.sem_inc(y_free[u], 16)
            for n in range(JOBS):
                cut_low(dve, n)
            x_lo(0, 0)
            x_lo(1, 1)
            h_lo(0, 0)
            over_tiles(dve, step)


def norm_of_sorted(nc, mem, routed, tag, x_kept, out):
    with ExitStack() as ctx:
        sem, sb, ps = open_stage(nc, ctx, tag)
        K = routed.k
        tl = Tail(sem, sb)
        x = [sb(f"x{u}", [P, 2, D]) for u in range(2)]
        index = [sb(f"index{u}", [P, K, 2], U32) for u in range(2)]
        y = [sb(f"y{u}", [P, K, 2, D]) for u in range(2)]
        M = ps("M", [P, 2, PT])
        x_loaded, fetched = [sem(f"x_loaded{u}") for u in range(2)], [sem(f"fetched{u}") for u in range(2)]
        r_added, r_complete, out_stored = sem("r_added"), sem("r_complete"), sem("out_stored")
        block = ctx.enter_context(nc.Block())

        @block.gpsimd
        def _(pool):
            def fetch(p, u):
                pool.tensor_copy(index[u][:], routed.slot[:, :, pair_tiles(p)])
                pool.drain()
                for k in range(K):
                    for j in range(2):
                        pool.indirect_dma_start(y[u][:, k, j, :], None, routed.rows_out,
                                                bass.IndirectOffsetOnAxis(index[u][:, k, j:j + 1], 0))\
                            .then_inc(fetched[u], 16)

            fetch(0, 0)
            fetch(1, 1)
            with pool.Fori(0, NP // 2 - 1) as i:
                for u in range(2):
                    tail_rstd(pool, mem, tl, 2 * i + u)
                    pool.wait_ge(r_complete, 2 * i + u + 1)
                    fetch(2 * i + 2 + u, u)
            tail_rstd(pool, mem, tl, NP - 2)
            tail_rstd(pool, mem, tl, NP - 1)

        @block.vector
        def _(dve):
            def step(p, q, u, first, last):
                dve.wait_ge(x_loaded[u], 16 * (q + 1))
                dve.wait_ge(fetched[u], 32 * K * (q + 1))
                after(dve, tl.xn_done, 2 * p)
                for k in range(K):
                    if k:
                        after(dve, r_added, (K - 1) * p + k)
                    for j in range(2):
                        tile = bass.ds(2 * p + j, 1)
                        so_far = tl.r[:, j, :] if k else x[u][:, j, :]
                        done = r_added if k < K - 1 else r_complete
                        added = dve.scalar_tensor_tensor(tl.r[:, j, :], y[u][:, k, j, :], routed.gate[:, k, tile],
                                                         so_far, ALU.mult, ALU.add)
                    added.then_inc(done, 1)
                after(dve, r_complete, p + 1)
                tail_stats(dve, tl, p, tl.r)
                if out is None and not first:
                    tail_xT_low(dve, mem, tl, p - 1, M[:])
                    after(dve, tl.xT_done, p)
                tail_apply(dve, tl, p, tl.r, tl.x_stored)

            over_pairs(dve, step)
            if out is None:
                tail_xT_low(dve, mem, tl, NP - 1, M[:])

        @block.sync
        def _(sp):
            def step(p, k, u, first, last):
                after(sp, r_complete, p - 1)
                sp.dma_start(x[u][:], x_kept[:, pair_tiles(p), :]).then_inc(x_loaded[u], 16)
                if out is not None and not first:
                    store(p - 1)

            def store(p):
                after(sp, tl.xn_done, 2 * p + 2)
                sp.dma_start(out[:, pair_tiles(p), :], tl.xn[:]).then_inc(out_stored, 16)
                after(sp, out_stored, 16 * (p + 1))
                sp.sem_inc(tl.x_stored, 1)

            step(0, 0, 0, True, False)
            step(1, 0, 1, False, False)
            with sp.Fori(0, (NP - 2) // 2) as i:
                step(2 * i + 2, i + 1, 0, False, False)
                step(2 * i + 3, i + 1, 1, False, False)
            if out is not None:
                store(NP - 1)

        if out is None:
            @block.tensor
            def _(pe):
                over_pairs(pe, lambda p, k, u, first, last: tail_transpose(pe, mem, tl, p, M))

            @block.scalar
            def _(act):
                def step(p, k, u, first, last):
                    after(act, tl.xn_done, 2 * p + 2)
                    act.activation(mem.x[:, pair_tiles(p), :], tl.xn[:], ACT.Copy).then_inc(tl.x_stored, 1)
                    tail_xT_high(act, mem, tl, p, M[:])

                over_pairs(act, step)



def window_attention(nc, mem, w_qkv, w_out, b_out):
    with ExitStack() as ctx:
        sem, sb, ps = open_stage(nc, ctx, "wa")
        WQ, WK, WO = range(3)
        w = Weights(sem, sb, [[P, DB, D]] * 3)
        b_o = sb("bo", [P, D])
        xb = [sb(f"xb{u}", [P, 2, D]) for u in range(2)]
        q_T = parts(sb, "qT", [P, DB, PT])
        k_T = parts(sb, "kT", [P, DB, PT])
        keys = [parts(sb, f"keys{u}", [P, 2, D]) for u in range(2)]
        sim = sb("sim", [P, 2, P])
        row_max, neg_max = sb("row_max", [P, 2]), sb("neg_max", [P, 2])
        prob = sb("prob", [P, 2, P])
        own_sum, pad, total, inv = (sb(n, [P, 2]) for n in ("own_sum", "pad", "total", "inv"))
        probn, probT = sb("probn", [P, 2, P]), parts(sb, "probT", [P, 2, P])
        oT = parts(sb, "oT", [P, DB, PT])
        tl = Tail(sem, sb)
        Q, K = ps("Q", [P, DB, PT]), ps("K", [P, DB, PT])
        S = ps("S", [P, 2, 2 * P])
        KEYS = ps("KEYS", [P, 2, D])
        PB = ps("PB", [P, 2, 2 * P])
        OB = ps("OB", [P, DB, PT])
        Y = ps("Y", [P, 2, D])
        XB = ps("XB", [P, DB, PT])
        names = ("bias_loaded q_done q_high q_low k_done k_high k_low keys_done keys_high keys_low s_done sim_done "
                 "max_done neg_done exp_done pad_done total_done inv_done probn_done pT_done pT_high pT_low o_done "
                 "o_high o_low xb_ready")
        (bias_loaded, q_done, q_high, q_low, k_done, k_high, k_low, keys_done, keys_high, keys_low, s_done, sim_done,
         max_done, neg_done, exp_done, pad_done, total_done, inv_done, probn_done, pT_done, pT_high, pT_low, o_done,
         o_high, o_low, xb_ready) = (sem(n) for n in names.split())
        block = ctx.enter_context(nc.Block())

        @block.sync
        def _(sp):
            w.load(sp, WQ, w_qkv[:, :, 0:D])
            w.load(sp, WK, w_qkv[:, :, D:2 * D])
            sp.dma_start(b_o[:], b_out.to_broadcast([P, D])).then_inc(bias_loaded, 16)
            w.load(sp, WO, w_out)

        @block.gpsimd
        def _(pool):
            def add_bias(p, u):
                pool.tensor_tensor(xb[u][:], mem.x[:, pair_tiles(p), :],
                                   b_o[:].unsqueeze(1).to_broadcast([P, 2, D]), ALU.add).then_inc(xb_ready, 1)

            def step(p, k, u, before, more):
                if before:
                    tail_rstd(pool, mem, tl, p - 1)
                if more:
                    after(pool, tl.r_done, p)
                    add_bias(p + 1, 1 - u)

            for n in (WQ, WK, WO):
                w.low(pool, n)
            pool.wait_ge(bias_loaded, 16)
            add_bias(0, 0)
            over_pairs_deep(pool, step)
            tail_rstd(pool, mem, tl, NP - 1)

        @block.scalar
        def _(act):
            def high(p, part, source, done, high_done):
                after(act, done, p + 1)
                act.activation(part.hi[:], source, ACT.Copy).then_inc(high_done, 1)

            def softmax(p):
                after(act, neg_done, p + 1)
                after(act, total_done, p)
                for j in range(2):
                    act.activation(prob[:, j, :], sim[:, j, :], ACT.Exp, bias=neg_max[:, j:j + 1],
                                   scale=WIN_SCALE, accum_out=own_sum[:, j:j + 1]).then_inc(exp_done, 1)
                act.activation(pad[:], neg_max[:], ACT.Exp).then_inc(pad_done, 1)

            def step(p, k, u, before, more):
                high(p, probT, PB[:, :, 0:P], pT_done, pT_high)
                if more:
                    softmax(p + 1)
                if more >= 2:
                    high(p + 2, q_T, Q[:], q_done, q_high)
                    high(p + 2, k_T, K[:], k_done, k_high)
                high(p, oT, OB[:], o_done, o_high)
                if before:
                    tail_copy_x(act, mem, tl, p - 1)
                    tail_xT_high(act, mem, tl, p - 1, XB[:])
                if more:
                    high(p + 1, keys[1 - u], KEYS[:], keys_done, keys_high)

            for n in (WQ, WK, WO):
                w.high(act, n)
            high(0, q_T, Q[:], q_done, q_high)
            high(0, k_T, K[:], k_done, k_high)
            high(0, keys[0], KEYS[:], keys_done, keys_high)
            softmax(0)
            high(1, q_T, Q[:], q_done, q_high)
            high(1, k_T, K[:], k_done, k_high)
            over_pairs_deep(act, step)
            tail_copy_x(act, mem, tl, NP - 1)
            tail_xT_high(act, mem, tl, NP - 1, XB[:])

        @block.vector
        def _(dve):
            def low(p, part, source, high_done, low_done):
                after(dve, high_done, p + 1)
                dve.tensor_tensor(part.lo[:], source, part.hi[:], ALU.subtract).then_inc(low_done, 1)

            def shift(p):
                after(dve, s_done, p + 1)
                after(dve, exp_done, 2 * p)
                dve.tensor_tensor(sim[:], S[:, :, 0:P], mem.causal.unsqueeze(1).to_broadcast([P, 2, P]), ALU.add)\
                    .then_inc(sim_done, 1)
                after(dve, sim_done, p + 1)
                dve.tensor_reduce(row_max[:], sim[:], AX.X, ALU.max).then_inc(max_done, 1)
                after(dve, max_done, p + 1)
                after(dve, pad_done, p)
                dve.tensor_scalar(neg_max[:], row_max[:], 0.0, -WIN_SCALE, ALU.max, ALU.mult)\
                    .then_inc(neg_done, 1)

            def normalize(p):
                after(dve, exp_done, 2 * p + 2)
                after(dve, pad_done, p + 1)
                dve.scalar_tensor_tensor(total[:], pad[:], float(P), own_sum[:], ALU.mult, ALU.add)\
                    .then_inc(total_done, 1)
                after(dve, total_done, p + 1)
                dve.reciprocal(inv[:], total[:]).then_inc(inv_done, 1)
                after(dve, inv_done, p + 1)
                for j in range(2):
                    dve.tensor_scalar(probn[:, j, :], prob[:, j, :], inv[:, j:j + 1], None, ALU.mult)\
                        .then_inc(probn_done, 1)

            def residual(p, u):
                after(dve, xb_ready, p + 1)
                tail_residual(dve, tl, p, Y[:], xb[u][:])
                tail_stats(dve, tl, p, tl.r)

            def step(p, k, u, before, more):
                if more:
                    shift(p + 1)
                low(p, probT, PB[:, :, 0:P], pT_high, pT_low)
                if before:
                    residual(p - 1, 1 - u)
                if more:
                    normalize(p + 1)
                if more >= 2:
                    low(p + 2, q_T, Q[:], q_high, q_low)
                    low(p + 2, k_T, K[:], k_high, k_low)
                low(p, oT, OB[:], o_high, o_low)
                if before:
                    tail_apply(dve, tl, p - 1, tl.r, tl.x_stored)
                if more:
                    low(p + 1, keys[1 - u], KEYS[:], keys_high, keys_low)
                if before:
                    tail_xT_low(dve, mem, tl, p - 1, XB[:])

            low(0, q_T, Q[:], q_high, q_low)
            low(0, k_T, K[:], k_high, k_low)
            low(0, keys[0], KEYS[:], keys_high, keys_low)
            shift(0)
            normalize(0)
            low(1, q_T, Q[:], q_high, q_low)
            low(1, k_T, K[:], k_high, k_low)
            over_pairs_deep(dve, step)
            residual(NP - 1, 1)
            tail_apply(dve, tl, NP - 1, tl.r, tl.x_stored)
            tail_xT_low(dve, mem, tl, NP - 1, XB[:])

        @block.tensor
        def _(pe):
            def proj_q(p):
                after(pe, q_low, p)
                project_T(pe, Q, w.cut[WQ], blocks_at(mem.xT, pair_tokens(p))).then_inc(q_done, 1)

            def proj_k(p):
                after(pe, k_low, p)
                project_T(pe, K, w.cut[WK], blocks_at(mem.xT, pair_tokens(p))).then_inc(k_done, 1)

            def proj_keys(p, u):
                after(pe, keys_low, p)
                wk = w.cut[WK]
                for j in range(2):
                    for db in range(DB):
                        tok = bass.ds(p * PT + j * P, P)
                        last = product(pe, KEYS[:, j, :], (mem.xT.hi[:, db, tok], mem.xT.lo[:, db, tok]),
                                       (wk.hi[:, db, :], wk.lo[:, db, :]), start=(db == 0), stop=(db == DB - 1))
                last.then_inc(keys_done, 1)

            def scores(p):
                after(pe, q_low, p + 1)
                after(pe, k_low, p + 1)
                after(pe, sim_done, p)
                for j in range(2):
                    for db in range(DB):
                        tok = slice(j * P, (j + 1) * P)
                        last = product(pe, S[:, j, 0:P], (q_T.hi[:, db, tok], q_T.lo[:, db, tok]),
                                       (k_T.hi[:, db, tok], k_T.lo[:, db, tok]),
                                       start=(db == 0), stop=(db == DB - 1))
                last.then_inc(s_done, 1)

            def transpose_softmax(p):
                after(pe, probn_done, 2 * p + 2)
                after(pe, pT_low, p)
                for j in range(2):
                    last = pe.transpose(PB[:, j, 0:P], probn[:, j, :], mem.ident)
                last.then_inc(pT_done, 1)

            def values(p, u):
                after(pe, keys_low, p + 1)
                after(pe, pT_low, p + 1)
                after(pe, o_low, p)
                for db in range(DB):
                    for j in range(2):
                        f = slice(db * P, (db + 1) * P)
                        last = product(pe, OB[:, db, j * P:(j + 1) * P],
                                       (keys[u].hi[:, j, f], keys[u].lo[:, j, f]),
                                       (probT.hi[:, j, :], probT.lo[:, j, :]))
                last.then_inc(o_done, 1)

            def output(p):
                after(pe, o_low, p + 1)
                project(pe, Y, oT, w.cut[WO]).then_inc(tl.y_done, 1)

            def step(p, k, u, before, more):
                if more:
                    scores(p + 1)
                transpose_softmax(p)
                if before:
                    output(p - 1)
                if more >= 2:
                    proj_q(p + 2)
                    proj_k(p + 2)
                values(p, u)
                if before:
                    after(pe, tl.xT_low, p - 1)
                    tail_transpose(pe, mem, tl, p - 1, XB)
                if more:
                    proj_keys(p + 1, 1 - u)

            pe.wait_ge(w.lo_done, WQ + 1)
            proj_q(0)
            pe.wait_ge(w.lo_done, WK + 1)
            proj_k(0)
            proj_keys(0, 0)
            scores(0)
            proj_q(1)
            proj_k(1)
            pe.wait_ge(w.lo_done, WO + 1)
            over_pairs_deep(pe, step)
            output(NP - 1)
            tail_transpose(pe, mem, tl, NP - 1, XB)



def by_block(ap):
    return ap.rearrange("(b p) n -> p b n", p=P)


def row(ap):
    return ap.rearrange("(a n) -> a n", a=1)


def constants():
    r, c = np.arange(P)[:, None], np.arange(P)[None, :]
    return {
        "ident": r == c,
        "ones": np.ones((P, P)),
        "earlier": r < c,
        "causal": np.where(c <= r, 0.0, MASKED),
        "head_mask": np.arange(P)[:, None] // DH == np.arange(HH)[None, :],
        "neg_half": np.full((P, 2), -0.5),
        "eps": np.full((P, 2), EPS),
        "zeros32": np.zeros((P, NB)),
        "rising8": np.broadcast_to(E - np.arange(E), (P, E)),
        "tile_start": np.broadcast_to(RT * np.arange(most_tiles(TOPK)), (P, most_tiles(TOPK))),
        "lower8": np.broadcast_to((np.arange(E)[None, :] < np.arange(E)[:, None]).reshape(1, E * E), (P, E * E)),
    }


def constant_columns():
    at, found = 0, {}
    for name, value in constants().items():
        found[name] = (at, value.shape[1])
        at += value.shape[1]
    return found, at


def open_residents(nc, ctx, mem, tag):
    mem.x = ctx.enter_context(nc.sbuf_tensor(f"{tag}_x", [P, NB, D], F32))
    mem.xT = Parts(*(ctx.enter_context(nc.sbuf_tensor(f"{tag}_xT_{n}", [P, DB, T], F16)) for n in ("hi", "lo")))


def decoder(nc, a, out):
    with ExitStack() as ctx:
        columns, n_columns = constant_columns()
        mem = Mem()
        mem.ident16 = ctx.enter_context(nc.sbuf_tensor("ident16", [P, P], F16))
        const = ctx.enter_context(nc.sbuf_tensor("const", [P, n_columns], F32))

        def constant(name):
            at, size = columns[name]
            return const[:, at:at + size]

        mem.ident, mem.ones, mem.earlier, mem.causal = (constant(n) for n in ("ident", "ones", "earlier", "causal"))
        mem.head_mask = constant("head_mask")
        mem.neg_half, mem.zeros32, mem.rising8 = constant("neg_half"), constant("zeros32"), constant("rising8")
        mem.eps, mem.tile_start = constant("eps"), constant("tile_start")
        mem.lower8 = constant("lower8").rearrange("p (e o) -> p e o", e=E)

        def load_constants(sp, loaded):
            sp.dma_start(const[:], a["const"]).then_inc(loaded, 16)
            sp.dma_start(mem.ident16[:], a["ident16"]).then_inc(loaded, 16)

        mem.load_constants = load_constants

        ctxT = by_block(a["ctxT"])
        x_kept = nc.dram_tensor("x_kept", (T, D), F32).ap().rearrange("(b p) d -> p b d", p=P)
        rows_in, rows_out = (nc.dram_tensor(n, (most_tiles(TOPK) * RT, D), F32).ap() for n in ("rows_in", "rows_out"))
        routed = [Routed(nc, ctx, f"L{n}", k, rows_in, rows_out) for n, k in enumerate((TOPK, 1))]

        def context_layer(tag):
            weights = (by_block(a[f"{tag}_xattn_{n}"]) for n in ("Wq", "Wk", "Wv", "Wo"))
            cross_attention(nc, mem, f"{tag}x", ctxT, *weights, a[f"{tag}_xattn_bq"],
                            a[f"{tag}_xattn_bk"], row(a[f"{tag}_xattn_bv"]), row(a[f"{tag}_xattn_bo"]))

        def expert_layer(n, w_up, w_down, width, gelu):
            sorted_experts(nc, mem, routed[n], f"L{n}", w_up.rearrange("e (b p) h -> p b e h", p=P),
                           w_down.rearrange("e (b p) d -> p b e d", p=P), width, gelu)

        with ExitStack() as residents:
            open_residents(nc, residents, mem, "L0")
            gated_attention(nc, mem, rows_in, a["x"].rearrange("b p d -> p b d"), by_block(a["xT"]),
                            *(by_block(a[f"L0_attn_{n}"]) for n in ("Wq", "Wk", "Wv", "Wo", "Wg")),
                            a["L0_attn_bg"],
                            a["diagonals"].rearrange("p (h t) -> p h t", h=HH),
                            a["head_rows"].rearrange("p (h t) -> p h t", h=H))
            context_layer("L0")
            router(nc, mem, "r0", by_block(a["L0_ffn_router_w"]), top_experts, routed[0], x_kept)
        expert_layer(0, a["L0_ffn_up_w"], a["L0_ffn_down_w"], 4 * D, ACT.Gelu_apprx_tanh)
        with ExitStack() as residents:
            open_residents(nc, residents, mem, "L1")
            norm_of_sorted(nc, mem, routed[0], "n0", x_kept, None)
            window_attention(nc, mem, by_block(a["L1_attn_w_qkv"]), by_block(a["L1_attn_w_out"]),
                             row(a["L1_attn_b_out"]))
            context_layer("L1")
            router(nc, mem, "r1", by_block(a["L1_ffn_Wg"]), selected_expert, routed[1], x_kept)
        expert_layer(1, a["L1_ffn_W1"], a["L1_ffn_W2"], 2 * D, ACT.Gelu)
        norm_of_sorted(nc, mem, routed[1], "n1", x_kept, out.rearrange("b p d -> p b d"))



def kernel(**inputs):
    import concourse.bacc as bacc
    from concourse.bass_utils import run_bass_kernel_spmd

    arrays = {k: np.asarray(v) for k, v in inputs.items()}
    arrays["xT"] = arrays["x"].reshape(T, D).T
    arrays["ctxT"] = arrays.pop("ctx_1024").reshape(T, D).T
    for name in ("L0_attn_Wq", "L0_attn_Wk", "L0_attn_Wv", "L0_attn_Wo", "L0_attn_Wg",
                 "L0_xattn_Wq", "L0_xattn_Wk", "L0_xattn_Wv", "L0_xattn_Wo"):
        arrays[name] = arrays[name].T
    for name in ("L0_xattn_bq", "L0_xattn_bk", "L1_xattn_bq", "L1_xattn_bk"):
        arrays[name] = arrays[name].reshape(DB, P).T
    gate_w, gate_b = np.zeros((D, GROWS), np.float32), np.zeros((GROWS, 1), np.float32)
    for at in (0, 32):
        gate_w[:, at:at + H] = arrays["L0_attn_Wg"]
        gate_b[at:at + H, 0] = arrays["L0_attn_bg"]
    arrays["L0_attn_Wg"], arrays["L0_attn_bg"] = gate_w, gate_b
    eye = np.eye(P, dtype=np.float32)
    arrays["const"] = np.concatenate(list(constants().values()), axis=1).astype(np.float32)
    arrays["diagonals"] = np.tile(eye, (1, HH))
    arrays["ident16"] = eye.astype(np.float16)
    head_rows = np.zeros((GROWS, H, P), np.float16)
    for at in (0, 32):
        head_rows[at + np.arange(H), np.arange(H), :] = 1
    arrays["head_rows"] = head_rows.reshape(GROWS, H * P)
    arrays = {k: np.ascontiguousarray(v) for k, v in arrays.items()}

    nc = bacc.Bacc("TRN2", target_bir_lowering=False, num_devices=1)
    aps = {k: nc.dram_tensor(f"in_{k}", v.shape, mybir.dt.from_np(v.dtype), kind="ExternalInput").ap()
           for k, v in arrays.items()}
    out = nc.dram_tensor("out", (NB, P, D), F32, kind="ExternalOutput").ap()
    decoder(nc, aps, out)
    r = run_bass_kernel_spmd(nc, [{f"in_{k}": v for k, v in arrays.items()}], core_ids=[0])
    return r.results[0]["out"]
```
